# Optimizing a Trainium2 kernel written in Bass

```python
import numpy as np
import jax
import jax.numpy as jnp

def _softmax(x, axis=-1):
    return jax.nn.softmax(x, axis=axis)

def _gelu(x):
    return jax.nn.gelu(x, approximate=True)

def _silu(x):
    return jax.nn.silu(x)

def _sigmoid(x):
    return jax.nn.sigmoid(x)

def _layernorm(x, axis=-1, eps=1e-05):
    m = jnp.mean(x, axis=axis, keepdims=True)
    v = jnp.var(x, axis=axis, keepdims=True)
    return (x - m) / jnp.sqrt(v + eps)

def _scatter_add(tgt, idx, src, axis=0):
    return tgt.at[idx].add(src)

def _segment_sum(src, seg, n):
    return jax.ops.segment_sum(src, seg, n)
kernel_name = 'mk_gnn_ffn_d1_gnn_r8_fdf029'

def setup_inputs(seed: int=0):
    np.random.seed(seed)
    _w = jnp.asarray

    def _rec_inputs():
        import jax
        import jax.numpy as jnp
        _gk = jax.random.key(seed)
        x = -0.0003713 + 1 * jax.random.normal(jax.random.fold_in(_gk, 1), (6250, 256), jnp.float32)
        src = jax.random.randint(jax.random.fold_in(_gk, 2), (100000,), 0, 6250, jnp.int32)
        dst = jax.random.randint(jax.random.fold_in(_gk, 3), (100000,), 0, 6250, jnp.int32)
        _o = jnp.argsort(dst, stable=True)
        src = src[_o]
        dst = dst[_o]
        return (x, src, dst)
    x, src, dst = _rec_inputs()

    def _L0_gnn_setup():
        import jax, jax.numpy as jnp
        import numpy as np
        N = 6250
        DIM = 256
        E = 100000

        def _srgnn_conv(x, W, b, src, dst, num_nodes):
            xl = x @ W.T + b
            msgs = xl[src]
            agg = jax.ops.segment_sum(msgs, dst, num_segments=num_nodes)
            cnt = jax.ops.segment_sum(jnp.ones((src.shape[0],), x.dtype), dst, num_segments=num_nodes)
            return agg / jnp.maximum(cnt, 1.0)[:, None]
        key = jax.random.key(seed)
        ks = jax.random.split(key, 11)
        stdv = 1.0 / np.sqrt(DIM)
        u = lambda k, shape: jax.random.uniform(k, shape, jnp.float32, -stdv, stdv)
        hidden = jax.random.normal(ks[0], (N, DIM), jnp.float32)
        edge_index = jax.random.randint(ks[1], (2, E), 0, N, jnp.int64)
        return {'hidden': hidden, 'edge_index': edge_index, 'W_in': u(ks[2], (DIM, DIM)), 'b_in': u(ks[3], (DIM,)), 'W_out': u(ks[4], (DIM, DIM)), 'b_out': u(ks[5], (DIM,)), 'W_ih': u(ks[6], (3 * DIM, 2 * DIM)), 'b_ih': u(ks[7], (3 * DIM,)), 'W_hh': u(ks[8], (3 * DIM, DIM)), 'b_hh': u(ks[9], (3 * DIM,))}
    _L0_gnn_all = _L0_gnn_setup()
    _L0_gnn_in = {k: v for k, v in _L0_gnn_all.items() if k in ('W_in', 'b_in', 'W_out', 'b_out', 'W_ih', 'b_ih', 'W_hh', 'b_hh')}
    del _L0_gnn_all

    def _L0_ffn_setup():
        import jax, jax.numpy as jnp
        import numpy as np
        E, D, H, TOP_K = (6, 256, 256, 2)
        ROUTER_H = D // 2
        key = jax.random.key(seed)
        ks = jax.random.split(key, 12)
        s = 1.0 / np.sqrt(D)
        sh = 1.0 / np.sqrt(H)
        sr = 1.0 / np.sqrt(ROUTER_H)
        return {'features': jax.random.normal(ks[0], (8, 512, D), dtype=jnp.float32), 'router_w1': jax.random.uniform(ks[1], (D, ROUTER_H), jnp.float32, -s, s), 'router_b1': jnp.zeros((ROUTER_H,), jnp.float32), 'router_w2': jax.random.uniform(ks[2], (ROUTER_H, E), jnp.float32, -sr, sr), 'router_b2': jnp.zeros((E,), jnp.float32), 'expert_w1': jax.random.uniform(ks[3], (E, D, H), jnp.float32, -s, s), 'expert_b1': jnp.zeros((E, H), jnp.float32), 'expert_w2': jax.random.uniform(ks[4], (E, H, H), jnp.float32, -sh, sh), 'expert_b2': jnp.zeros((E, H), jnp.float32), 'expert_w3': jax.random.uniform(ks[5], (E, H, D), jnp.float32, -sh, sh), 'expert_b3': jnp.zeros((E, D), jnp.float32)}
    _L0_ffn_all = _L0_ffn_setup()
    _L0_ffn_in = {k: v for k, v in _L0_ffn_all.items() if k in ('router_w1', 'router_b1', 'router_w2', 'router_b2', 'expert_w1', 'expert_b1', 'expert_w2', 'expert_b2', 'expert_w3', 'expert_b3')}
    del _L0_ffn_all
    return {'x': x, 'src': src, 'dst': dst, 'L0_gnn_W_in': _L0_gnn_in['W_in'], 'L0_gnn_b_in': _L0_gnn_in['b_in'], 'L0_gnn_W_out': _L0_gnn_in['W_out'], 'L0_gnn_b_out': _L0_gnn_in['b_out'], 'L0_gnn_W_ih': _L0_gnn_in['W_ih'], 'L0_gnn_b_ih': _L0_gnn_in['b_ih'], 'L0_gnn_W_hh': _L0_gnn_in['W_hh'], 'L0_gnn_b_hh': _L0_gnn_in['b_hh'], 'L0_ffn_router_w1': _L0_ffn_in['router_w1'], 'L0_ffn_router_b1': _L0_ffn_in['router_b1'], 'L0_ffn_router_w2': _L0_ffn_in['router_w2'], 'L0_ffn_router_b2': _L0_ffn_in['router_b2'], 'L0_ffn_expert_w1': _L0_ffn_in['expert_w1'], 'L0_ffn_expert_b1': _L0_ffn_in['expert_b1'], 'L0_ffn_expert_w2': _L0_ffn_in['expert_w2'], 'L0_ffn_expert_b2': _L0_ffn_in['expert_b2'], 'L0_ffn_expert_w3': _L0_ffn_in['expert_w3'], 'L0_ffn_expert_b3': _L0_ffn_in['expert_b3']}

def reference(x, src, dst, L0_gnn_W_in, L0_gnn_b_in, L0_gnn_W_out, L0_gnn_b_out, L0_gnn_W_ih, L0_gnn_b_ih, L0_gnn_W_hh, L0_gnn_b_hh, L0_ffn_router_w1, L0_ffn_router_b1, L0_ffn_router_w2, L0_ffn_router_b2, L0_ffn_expert_w1, L0_ffn_expert_b1, L0_ffn_expert_w2, L0_ffn_expert_b2, L0_ffn_expert_w3, L0_ffn_expert_b3):
    import jax
    import jax.numpy as jnp

    def _L0_gnn_ref(hidden, edge_index, W_in, b_in, W_out, b_out, W_ih, b_ih, W_hh, b_hh):
        import jax, jax.numpy as jnp
        import numpy as np
        N = 6250
        DIM = 256
        E = 100000

        def _srgnn_conv(x, W, b, src, dst, num_nodes):
            xl = x @ W.T + b
            msgs = xl[src]
            agg = jax.ops.segment_sum(msgs, dst, num_segments=num_nodes)
            cnt = jax.ops.segment_sum(jnp.ones((src.shape[0],), x.dtype), dst, num_segments=num_nodes)
            return agg / jnp.maximum(cnt, 1.0)[:, None]
        src, dst = (edge_index[0], edge_index[1])
        n = hidden.shape[0]
        input_in = _srgnn_conv(hidden, W_in, b_in, src, dst, n)
        input_out = _srgnn_conv(hidden, W_out, b_out, dst, src, n)
        inputs = jnp.concatenate([input_in, input_out], axis=-1)
        gi = inputs @ W_ih.T + b_ih
        gh = hidden @ W_hh.T + b_hh
        i_r, i_i, i_n = jnp.split(gi, 3, axis=-1)
        h_r, h_i, h_n = jnp.split(gh, 3, axis=-1)
        reset_gate = jax.nn.sigmoid(i_r + h_r)
        input_gate = jax.nn.sigmoid(i_i + h_i)
        new_gate = jnp.tanh(i_n + reset_gate * h_n)
        return (1.0 - input_gate) * hidden + input_gate * new_gate

    def _L0_ffn_ref(features, router_w1, router_b1, router_w2, router_b2, expert_w1, expert_b1, expert_w2, expert_b2, expert_w3, expert_b3):
        import jax, jax.numpy as jnp
        import numpy as np
        E, D, H, TOP_K = (6, 256, 256, 2)
        ROUTER_H = D // 2
        rh = jax.nn.relu(features @ router_w1 + router_b1)
        expert_logits = jax.nn.softmax(rh @ router_w2 + router_b2, axis=-1)
        top_w, top_i = jax.lax.top_k(expert_logits, TOP_K)
        routing_weights = jax.nn.softmax(top_w, axis=-1)
        h1 = jax.nn.relu(jnp.einsum('bsd,edh->bseh', features, expert_w1) + expert_b1)
        h2 = jax.nn.relu(jnp.einsum('bseh,ehf->bsef', h1, expert_w2) + expert_b2)
        expert_out = jnp.einsum('bsef,efo->bseo', h2, expert_w3) + expert_b3
        sel = jnp.take_along_axis(expert_out, top_i[:, :, :, None], axis=2)
        combined = jnp.sum(sel * routing_weights[..., None], axis=2)
        return combined
    edge_index = jnp.stack([src, dst])
    x = x + _L0_gnn_ref(_layernorm(x, axis=-1), edge_index, L0_gnn_W_in, L0_gnn_b_in, L0_gnn_W_out, L0_gnn_b_out, L0_gnn_W_ih, L0_gnn_b_ih, L0_gnn_W_hh, L0_gnn_b_hh)
    x = x + _L0_ffn_ref(_layernorm(x, axis=-1)[None], L0_ffn_router_w1, L0_ffn_router_b1, L0_ffn_router_w2, L0_ffn_router_b2, L0_ffn_expert_w1, L0_ffn_expert_b1, L0_ffn_expert_w2, L0_ffn_expert_b2, L0_ffn_expert_w3, L0_ffn_expert_b3)[0]
    return x

_drawn_inputs = setup_inputs


def setup_inputs(seed=0):
    import zlib

    import numpy as np

    out = dict(_drawn_inputs(seed))
    spreads = {'L0_ffn_router_b1': (0.0, 0.308),
     'L0_ffn_router_b2': (0.0, 0.1),
     'L0_ffn_expert_b1': (0.0, 0.8),
     'L0_ffn_expert_b2': (0.0, 0.434),
     'L0_ffn_expert_b3': (0.0, 0.1)}
    factors = {'L0_gnn_b_in': 6.902, 'L0_gnn_b_out': 6.149, 'L0_gnn_b_ih': 4.189, 'L0_gnn_b_hh': 5.624}
    for name, (base, spread) in spreads.items():
        noise = np.random.default_rng([zlib.crc32(name.encode()), seed]).standard_normal(out[name].shape)
        drawn = base * np.exp(spread * noise) if base else spread * noise
        out[name] = jnp.asarray(drawn.astype(out[name].dtype))
    for name, factor in factors.items():
        out[name] = (out[name] * factor).astype(out[name].dtype)
    return out
```

```python
from contextlib import ExitStack

import concourse.bass as bass
from concourse import mybir

F32 = mybir.dt.float32
F16 = mybir.dt.float16
I32 = mybir.dt.int32
U16 = mybir.dt.uint16
U32 = mybir.dt.uint32
ALU = mybir.AluOpType
ACT = mybir.ActivationFunctionType
AX_X = mybir.AxisListType.X

P = 128
NODES = 6250
EDGES = 100000
D = 256
NB = 50
NP = NB * P
NS = 832
HS = NS // 2
HALF = 64
RADIX = 64
LO_SCALE = 2048.0
BATCH = 8
RINGS = 4
RING = BATCH * RINGS
OH = 16
SCATTER = 32
SORTED_TILES = 640
LIST = 2 * NS * P
SENTINEL = 8191
EPS = 1e-5
NE = 6
G3 = 3 * D
CREDIT = 2
assert EDGES // P + NB + 1 <= NS and NS % BATCH == 0


def gnn_moe_program(nc, x, edges, w, out, table, lists):
    ctx = ExitStack()
    with ctx:
        def sb(name, shape, dt):
            return ctx.enter_context(nc.sbuf_tensor(name, shape, dt))

        def sem(name):
            return ctx.enter_context(nc.semaphore(name))

        banks = [ctx.enter_context(nc.psum_tensor(f"bank{i}", [P, 512], F32)) for i in range(8)]

        iota_cols = sb("iota_cols", [P, NS], F16)
        pad_position = sb("pad_position", [P, 1], F32)
        iota_bucket = sb("iota_bucket", [P, NB], F32)
        lower = sb("lower", [P, P], F16)
        iota_down = sb("iota_down", [P, NB], F32)
        pick_row = sb("pick_row", [P, 256], F16)
        lower_bucket = sb("lower_bucket", [P, P], F16)
        ones_col = sb("ones_col", [P, 1], F16)
        ones_wide = sb("ones_wide", [P, HS], F32)
        zeros16 = sb("zeros16", [P, 512], F16)
        ident = sb("ident", [P, P], F32)

        REGION = 18368
        region = sb("region", [P, REGION], F32)
        at = {"sort": 0, "dense": 0}

        def carve(user, shape, dt=F32):
            words = 1
            for n in shape:
                words *= n
            words = words // 2 if dt == F16 else words
            a = at[user]
            at[user] += words
            assert at[user] <= REGION, (user, at[user])
            view = region[:, a:a + words]
            view = view if dt == F32 else view.bitcast(dt)
            if len(shape) == 2:
                view = view.rearrange("p (a b) -> p a b", a=shape[0])
            if len(shape) == 3:
                view = view.rearrange("p (a b c) -> p a b c", a=shape[0], b=shape[1])
            return view

        spread_row = carve("sort", [NB, P], F16)
        key = carve("sort", [2, NS], I32)
        scratch = [carve("sort", [NS], I32) for i in range(3)]
        valid = carve("sort", [NS], F32)
        bucket = carve("sort", [NS], F16)
        prefix = carve("sort", [NS], F32)
        base_digits = carve("sort", [NS], F16)
        bucket_slots = sb("bucket_slots", [P, 4], F32)
        bucket_slots16 = sb("bucket_slots16", [P, 1], F16)
        bucket_i = sb("bucket_i", [P, 2], I32)
        onehot_bucket = carve("sort", [2, NS], F16)
        position = carve("sort", [NS], F32)
        slot_of = carve("sort", [NS])
        row_of = carve("sort", [NS])
        pay_hi = carve("sort", [NS])
        pay_lo = carve("sort", [NS])
        list_at = carve("sort", [2, NS], I32)
        payload = carve("sort", [2, NS], I32)
        raw_list = list_at
        at_stage = carve("sort", [2, SCATTER], I32)
        payload_stage = carve("sort", [2, SCATTER], I32)
        first_slot = sb("first_slot", [1, 2, 64], I32)
        row_payload = sb("row_payload", [P, 2, 2 * P], F16)
        slot_onehot = onehot_bucket
        gather_row = sb("gather_row", [P, 2, NS], I32)
        node_in_bucket = sb("node_in_bucket", [P, 2, NS], F32)

        mean_a = sb("mean_a", [P, NB, D], F32)
        moments = sb("moments", [P, NB, 2], F32)
        rstd = sb("rstd", [P, NB], F32)
        std = sb("std", [P, NB], F32)
        stats6 = sb("stats6", [P, 2, 6], F32)
        mv2 = sb("mv2", [P, 2, 2], F32)
        eps_col = sb("eps_col", [P, 1], F32)

        ring = sb("ring", [P, RING, 2 * D], F16)
        index_stage = sb("index_stage", [P, RINGS, BATCH], I32)
        onehot_node = sb("onehot_node", [P, OH, P], F16)
        inv_count = sb("inv_count", [P, 4], F32)
        hi_mean = sb("hi_mean", [P, D], F32)
        mean_b = sb("mean_b", [P, D], F32)
        has_edge = sb("has_edge", [P, 2, NB], F32)

        w_gate = sb("w_gate", [P, 6, G3], F32)
        gate_bias = sb("gate_bias", [4, G3 + D], F32)
        ring_words = ring[:].rearrange("p a b -> p (a b)").bitcast(F32)
        w_ih_raw = ring_words[:, 0:4 * G3].rearrange("p (a b) -> p a b", a=4)
        w_conv = ring_words[:, 4 * G3:4 * G3 + 4 * D].rearrange("p (a b) -> p a b", a=4)
        norm_rows = ring_words[:, 4 * G3 + 4 * D:4 * G3 + 4 * D + 6 * D].rearrange("p (a b) -> p a b", a=6)
        h_row, h_diff = norm_rows[:, 0:2, :], norm_rows[:, 2:4, :]
        h_split = norm_rows[:, 4:6, :].bitcast(F16)
        b_conv = sb("b_conv", [P, 8], F32)
        r_b1 = sb("r_b1", [P, 1], F32)
        r_w2 = sb("r_w2", [P, NE], F32)
        r_b2 = sb("r_b2", [P, 2, NE], F32)
        e_b1 = sb("e_b1", [P, NE, 2], F32)
        e_b2 = sb("e_b2", [P, NE, 2], F32)
        r_w1 = carve("dense", [2, P])
        e_b3 = carve("dense", [D])[0:NE, :]
        e_w = [carve("dense", [NE * 2, D]) for _ in range(3)]
        x_t = carve("dense", [2, D])
        h_t = carve("dense", [D])
        mean_a_t = carve("dense", [D])
        xh_t = carve("dense", [D])
        tile_in = carve("dense", [6, P])
        gates = carve("dense", [2 * D])
        gate_tmp = carve("dense", [D])
        new_t = carve("dense", [D])
        x1 = carve("dense", [2, D])
        xn = carve("dense", [D])
        xn_T = carve("dense", [2, 2 * P])
        router_h = carve("dense", [2 * P])
        h1 = carve("dense", [2, 2, 2 * P])
        h2 = carve("dense", [2, 2, 2 * P])
        acc = carve("dense", [2, D])
        flags = sb("flags", [P, 4], F32)
        flags_T = carve("dense", [P])[0:4, :]
        ln_s = sb("ln_s", [P, 12], F32)
        logits = sb("logits", [P, 2, NE], F32)
        prob = sb("prob", [P, 2, 8], F32)
        top = sb("top", [P, 2, 8], F32)
        top_at = sb("top_at", [P, 2, 8], U32)
        rt = sb("rt", [P, 24], F32)
        coef = sb("coef", [P, 2, NE], F32)
        coef2 = sb("coef2", [P, 2, NE], F32)
        coef_T = carve("dense", [2, P])[0:NE]

        names = ("consts const_step edges_in x_in moments_done moments_step sqrt_done h_ready hi_ready "
                 "diff_ready split_ready table_stored dve_step onehot_ready onehot_used slots16_ready "
                 "slot_prefix_ready base_ready list_at_ready list_zeroed list_in scatter_staged merged sort_ready sort_used sort_summed decoded stage_ready "
                 "turn rows_landed slot_done node_onehot_ready bucket_done inv_ready hi_mean_ready "
                 "inv_step evac_done out_done fold_in fold_zero small_in fold_summed fold_done experts_in x_used "
                 "h_tile_ready tile_a_turned tile_a_ready tile_b_turned tile_b_ready flags_ready rz_summed "
                 "n_summed rz_ready pre_new_ready new_ready x1_ready dve_tile var_ready std_ready xn_ready "
                 "xn_turned xn_T_ready router_summed router_ready logits_summed shifted_ready exp_ready "
                 "prob_gap_ready gap_exp_ready coef_ready coef_turned coef_T_ready b3_summed l1_summed h1_ready "
                 "l2_summed h2_ready l3_summed combined acc_done acc_free out_landed").split()
        x_landed = [sem(f"x_landed{i}") for i in range(2)]
        S = {n: sem(n) for n in names}
        scatter_landed = [sem(f"scatter_landed{i}") for i in range(2)]
        ring_landed = [sem(f"ring_landed{i}") for i in range(RINGS)]
        store_landed = [sem(f"store_landed{i}") for i in range(2)]
        N_CONSTS = 14
        sums, counts = banks[4], banks[5]
        sort_hi, sort_lo = banks[0:2], banks[2:4]

        block = ctx.enter_context(nc.Block())

        @block.gpsimd
        def _(pool):
            g = nc.gpsimd
            c = S["consts"]
            g.iota(iota_cols[:], [[1, NS]], base=0, channel_multiplier=0,
                   allow_small_or_imprecise_dtypes=True).then_inc(c, 1)
            g.iota(iota_bucket[:], [[1, NB]], base=0, channel_multiplier=0,
                   allow_small_or_imprecise_dtypes=True).then_inc(c, 1)
            g.iota(iota_down[:], [[-1, NB]], base=NB - 1, channel_multiplier=0,
                   allow_small_or_imprecise_dtypes=True).then_inc(c, 1)
            g.iota(pad_position[:], [[0, 1]], base=NS * P, channel_multiplier=1,
                   allow_small_or_imprecise_dtypes=True).then_inc(c, 1)
            g.memset(ones_col[:], 1.0).then_inc(c, 1)
            g.memset(zeros16[:], 0.0).then_inc(c, 1)
            g.memset(first_slot[:], NS).then_inc(c, 1)
            g.memset(ones_wide[:], 1.0).then_inc(c, 1)
            g.memset(lower[:], 1.0).then_inc(S["const_step"], 1)
            g.memset(pick_row[:], 0.0).then_inc(S["const_step"], 1)
            g.memset(spread_row, 0.0).then_inc(S["const_step"], 1)
            g.memset(lower_bucket[:], 1.0).then_inc(S["const_step"], 1)
            g.memset(ident[:], 0.0).then_inc(S["const_step"], 1)
            g.memset(gate_bias[:], 0.0).then_inc(S["fold_zero"], 1)
            g.memset(b_conv[:], 0.0).then_inc(S["fold_zero"], 1)
            g.memset(flags[:], 1.0).then_inc(c, 1)
            g.memset(prob[:], -1.0).then_inc(c, 1)
            pool.wait_ge(S["const_step"], 5)
            g.affine_select(out=spread_row, in_=spread_row, compare_op=ALU.not_equal, fill=float(RADIX),
                            base=0, pattern=[[-1, NB], [0, P]], channel_multiplier=1
                            ).then_inc(S["const_step"], 1)
            g.memset(pick_row[:, 127:128], 1.0).then_inc(S["const_step"], 1)
            g.memset(pick_row[:, 127 + HALF:128 + HALF], 1.0).then_inc(S["const_step"], 1)
            g.affine_select(out=lower[:], in_=lower[:], compare_op=ALU.is_gt, fill=0.0, base=0,
                            pattern=[[1, P]], channel_multiplier=-1).then_inc(c, 1)
            lb = lower_bucket[:].rearrange("p (a m) -> p a m", a=2)
            g.affine_select(out=lb, in_=lb, compare_op=ALU.is_gt, fill=0.0, base=0,
                            pattern=[[0, 2], [1, HALF]], channel_multiplier=-1).then_inc(c, 1)
            g.affine_select(out=ident[:], in_=ident[:], compare_op=ALU.not_equal, fill=1.0, base=0,
                            pattern=[[-1, P]], channel_multiplier=1).then_inc(c, 1)
            pool.wait_ge(S["const_step"], 8)
            g.affine_select(out=spread_row, in_=spread_row, compare_op=ALU.not_equal, fill=1.0,
                            base=-HALF, pattern=[[-1, NB], [0, P]], channel_multiplier=1).then_inc(c, 1)

            pool.wait_ge(S["list_zeroed"], 8 * 16)
            first = SORTED_TILES // (2 * SCATTER)
            for d, r_lo, past in ((0, first, -first), (1, 0, NS // (2 * SCATTER) - first)):
                pool.wait_ge(S["list_at_ready"], d + 1)
                with pool.Fori(r_lo, NS // (2 * SCATTER)) as r:
                    for k in range(2):
                        n_ = r + past
                        tiles = bass.ds(r * (2 * SCATTER) + k * SCATTER, SCATTER)
                        g.tensor_copy(at_stage[:, k, :], list_at[:, d, tiles]).then_inc(S["scatter_staged"], 1)
                        g.tensor_copy(payload_stage[:, k, :], payload[:, d, tiles]).then_inc(S["scatter_staged"], 1)
                        pool.wait_ge(S["scatter_staged"], n_ * 4 + (2 * k + 2))
                        pool.sem_inc(S["turn"], 1)
                        for q in range(SCATTER):
                            g.indirect_dma_start(
                                out=lists[d][:], out_offset=bass.IndirectOffsetOnAxis(ap=at_stage[:, k, q:q + 1], axis=0),
                                in_=payload_stage[:, k, q:q + 1], in_offset=None,
                            ).then_inc(scatter_landed[k], 16)
                    for k in range(2):
                        pool.wait_ge(scatter_landed[k], n_ * (16 * SCATTER) + 16 * SCATTER)
                    pool.sem_inc(S["turn"], 1)

            pool.wait_ge(S["table_stored"], NB + 2)
            pool.wait_ge(S["fold_done"], 2)
            for d in range(2):
                pool.wait_ge(S["decoded"], d + 1)
                with pool.Fori(0, NS // RING) as r:
                    for k in range(RINGS):
                        pool.wait_ge(S["slot_done"], r * RING + (d * NS + k * BATCH + BATCH))
                        pool.sem_inc(S["turn"], 1)
                        g.tensor_copy(index_stage[:, k, :], gather_row[:, d, bass.ds(r * RING + k * BATCH, BATCH)]
                                      ).then_inc(S["stage_ready"], 1)
                        pool.wait_ge(S["stage_ready"], r * RINGS + (d * (NS // BATCH) + k + 1))
                        pool.sem_inc(S["turn"], 1)
                        for q in range(BATCH):
                            g.indirect_dma_start(
                                out=ring[:, k * BATCH + q, :], out_offset=None, in_=table[:],
                                in_offset=bass.IndirectOffsetOnAxis(ap=index_stage[:, k, q:q + 1], axis=0),
                            ).then_inc(ring_landed[k], 16)

        @block.sync
        def _(sp):
            sp.dma_start(key, edges).then_inc(S["edges_in"], 16)
            sp.wait_ge(S["consts"], N_CONSTS)
            for d in range(2):
                entries = lists[d].rearrange("(p n) o -> p (n o)", p=P)[:, 0:NS]
                for q in range(4):
                    sp.dma_start(entries[:, q * (NS // 4):(q + 1) * (NS // 4)],
                                 zeros16[:, 0:NS // 2].bitcast(I32)).then_inc(S["list_zeroed"], 16)
            sp.dma_start(mean_a[:], x.rearrange("(j p) d -> p j d", p=P)).then_inc(S["x_in"], 16)
            sp.sem_inc(S["table_stored"], 2)
            tab = table.rearrange("(j p) d -> j p d", p=P)
            with sp.Fori(0, NB // 2) as r:
                for k in range(2):
                    sp.wait_ge(S["split_ready"], r * 2 + (k + 3))
                    sp.dma_start(tab[bass.ds(r * 2 + k, 1), :, :].rearrange("a p d -> (a p) d"),
                                 h_split[:, k, :]).then_inc(store_landed[k], 16)
                for k in range(2):
                    sp.wait_ge(store_landed[k], r * 16 + 16)
                    sp.sem_inc(S["table_stored"], 1)
            for d in range(2):
                rounds = (d + 1) * (NS // (2 * SCATTER)) - SORTED_TILES // (2 * SCATTER)
                for k in range(2):
                    sp.wait_ge(scatter_landed[k], rounds * 16 * SCATTER)
                sp.dma_start(raw_list[:, d, :], lists[d].rearrange("(p n) o -> p (n o)", p=P)[:, 0:NS]
                             ).then_inc(S["list_in"], 16)
                sp.wait_ge(S["list_in"], d * 16 + 16)
            for d in range(2):
                if d == 1:
                    sp.wait_ge(S["decoded"], 2)
                    sp.dma_start(r_w1, w["r_w1"].rearrange("(c p) n -> p c n", p=P)).then_inc(S["experts_in"], 16)
                    sp.dma_start(e_b3, w["e_b3"]).then_inc(S["experts_in"], 16)
                    for n, name in enumerate(("e_w1", "e_w2", "e_w3")):
                        sp.dma_start(e_w[n], w[name].rearrange("e (c p) n -> p (e c) n", p=P)
                                     ).then_inc(S["experts_in"], 16)
                with sp.Fori(0, NS // RING) as r:
                    for k in range(RINGS):
                        sp.wait_ge(ring_landed[k], r * (16 * BATCH) + (d * (NS // RING) + 1) * 16 * BATCH)
                        sp.sem_inc(S["rows_landed"], BATCH)

        @block.scalar
        def _(act):
            a = nc.scalar
            for dst_, src_ in ((w_ih_raw, w["w_ih_T"].rearrange("(c p) n -> p c n", p=P)),
                               (w_conv[:, 0:2, :], w["w_in"].rearrange("(c p) n -> p c n", p=P)),
                               (w_conv[:, 2:4, :], w["w_out"].rearrange("(c p) n -> p c n", p=P)),
                               (w_gate[:, 4:6, :], w["w_hh_T"].rearrange("(c p) n -> p c n", p=P))):
                act.dma_start(dst_, src_).then_inc(S["fold_in"], 16)
            act.wait_ge(S["fold_zero"], 2)
            act.dma_start(gate_bias[2:3, 0:G3], w["b_ih"]).then_inc(S["fold_in"], 16)
            act.dma_start(gate_bias[2:3, G3:G3 + D], w["b_hh"][:, 2 * D:G3]).then_inc(S["fold_in"], 16)
            act.dma_start(gate_bias[3:4, 0:2 * D], w["b_hh"][:, 0:2 * D]).then_inc(S["fold_in"], 16)
            bc = b_conv[:].rearrange("p (a c m) -> p a c m", a=2, c=2)
            for n, name in enumerate(("b_in", "b_out")):
                for c in range(2):
                    act.dma_start(bc[:, n, c, n:n + 1], w[name][c * P:c * P + P, :]).then_inc(S["fold_in"], 16)
            smalls = ((r_b1[:], w["r_b1"]),
                      (r_w2[:], w["r_w2"]), (r_b2[:, 0, :], w["r_b2"].to_broadcast([P, NE])),
                      (r_b2[:, 1, :], w["r_b2"].to_broadcast([P, NE])), (e_b1[:], w["e_b1"]),
                      (e_b2[:], w["e_b2"]))
            for dst_, src_ in smalls:
                act.dma_start(dst_, src_).then_inc(S["small_in"], 16)
            act.wait_ge(S["fold_summed"], 1)
            for m in range(4):
                a.copy(w_gate[:, m, 0:2 * D], banks[2 * m][:, 0:2 * D])
                ins = a.copy(w_gate[:, m, 2 * D:G3], banks[2 * m + 1][:, 0:D])
            ins.then_inc(S["fold_done"], 1)
            act.wait_ge(S["fold_summed"], 2)
            a.copy(gate_bias[0:2, 0:2 * D], banks[0][0:2, 0:2 * D])
            a.copy(gate_bias[0:2, 2 * D:G3], banks[1][0:2, 0:D]).then_inc(S["fold_done"], 1)
            act.sem_inc(S["split_ready"], 2)
            act.wait_ge(S["moments_done"], 1)
            a.activation(std[:], moments[:, :, 1], ACT.Sqrt, bias=eps_col[:, 0:1]).then_inc(S["sqrt_done"], 1)
            with act.Fori(0, NB // 2) as r:
                for k in range(2):
                    act.wait_ge(S["table_stored"], r * 2 + (k + 1))
                    act.wait_ge(S["h_ready"], r * 2 + (k + 1))
                    a.copy(h_split[:, k, 0:D], h_row[:, k, :]).then_inc(S["hi_ready"], 1)
                    act.wait_ge(S["diff_ready"], r * 2 + (k + 1))
                    a.activation(h_split[:, k, D:2 * D], h_diff[:, k, :], ACT.Copy, scale=LO_SCALE
                                 ).then_inc(S["split_ready"], 1)
            def hi_mean_step(q):
                act.wait_ge(S["inv_ready"], q)
                a.activation(hi_mean[:], sums[:, 0:D], ACT.Copy, scale=inv_count[:, 1:2]
                             ).then_inc(S["hi_mean_ready"], 1)

            with act.Fori(0, NB) as j:
                hi_mean_step(j + 1)
            x_tiles = x.rearrange("(j p) d -> j p d", p=P)
            out_tiles = out.rearrange("(j p) d -> j p d", p=P)
            act.sem_inc(S["acc_free"], 1)
            act.sem_inc(S["h1_ready"], CREDIT)
            act.wait_ge(S["decoded"], 2)
            with act.Fori(0, NB // 2) as r:
                for jj in range(2):
                    act.wait_ge(S["x_used"], r * 2 + (jj + 1))
                    act.dma_start(x_t[:, jj, :], x_tiles[bass.ds(r * 2 + jj, 1), :, :].rearrange("a p d -> (a p) d")
                                  ).then_inc(x_landed[jj], 16)
                for jj in range(2):
                    j1 = r * 2 + (jj + 1)
                    act.wait_ge(S["tile_a_turned"], j1)
                    a.copy(tile_in[:, 0:4, :], banks[0][:].rearrange("p (a b) -> p a b", a=4)
                           ).then_inc(S["tile_a_ready"], 1)
                    hi_mean_step(r * 2 + (NB + jj + 1))
                    act.wait_ge(S["rz_summed"], j1)
                    a.activation(gates, banks[2][:], ACT.Tanh, scale=0.5).then_inc(S["rz_ready"], 1)
                    act.wait_ge(S["pre_new_ready"], j1)
                    a.activation(new_t, gate_tmp, ACT.Tanh).then_inc(S["new_ready"], 1)
                    act.wait_ge(S["var_ready"], j1)
                    a.activation(ln_s[:, 8:9], ln_s[:, 7:8], ACT.Sqrt, bias=eps_col[:, 0:1]
                                 ).then_inc(S["std_ready"], 1)
                    act.wait_ge(S["xn_turned"], j1)
                    a.copy(xn_T[:, :, jj * P:jj * P + P], banks[6][:, 0:2 * P].rearrange("p (a b) -> p a b", a=2)
                           ).then_inc(S["xn_T_ready"], 1)
                act.wait_ge(S["router_summed"], r + 1)
                a.activation(router_h, banks[7][:, 0:2 * P], ACT.Relu, bias=r_b1[:, 0:1]
                             ).then_inc(S["router_ready"], 1)
                for tt in range(2):
                    act.wait_ge(S["shifted_ready"], r * 2 + (tt + 1))
                    a.activation(prob[:, tt, 0:NE], logits[:, tt, :], ACT.Exp, bias=rt[:, 2 + tt:3 + tt],
                                 accum_out=rt[:, 4 + tt:5 + tt]).then_inc(S["exp_ready"], 1)
                act.wait_ge(S["prob_gap_ready"], r + 1)
                a.activation(rt[:, 10:12], rt[:, 8:10], ACT.Exp).then_inc(S["gap_exp_ready"], 1)
                for e in range(NE):
                    act.wait_ge(S["l2_summed"], r * NE + (e + 1))
                    act.sem_inc(S["turn"], 1)
                    act.wait_ge(S["l1_summed"], r * NE + (e + 1))
                    bank = banks[0 if e % 2 == 0 else 6]
                    for m in range(2):
                        ins = a.activation(h1[:, e % 2, m, :], bank[:, m * 2 * P:(m + 1) * 2 * P], ACT.Relu,
                                           bias=e_b1[:, e, m:m + 1])
                    ins.then_inc(S["h1_ready"], 1)
                act.wait_ge(S["acc_done"], r + 1)
                for tt in range(2):
                    act.dma_start(out_tiles[bass.ds(r * 2 + tt, 1), :, :].rearrange("a p d -> (a p) d"),
                                  acc[:, tt, :]).then_inc(S["out_landed"], 16)
                act.wait_ge(S["out_landed"], r * 32 + 32)
                act.sem_inc(S["acc_free"], 1)

        @block.vector
        def _(v):
            e = nc.vector
            steps = [0]

            def step(ins):
                steps[0] += 1
                ins.then_inc(S["dve_step"], 1)
                v.wait_ge(S["dve_step"], steps[0])

            step(e.memset(eps_col[:], EPS))
            v.wait_ge(S["consts"], N_CONSTS)
            v.wait_ge(S["edges_in"], 16)
            v.sem_inc(S["merged"], 2)
            def layer_norm():
                v.wait_ge(S["x_in"], 16)
                with v.Fori(0, NB) as j:
                    e.bn_stats(stats6[:, 0, :], mean_a[:, bass.ds(j, 1), :].rearrange("p a d -> p (a d)")
                               ).then_inc(S["moments_step"], 1)
                    v.wait_ge(S["moments_step"], j * 3 + 1)
                    v.sem_inc(S["turn"], 1)
                    e.bn_aggr(mv2[:, 0, :], stats6[:, 0, :]).then_inc(S["moments_step"], 1)
                    v.wait_ge(S["moments_step"], j * 3 + 2)
                    e.tensor_copy(moments[:, bass.ds(j, 1), :].rearrange("p a d -> p (a d)"), mv2[:, 0, :]
                                  ).then_inc(S["moments_step"], 1)
                    v.wait_ge(S["moments_step"], j * 3 + 3)
                e.tensor_copy(mv2[:, 1, :], mv2[:, 0, :]).then_inc(S["moments_done"], 1)
                v.wait_ge(S["sqrt_done"], 1)
                step(e.reciprocal(rstd[:], std[:]))
                with v.Fori(0, NB // 2) as r:
                    for k in range(2):
                        v.wait_ge(S["split_ready"], r * 2 + (k + 1))
                        e.tensor_scalar(h_row[:, k, :], mean_a[:, bass.ds(r * 2 + k, 1), :].rearrange("p a d -> p (a d)"),
                                        moments[:, bass.ds(r * 2 + k, 1), 0], rstd[:, bass.ds(r * 2 + k, 1)],
                                        ALU.subtract, ALU.mult).then_inc(S["h_ready"], 1)
                        v.wait_ge(S["hi_ready"], r * 2 + (k + 1))
                        e.tensor_tensor(h_diff[:, k, :], h_row[:, k, :], h_split[:, k, 0:D], ALU.subtract
                                        ).then_inc(S["diff_ready"], 1)

            def positions(d):
                q0 = d * 2 * NB
                k_, v_ = key[:, d, :], key[:, 1 - d, :]
                s0, s1, s2 = scratch
                step(e.tensor_single_scalar(s0, k_, 7, ALU.arith_shift_right))
                e.tensor_copy(bucket, s0)
                e.tensor_scalar(valid, k_, float(SENTINEL), None, ALU.is_lt)
                step(e.tensor_single_scalar(s1, k_, P - 1, ALU.bitwise_and))
                step(e.scalar_tensor_tensor(out=s2, in0=v_, scalar=256.0, in1=s1, op0=ALU.mult, op1=ALU.add))
                step(e.scalar_tensor_tensor(out=payload[:, d, :], in0=s2, scalar=1.0, in1=valid,
                                            op0=ALU.add, op1=ALU.mult))
                if d == 0:
                    e.tensor_single_scalar(s0, payload[:, d, :], 11, ALU.arith_shift_right)
                    step(e.tensor_single_scalar(s1, payload[:, d, :], 2047, ALU.bitwise_and))
                    e.tensor_copy(pay_hi, s0)
                    step(e.tensor_copy(pay_lo, s1))
                step(e.tensor_scalar(position, iota_cols[:], float(P), pad_position[:, 0:1], ALU.mult, ALU.add))

                def onehot(b, k, q, number=iota_bucket):
                    v.wait_ge(S["onehot_used"], q)
                    e.tensor_scalar(onehot_bucket[:, k, :], bucket, number[:, b], None, ALU.is_equal
                                    ).then_inc(S["onehot_ready"], 1)

                with v.Fori(0, NB // 2) as r:
                    for k in range(2):
                        onehot(bass.ds(r * 2 + k, 1), k, r * 2 + (q0 + k + 1), iota_down)
                v.wait_ge(S["onehot_used"], q0 + NB + 2)
                for h in range(2):
                    cols = slice(h * HS, h * HS + HS)
                    step(e.tensor_tensor_scan(prefix[:, cols], ones_wide[:], banks[h][:, 0:HS],
                                              prefix[:, HS - 1:HS] if h else 0.0, ALU.mult, ALU.add))
                step(e.tensor_scalar(bucket_i[:, 0:1], prefix[:, NS - 1:NS], float(P - 1), None, ALU.add))
                step(e.tensor_single_scalar(bucket_i[:, 1:2], bucket_i[:, 0:1], 7, ALU.arith_shift_right))
                e.tensor_scalar(bucket_slots16[:], bucket_i[:, 1:2], 1.0, None, ALU.max
                                ).then_inc(S["slots16_ready"], 1)
                v.wait_ge(S["slot_prefix_ready"], d + 1)
                step(e.tensor_copy(first_slot[0:1, d, 0:NB], banks[7][0:1, 0:NB]))
                step(e.tensor_scalar(bucket_slots[:, 0:1], banks[6][:, 0:1], float(P), None, ALU.mult))
                for h in range(2):
                    cols = slice(h * HS, h * HS + HS)
                    step(e.scalar_tensor_tensor(out=s0[:, cols], in0=prefix[:, cols], scalar=bucket_slots[:, 0:1],
                                                in1=banks[h][:, 0:HS], op0=ALU.add, op1=ALU.subtract))
                e.tensor_single_scalar(s1[0:HALF], s0[0:HALF], 6, ALU.arith_shift_right)
                step(e.tensor_single_scalar(s1[HALF:P], s0[HALF:P], RADIX - 1, ALU.bitwise_and))
                e.tensor_copy(base_digits, s1).then_inc(S["base_ready"], 1)
                def merge(k, q, m):
                    v.wait_ge(S["onehot_used"], q)
                    v.sem_inc(S["turn"], 1)
                    for h in range(2):
                        cols = slice(h * HS, h * HS + HS)
                        ins = e.copy_predicated(position[:, cols], onehot_bucket[:, k, cols].bitcast(U16),
                                                banks[2 + 2 * k + h][:, 0:HS])
                    ins.then_inc(S["merged"], 1)
                    v.wait_ge(S["merged"], m)
                q1 = q0 + NB
                with v.Fori(0, NB // 2) as r:
                    for k in range(2):
                        onehot(bass.ds(r * 2 + k, 1), k, r * 2 + (q1 + k + 1))
                        merge(k, r * 2 + (q1 + k + 3), r * 2 + (d * NB + k + 3))
                step(e.tensor_copy(s0, position))
                e.tensor_single_scalar(s1, s0, 7, ALU.arith_shift_right)
                step(e.tensor_single_scalar(s2, s0, P - 1, ALU.bitwise_and))
                if d == 0:
                    e.tensor_copy(slot_of, s1)
                    e.tensor_copy(row_of, s2)
                e.scalar_tensor_tensor(out=list_at[:, d, :], in0=s2, scalar=float(2 * NS), in1=s1,
                                       op0=ALU.mult, op1=ALU.add).then_inc(S["list_at_ready"], 1)
                v.wait_ge(S["list_at_ready"], d + 1)

            positions(0)
            positions(1)
            layer_norm()

            def sort_step(t, k, u):
                v.wait_ge(S["sort_used"], u)
                for half, pay in ((0, pay_hi), (1, pay_lo)):
                    e.tensor_scalar(row_payload[:, k, half * P:half * P + P], iota_cols[:, 0:P],
                                    row_of[:, bass.ds(t, 1)], pay[:, bass.ds(t, 1)],
                                    ALU.is_equal, ALU.mult)
                e.tensor_scalar(slot_onehot[:, k, :], iota_cols[:], slot_of[:, bass.ds(t, 1)], None,
                                ALU.is_equal).then_inc(S["sort_ready"], 1)

            with v.Fori(0, SORTED_TILES // 2) as r:
                for k in range(2):
                    sort_step(r * 2 + k, k, r * 2 + (k + 1))
            v.wait_ge(S["sort_summed"], 1)
            for d in range(2):
                s0, s1, s2 = scratch
                v.wait_ge(S["list_in"], d * 16 + 16)
                listed = raw_list[:, d, :]
                if d == 0:
                    for h in range(2):
                        cols = slice(h * HS, h * HS + HS)
                        step(e.tensor_tensor(s0[:, cols], sort_lo[h][:, 0:HS], listed[:, cols], ALU.add))
                        step(e.scalar_tensor_tensor(out=s1[:, cols], in0=sort_hi[h][:, 0:HS], scalar=2048.0,
                                                    in1=s0[:, cols], op0=ALU.mult, op1=ALU.add))
                    listed = s1
                step(e.tensor_single_scalar(s2, listed, 255, ALU.bitwise_and))
                step(e.tensor_scalar(node_in_bucket[:, d, :], s2, -1.0, None, ALU.add))
                e.tensor_single_scalar(gather_row[:, d, :], listed, 8, ALU.arith_shift_right
                                       ).then_inc(S["decoded"], 1)
                v.wait_ge(S["decoded"], d + 1)

            def bucket_mean(d, j, dest):
                lo = v.value_load(first_slot[0:1, d, bass.ds(j, 1)], min_val=0, max_val=NS - 1)
                hi = v.value_load(first_slot[0:1, d, bass.ds(j + 1, 1)], min_val=1, max_val=NS)
                with v.Fori(lo, hi) as i:
                    v.wait_ge(S["slot_done"], i + (d * NS + RING + 1 - OH))
                    e.tensor_scalar(onehot_node[:, bass.ds(i % OH, 1), :].rearrange("p a m -> p (a m)"),
                                    iota_cols[:, 0:P], node_in_bucket[:, d, bass.ds(i, 1)], None,
                                    ALU.is_equal).then_inc(S["node_onehot_ready"], 1)
                v.wait_ge(S["bucket_done"], j + (d * NB + 1))
                e.tensor_scalar(has_edge[:, d, bass.ds(j, 1)], counts[:, 0:1], 1.0, None, ALU.min)
                e.tensor_scalar(inv_count[:, 0:1], counts[:, 0:1], 1.0, None, ALU.max
                                ).then_inc(S["inv_step"], 1)
                v.wait_ge(S["inv_step"], j * 2 + (d * 2 * NB + 1))
                e.reciprocal(inv_count[:, 1:2], inv_count[:, 0:1]).then_inc(S["inv_ready"], 1)
                v.wait_ge(S["inv_ready"], j + (d * NB + 1))
                e.tensor_scalar(inv_count[:, 2:3], inv_count[:, 1:2], 1.0 / LO_SCALE, None, ALU.mult
                                ).then_inc(S["inv_step"], 1)
                v.wait_ge(S["inv_step"], j * 2 + (d * 2 * NB + 2))
                v.wait_ge(S["hi_mean_ready"], j + (d * NB + 1))
                e.scalar_tensor_tensor(out=dest, in0=sums[:, D:2 * D], scalar=inv_count[:, 2:3],
                                       in1=hi_mean[:], op0=ALU.mult, op1=ALU.add).then_inc(S["evac_done"], 1)

            with v.Fori(0, NB) as j:
                bucket_mean(0, j, mean_a[:, bass.ds(j, 1), :].rearrange("p a d -> p (a d)"))
                v.wait_ge(S["evac_done"], j + 2)

            v.sem_inc(S["x_used"], CREDIT)
            v.sem_inc(S["h2_ready"], CREDIT)
            v.sem_inc(S["combined"], CREDIT)
            PER = 56
            v.wait_ge(S["small_in"], 6 * 16)
            with v.Fori(0, NB // 2) as r:
                n = [0]

                def link(ins):
                    n[0] += 1
                    ins.then_inc(S["dve_tile"], 1)
                    v.wait_ge(S["dve_tile"], r * PER + n[0])

                for jj in range(2):
                    j = r * 2 + jj
                    j1 = r * 2 + (jj + 1)
                    e.tensor_copy(mean_a_t, mean_a[:, bass.ds(j, 1), :].rearrange("p a d -> p (a d)"))
                    v.wait_ge(x_landed[jj], r * 16 + 16)
                    e.tensor_scalar(h_t, x_t[:, jj, :], moments[:, bass.ds(j, 1), 0], rstd[:, bass.ds(j, 1)],
                                    ALU.subtract, ALU.mult).then_inc(S["h_tile_ready"], 1)
                    v.wait_ge(S["h_tile_ready"], j1)
                    e.tensor_tensor(xh_t, x_t[:, jj, :], h_t, ALU.add).then_inc(S["x_used"], 1)
                    bucket_mean(1, j, mean_b[:])
                    e.tensor_copy(flags[:, 0:2], has_edge[:, :, bass.ds(j, 1)].rearrange("p a b -> p (a b)")
                                  ).then_inc(S["flags_ready"], 1)
                    v.wait_ge(S["tile_b_turned"], j1)
                    e.tensor_copy(tile_in[:, 4:6, :], banks[1][:, 0:D].rearrange("p (a b) -> p a b", a=2))
                    e.tensor_copy(flags_T, banks[1][0:4, D:D + P]).then_inc(S["tile_b_ready"], 1)
                    v.wait_ge(S["n_summed"], j1)
                    v.wait_ge(S["rz_ready"], j1)
                    link(e.scalar_tensor_tensor(out=gate_tmp, in0=gates[:, 0:D], scalar=1.0,
                                                in1=banks[3][:, D:2 * D], op0=ALU.add, op1=ALU.mult))
                    e.scalar_tensor_tensor(out=gate_tmp, in0=gate_tmp, scalar=0.5, in1=banks[3][:, 0:D],
                                           op0=ALU.mult, op1=ALU.add).then_inc(S["pre_new_ready"], 1)
                    v.wait_ge(S["new_ready"], j1)
                    link(e.tensor_tensor(new_t, new_t, h_t, ALU.subtract))
                    link(e.scalar_tensor_tensor(out=new_t, in0=gates[:, D:2 * D], scalar=1.0, in1=new_t,
                                                op0=ALU.add, op1=ALU.mult))
                    link(e.scalar_tensor_tensor(out=x1[:, jj, :], in0=new_t, scalar=0.5, in1=xh_t,
                                                op0=ALU.mult, op1=ALU.add))
                    link(e.bn_stats(ln_s[:, 0:6], x1[:, jj, :]))
                    v.sem_inc(S["turn"], 1)
                    e.bn_aggr(ln_s[:, 6:8], ln_s[:, 0:6]).then_inc(S["var_ready"], 1)
                    v.wait_ge(S["std_ready"], j1)
                    link(e.reciprocal(ln_s[:, 9:10], ln_s[:, 8:9]))
                    e.tensor_scalar(xn, x1[:, jj, :], ln_s[:, 6:7], ln_s[:, 9:10], ALU.subtract, ALU.mult
                                    ).then_inc(S["xn_ready"], 1)

                v.wait_ge(S["logits_summed"], r + 1)
                link(e.tensor_tensor(logits[:], banks[6][:, 0:2 * NE].rearrange("p (a b) -> p a b", a=2),
                                     r_b2[:], ALU.add))
                link(e.tensor_reduce(rt[:, 0:2], logits[:], AX_X, ALU.max))
                link(e.tensor_scalar(rt[:, 2:4], rt[:, 0:2], -1.0, None, ALU.mult))
                v.sem_inc(S["shifted_ready"], 2)
                v.wait_ge(S["exp_ready"], r * 2 + 2)
                link(e.reciprocal(rt[:, 6:8], rt[:, 4:6]))
                for tt in range(2):
                    link(e.tensor_scalar(prob[:, tt, 0:NE], prob[:, tt, 0:NE], rt[:, 6 + tt:7 + tt], None,
                                         ALU.mult))
                for tt in range(2):
                    v.sem_inc(S["turn"], 1)
                    link(e.max(top[:, tt, :], prob[:, tt, :]))
                    v.sem_inc(S["turn"], 1)
                    link(e.max_index(top_at[:, tt, :], top[:, tt, :], prob[:, tt, :]))
                e.tensor_tensor(rt[:, 8:10], top[:, :, 1], top[:, :, 0], ALU.subtract
                                ).then_inc(S["prob_gap_ready"], 1)
                link(e.tensor_copy(rt[:, 16:20].rearrange("p (a b) -> p a b", a=2), top_at[:, :, 0:2]))
                v.wait_ge(S["gap_exp_ready"], r + 1)
                link(e.tensor_scalar(rt[:, 12:14], rt[:, 10:12], 1.0, None, ALU.add))
                link(e.reciprocal(rt[:, 20:22], rt[:, 12:14]))
                link(e.tensor_tensor(rt[:, 22:24], rt[:, 10:12], rt[:, 20:22], ALU.mult))
                for tt in range(2):
                    e.tensor_scalar(coef[:, tt, :], iota_bucket[:, 0:NE], rt[:, 16 + 2 * tt:17 + 2 * tt],
                                    rt[:, 20 + tt:21 + tt], ALU.is_equal, ALU.mult)
                    link(e.tensor_scalar(coef2[:, tt, :], iota_bucket[:, 0:NE], rt[:, 17 + 2 * tt:18 + 2 * tt],
                                         rt[:, 22 + tt:23 + tt], ALU.is_equal, ALU.mult))
                link(e.tensor_tensor(coef[:], coef[:], coef2[:], ALU.add))
                v.sem_inc(S["coef_ready"], 1)

                def expert_layer2(x_):
                    v.wait_ge(S["l3_summed"], r * NE + (x_ + 1))
                    v.sem_inc(S["turn"], 1)
                    v.wait_ge(S["l2_summed"], r * NE + (x_ + 1 + CREDIT))
                    bank = banks[1 if x_ % 2 == 0 else 5]
                    for m in range(2):
                        ins = e.tensor_scalar(h2[:, x_ % 2, m, :], bank[:, m * 2 * P:(m + 1) * 2 * P],
                                              e_b2[:, x_, m:m + 1], 0.0, ALU.add, ALU.max)
                    ins.then_inc(S["h2_ready"], 1)

                def combine(x_):
                    v.wait_ge(S["l3_summed"], r * NE + (x_ + 1 + CREDIT))
                    for tt in range(2):
                        ins = e.scalar_tensor_tensor(out=acc[:, tt, :], in0=banks[2 + x_ % 2][:, tt * D:tt * D + D],
                                                     scalar=coef[:, tt, x_:x_ + 1], in1=acc[:, tt, :],
                                                     op0=ALU.mult, op1=ALU.add)
                    ins.then_inc(S["combined"], 1)
                    v.wait_ge(S["combined"], r * NE + (x_ + 1 + CREDIT))

                v.wait_ge(S["coef_turned"], r + 1)
                e.tensor_copy(coef_T, banks[7][0:NE, 0:2 * P].rearrange("p (a b) -> p a b", a=2)
                              ).then_inc(S["coef_T_ready"], 1)
                expert_layer2(0)
                v.wait_ge(S["acc_free"], r + 1)
                v.sem_inc(S["turn"], 1)
                v.wait_ge(S["b3_summed"], r + 1)
                for tt in range(2):
                    link(e.tensor_tensor(acc[:, tt, :], banks[7][:, tt * D:tt * D + D], x1[:, tt, :], ALU.add))
                for x_ in range(1, NE + 1):
                    if x_ < NE:
                        expert_layer2(x_)
                    combine(x_ - 1)
                v.sem_inc(S["acc_done"], 1)
                while n[0] < PER:
                    v.sem_inc(S["dve_tile"], 1)
                    n[0] += 1

        @block.tensor
        def _(pe):
            t = nc.tensor
            pe.sem_inc(S["onehot_used"], 2)
            pe.sem_inc(S["sort_used"], 2)
            pe.sem_inc(S["slot_done"], RING)
            pe.sem_inc(S["evac_done"], 1)
            pe.sem_inc(S["l2_summed"], CREDIT)
            pe.sem_inc(S["l3_summed"], CREDIT)
            pe.wait_ge(S["fold_in"], 11 * 16)
            for a_ in range(2):
                for c in range(2):
                    m = 2 * a_ + c
                    for bank, lo_, hi_ in ((banks[2 * m], 0, 2 * D), (banks[2 * m + 1], 2 * D, G3)):
                        for k in range(2):
                            ins = t.matmul(bank[:, 0:hi_ - lo_], w_conv[:, 2 * a_ + k, c * P:c * P + P],
                                           w_ih_raw[:, 2 * a_ + k, lo_:hi_], start=(k == 0), stop=(k == 1))
            ins.then_inc(S["fold_summed"], 1)
            pe.wait_ge(S["fold_done"], 1)
            bc = b_conv[:].rearrange("p (a c m) -> p a c m", a=2, c=2)
            for bank, lo_, hi_ in ((banks[0], 0, 2 * D), (banks[1], 2 * D, G3)):
                for n_ in range(4):
                    ins = t.matmul(bank[0:2, 0:hi_ - lo_], bc[:, n_ // 2, n_ % 2, :], w_ih_raw[:, n_, lo_:hi_],
                                   start=(n_ == 0), stop=(n_ == 3))
            ins.then_inc(S["fold_summed"], 1)
            pe.wait_ge(S["fold_done"], 2)
            pe.wait_ge(S["consts"], N_CONSTS)
            for d in range(2):
                q0 = d * 2 * NB
                for h in range(2):
                    t.matmul(banks[h][:, 0:HS], zeros16[:, 0:P], zeros16[:, 0:HS], start=True, stop=False,
                             skip_group_check=True)
                with pe.Fori(0, NB // 2) as r:
                    for k in range(2):
                        b = r * 2 + k
                        pe.wait_ge(S["onehot_ready"], r * 2 + (q0 + k + 1))
                        for h in range(2):
                            ins = t.matmul(banks[h][:, 0:HS], pick_row[:, bass.ds(b + (P - NB), P)],
                                           onehot_bucket[:, k, h * HS:h * HS + HS], start=False, stop=False,
                                           skip_group_check=True)
                        ins.then_inc(S["onehot_used"], 1)
                pe.wait_ge(S["slots16_ready"], d + 1)
                t.matmul(banks[6][:, 0:1], lower_bucket[:], bucket_slots16[:], start=True, stop=True)
                t.matmul(banks[7][0:1, 0:NB], bucket_slots16[:], lower_bucket[:, 0:NB], start=True, stop=True
                         ).then_inc(S["slot_prefix_ready"], 1)
                pe.wait_ge(S["base_ready"], d + 1)
                with pe.Fori(0, NB // 2) as r:
                    for k in range(2):
                        b = r * 2 + k
                        pe.wait_ge(S["merged"], r * 2 + (d * NB + k + 1))
                        pe.wait_ge(S["onehot_ready"], r * 2 + (q0 + NB + k + 1))
                        for h in range(2):
                            o = banks[2 + 2 * k + h][:, 0:HS]
                            cols = slice(h * HS, h * HS + HS)
                            t.matmul(o, lower[:], onehot_bucket[:, k, cols], start=True, stop=False)
                            ins = t.matmul(o, spread_row[:, bass.ds(b, 1), :].rearrange("p a m -> p (a m)"),
                                           base_digits[:, cols], start=False, stop=True)
                        ins.then_inc(S["onehot_used"], 1)

            def sort_products(k):
                for bank, half in ((sort_hi, 0), (sort_lo, 1)):
                    for h in range(2):
                        ins = t.matmul(bank[h][:, 0:HS], row_payload[:, k, half * P:half * P + P],
                                       slot_onehot[:, k, h * HS:h * HS + HS], start=False, stop=False,
                                       skip_group_check=True)
                return ins

            def clear_sort():
                for bank in (*sort_hi, *sort_lo):
                    t.matmul(bank[:, 0:HS], zeros16[:, 0:P], zeros16[:, 0:HS], start=True, stop=False,
                             skip_group_check=True)

            pe.wait_ge(S["merged"], 2 * NB + 2)
            clear_sort()
            with pe.Fori(0, SORTED_TILES // 2) as r:
                for k in range(2):
                    pe.wait_ge(S["sort_ready"], r * 2 + (k + 1))
                    sort_products(k).then_inc(S["sort_used"], 1)
            pe.wait_ge(S["sort_used"], SORTED_TILES + 2)
            pe.sem_inc(S["sort_summed"], 1)

            def bucket_sum(d, j):
                lo = pe.value_load(first_slot[0:1, d, bass.ds(j, 1)], min_val=0, max_val=NS - 1)
                hi = pe.value_load(first_slot[0:1, d, bass.ds(j + 1, 1)], min_val=1, max_val=NS)
                pe.wait_ge(S["evac_done"], j + (d * NB + 1))
                t.matmul(sums[:, :], zeros16[:, 0:P], zeros16[:], start=True, stop=False,
                         skip_group_check=True)
                t.matmul(counts[:, 0:1], zeros16[:, 0:P], ones_col[:], start=True, stop=False,
                         skip_group_check=True)
                with pe.Fori(lo, hi) as i:
                    pe.wait_ge(S["node_onehot_ready"], i + (d * NS + 1))
                    pe.wait_ge(S["rows_landed"], i + (d * NS + 1))
                    pe.sem_inc(S["turn"], 1)
                    oh = onehot_node[:, bass.ds(i % OH, 1), :].rearrange("p a m -> p (a m)")
                    t.matmul(sums[:, :], oh, ring[:, bass.ds(i % RING, 1), :].rearrange("p a m -> p (a m)"),
                             start=False, stop=False, skip_group_check=True)
                    t.matmul(counts[:, 0:1], oh, ones_col[:], start=False, stop=False,
                             skip_group_check=True).then_inc(S["slot_done"], 1)
                t.matmul(counts[:, 0:1], zeros16[:, 0:P], ones_col[:], start=False, stop=True,
                         skip_group_check=True).then_inc(S["bucket_done"], 1)

            with pe.Fori(0, NB) as j:
                bucket_sum(0, j)
            pe.wait_ge(S["small_in"], 6 * 16)
            pe.wait_ge(S["experts_in"], 5 * 16)

            with pe.Fori(0, NB // 2) as r:
                for jj in range(2):
                    j = r * 2 + jj
                    j1 = r * 2 + (jj + 1)
                    pe.wait_ge(S["h_tile_ready"], j1)
                    for c in range(2):
                        t.transpose(banks[0][:, c * P:c * P + P], mean_a_t[:, c * P:c * P + P], ident[:])
                    for c in range(2):
                        ins = t.transpose(banks[0][:, (2 + c) * P:(3 + c) * P], h_t[:, c * P:c * P + P], ident[:])
                    ins.then_inc(S["tile_a_turned"], 1)
                    bucket_sum(1, j)
                    pe.wait_ge(S["evac_done"], r * 2 + (NB + 2 + jj))
                    for c in range(2):
                        t.transpose(banks[1][:, c * P:c * P + P], mean_b[:, c * P:c * P + P], ident[:])
                    pe.wait_ge(S["flags_ready"], j1)
                    t.transpose(banks[1][0:4, D:D + P], flags[:], ident[:]).then_inc(S["tile_b_turned"], 1)
                    pe.wait_ge(S["tile_a_ready"], j1)
                    order = ((0, 0), (1, 1), (2, 4), (3, 5), (4, 2), (5, 3))
                    for n_, (src_, wt) in enumerate(order):
                        if n_ == 4:
                            pe.wait_ge(S["tile_b_ready"], j1)
                        t.matmul(banks[2][:], tile_in[:, src_, :], w_gate[:, wt, 0:2 * D], start=(n_ == 0),
                                 stop=False)
                    t.matmul(banks[2][:], flags_T, gate_bias[:, 0:2 * D], start=False, stop=True
                             ).then_inc(S["rz_summed"], 1)
                    for n_, (src_, wt) in enumerate(order):
                        part = slice(D, 2 * D) if wt >= 4 else slice(0, D)
                        t.matmul(banks[3][:, part], tile_in[:, src_, :], w_gate[:, wt, 2 * D:G3],
                                 start=(n_ == 0), stop=False, skip_group_check=True)
                    t.matmul(banks[3][:], flags_T, gate_bias[:, 2 * D:G3 + D], start=False, stop=True,
                             skip_group_check=True).then_inc(S["n_summed"], 1)
                    pe.wait_ge(S["xn_ready"], j1)
                    for c in range(2):
                        ins = t.transpose(banks[6][:, c * P:c * P + P], xn[:, c * P:c * P + P], ident[:])
                    ins.then_inc(S["xn_turned"], 1)
                pe.wait_ge(S["xn_T_ready"], r * 2 + 2)
                for k in range(2):
                    ins = t.matmul(banks[7][:, 0:2 * P], r_w1[:, k, :], xn_T[:, k, :], start=(k == 0), stop=(k == 1))
                ins.then_inc(S["router_summed"], 1)

                def layer1(x_):
                    pe.wait_ge(S["h1_ready"], r * NE + (x_ + 1))
                    bank = banks[0 if x_ % 2 == 0 else 6]
                    for m in range(2):
                        for k in range(2):
                            ins = t.matmul(bank[:, m * 2 * P:(m + 1) * 2 * P],
                                           e_w[0][:, 2 * x_ + k, m * P:m * P + P], xn_T[:, k, :],
                                           start=(k == 0), stop=(k == 1))
                    ins.then_inc(S["l1_summed"], 1)

                def layer2(x_):
                    pe.wait_ge(S["h2_ready"], r * NE + (x_ + 1))
                    pe.wait_ge(S["h1_ready"], r * NE + (x_ + 1 + CREDIT))
                    bank = banks[1 if x_ % 2 == 0 else 5]
                    for m in range(2):
                        for k in range(2):
                            ins = t.matmul(bank[:, m * 2 * P:(m + 1) * 2 * P],
                                           e_w[1][:, 2 * x_ + k, m * P:m * P + P], h1[:, x_ % 2, k, :],
                                           start=(k == 0), stop=(k == 1))
                    ins.then_inc(S["l2_summed"], 1)

                def layer3(x_):
                    pe.wait_ge(S["combined"], r * NE + (x_ + 1))
                    pe.wait_ge(S["h2_ready"], r * NE + (x_ + 1 + CREDIT))
                    for tt in range(2):
                        for k in range(2):
                            ins = t.matmul(banks[2 + x_ % 2][:, tt * D:tt * D + D],
                                           h2[:, x_ % 2, k, tt * P:tt * P + P], e_w[2][:, 2 * x_ + k, :],
                                           start=(k == 0), stop=(k == 1))
                    ins.then_inc(S["l3_summed"], 1)

                layer1(0)
                pe.wait_ge(S["router_ready"], r + 1)
                for tt in range(2):
                    ins = t.matmul(banks[6][:, tt * NE:tt * NE + NE], router_h[:, tt * P:tt * P + P], r_w2[:],
                                   start=True, stop=True)
                ins.then_inc(S["logits_summed"], 1)
                pe.wait_ge(S["coef_ready"], r + 1)
                for tt in range(2):
                    ins = t.transpose(banks[7][0:NE, tt * P:tt * P + P], coef[:, tt, :], ident[:])
                ins.then_inc(S["coef_turned"], 1)
                layer1(1)
                layer2(0)
                pe.wait_ge(S["coef_T_ready"], r + 1)
                for tt in range(2):
                    ins = t.matmul(banks[7][:, tt * D:tt * D + D], coef_T[:, tt, :], e_b3[:], start=True, stop=True)
                ins.then_inc(S["b3_summed"], 1)
                for x_ in range(2, NE + 2):
                    if x_ < NE:
                        layer1(x_)
                    if x_ - 1 < NE:
                        layer2(x_ - 1)
                    layer3(x_ - 2)


def kernel(**inputs):
    import numpy as _np
    import concourse.bacc as _bacc
    from concourse.bass_utils import run_bass_kernel_spmd as _run

    nc = _bacc.Bacc("TRN2", target_bir_lowering=False, num_devices=1)
    x = _np.asarray(inputs["x"])
    xp = _np.zeros((NP, D), x.dtype)
    xp[:NODES] = x
    edges = _np.full((2, NS * P), SENTINEL, _np.int32)
    edges[0, :EDGES] = inputs["dst"]
    edges[1, :EDGES] = inputs["src"]
    edges = _np.ascontiguousarray(edges.reshape(2, NS, P).transpose(2, 0, 1))
    g = {n.split("_", 1)[1]: _np.asarray(a) for n, a in inputs.items() if n.startswith("L0_")}
    arrays = {
        "in_x": xp, "in_edges": edges,
        "in_w_ih_T": g["gnn_W_ih"].T, "in_w_hh_T": g["gnn_W_hh"].T, "in_w_in": g["gnn_W_in"],
        "in_w_out": g["gnn_W_out"], "in_b_in": g["gnn_b_in"][:, None], "in_b_out": g["gnn_b_out"][:, None],
        "in_b_ih": g["gnn_b_ih"][None], "in_b_hh": g["gnn_b_hh"][None],
        "in_r_w1": g["ffn_router_w1"], "in_r_b1": g["ffn_router_b1"][:, None],
        "in_r_w2": g["ffn_router_w2"], "in_r_b2": g["ffn_router_b2"][None],
        "in_e_w1": g["ffn_expert_w1"], "in_e_w2": g["ffn_expert_w2"], "in_e_w3": g["ffn_expert_w3"],
        "in_e_b1": g["ffn_expert_b1"].reshape(NE, 2, P).transpose(2, 0, 1),
        "in_e_b2": g["ffn_expert_b2"].reshape(NE, 2, P).transpose(2, 0, 1), "in_e_b3": g["ffn_expert_b3"],
    }
    arrays = {n: _np.ascontiguousarray(a) for n, a in arrays.items()}
    aps = {n: nc.dram_tensor(n, a.shape, mybir.dt.from_np(a.dtype), kind="ExternalInput").ap()
           for n, a in arrays.items()}
    out = nc.dram_tensor("out_0", (NP, D), F32, kind="ExternalOutput").ap()
    table = nc.dram_tensor("split_rows", (NP, 2 * D), F16, kind="Internal").ap()
    lists = [nc.dram_tensor(f"list_{d}", (LIST, 1), I32, kind="Internal").ap() for d in range(2)]
    gnn_moe_program(nc, aps["in_x"], aps["in_edges"], {n[3:]: ap for n, ap in aps.items()}, out, table, lists)
    r = _run(nc, [arrays], core_ids=[0])
    return r.results[0]["out_0"][:NODES]
```

```python
from contextlib import ExitStack

import concourse.bass as bass
from concourse import mybir

F32 = mybir.dt.float32
F32R = mybir.dt.float32r
F16 = mybir.dt.float16
I32 = mybir.dt.int32
U16 = mybir.dt.uint16
U32 = mybir.dt.uint32
ALU = mybir.AluOpType
ACT = mybir.ActivationFunctionType
AX_X = mybir.AxisListType.X

P = 128
NODES = 6250
EDGES = 100000
D = 256
NB = 50
NP = NB * P
NS = 832
HS = NS // 2
HALF = 64
RADIX = 64
LO_SCALE = 2048.0
BATCH = 4
RINGS = 4
RING = BATCH * RINGS
OH = 4
BATCHES = NS // BATCH
VISITS = BATCHES - 1 + NB
KEY = 256
SCATTER = 32
SORTED_TILES = 640
LIST = 2 * NS * P
SENTINEL = 8191
EPS = 1e-5
ROOT_SEED = 0x5F3759DF
ROOT_STEPS = 3
LB = 5
GATE_STEPS = 7 + 3 + 3 * ROOT_STEPS
FFN_STEPS = 19
LN_STEPS = 2 + 3 + 3 * ROOT_STEPS + 1
NE = 6
G3 = 3 * D
CREDIT = 2
assert EDGES // P + NB + 1 <= NS and NS % BATCH == 0


def gnn_moe_program(nc, x, edges, w, out, table, lists, means):
    ctx = ExitStack()
    with ctx:
        def sb(name, shape, dt):
            return ctx.enter_context(nc.sbuf_tensor(name, shape, dt))

        def sem(name):
            return ctx.enter_context(nc.semaphore(name))

        banks = [ctx.enter_context(nc.psum_tensor(f"bank{i}", [P, 512], F32)) for i in range(8)]

        iota_cols = sb("iota_cols", [P, NS], F16)
        pad_position = sb("pad_position", [P, 1], F32)
        iota_bucket = sb("iota_bucket", [P, NB], F32)
        iota_down = sb("iota_down", [P, NB], F32)
        ones_col = sb("ones_col", [P, 1], F16)
        zeros16 = sb("zeros16", [P, 512], F16)
        ident = sb("ident", [P, P], F32)

        REGION = 38272
        region_at = -(-nc.sbuf_base // 32) * 32
        sb("region", [P, REGION], F32)
        at = {"sort": 0, "dense": 0}

        def carve(user, shape, dt=F32, twin=False):
            words = 1
            for n in shape:
                words *= n
            words = words // 2 if dt == F16 else words
            words = -(-words // 8) * 8
            offset = region_at + 4 * at[user]
            at[user] += words
            assert at[user] <= REGION, (user, at[user])
            views = [nc.alloc_sbuf_tensor_at(f"{user}_{at[user]}{mark}", [P, *shape], dt_, offset=offset)[:]
                     for mark, dt_ in (("", dt), ("_low", F32R))[0:2 if twin else 1]]
            return views if twin else views[0]

        def twin_sb(name, shape):
            offset = -(-nc.sbuf_base // 32) * 32
            whole = sb(name, shape, F32)
            return whole, nc.alloc_sbuf_tensor_at(name + "_low", shape, F32R, offset=offset)

        ones_wide = carve("sort", [HS])
        lower = carve("sort", [P], F16)
        pick_row = carve("sort", [256], F16)
        lower_bucket = carve("sort", [P], F16)
        spread_row = carve("sort", [NB, P], F16)
        key = carve("sort", [2, NS], I32)
        scratch = [carve("sort", [NS], I32) for i in range(3)]
        valid = carve("sort", [NS], F32)
        bucket = carve("sort", [NS], F16)
        prefix = carve("sort", [NS], F32)
        base_digits = carve("sort", [NS], F16)
        bucket_slots = sb("bucket_slots", [P, 4], F32)
        bucket_slots16 = sb("bucket_slots16", [P, 1], F16)
        bucket_i = sb("bucket_i", [P, 2], I32)
        onehot_bucket = carve("sort", [2, NS], F16)
        position = carve("sort", [NS], F32)
        slot_of = carve("sort", [NS])
        row_of = carve("sort", [NS])
        pay_hi = carve("sort", [NS])
        pay_lo = carve("sort", [NS])
        list_at = carve("sort", [2, NS], I32)
        payload = carve("sort", [2, NS], I32)
        raw_list = list_at
        at_stage = carve("sort", [2, SCATTER], I32)
        payload_stage = carve("sort", [2, SCATTER], I32)
        first_slot = sb("first_slot", [P, 2], F32)
        first_batch = sb("first_batch", [1, 2, 64], I32)
        first_row = sb("first_row", [1, 64], I32)
        ones16 = sb("ones16", [NB, P], F16)
        bucket_key = sb("bucket_key", [P, NB], F32)
        node_key = sb("node_key", [P, P], F32)
        row_payload = carve("sort", [2, 2 * P], F16)
        gather_row_0 = carve("sort", [NS], I32)
        receiver_0 = carve("sort", [NS])
        at["norm"] = at["sort"]
        ln_x = [carve("norm", [LB, D]) for _ in range(2)]
        ln_h = [carve("norm", [LB, D]) for _ in range(2)]
        ln_split = [carve("norm", [LB, 2 * D], F16) for _ in range(2)]
        ln_stats = carve("norm", [2, LB, 6])
        ln_mv = carve("norm", [2, LB, 2])
        ln_rstd = carve("norm", [2, LB])
        ln_work = carve("norm", [2, 2, LB])
        slot_onehot = onehot_bucket
        gather_row = [gather_row_0, sb("gather_row_1", [P, NS], I32)]
        receiver = [receiver_0, sb("receiver_1", [P, NS], F32)]

        moments = sb("moments", [P, NB, 2], F32)
        rstd = sb("rstd", [P, NB], F32)

        ring = sb("ring", [P, RING, 2 * D], F16)
        index_stage = sb("index_stage", [P, RINGS, BATCH], I32)
        onehot_node = sb("onehot_node", [P, OH, BATCH, P], F16)
        inv_count = sb("inv_count", [P, 4], F32)
        hi_mean = sb("hi_mean", [P, D], F32)
        mean_b = sb("mean_b", [P, D], F32)
        has_edge = sb("has_edge", [P, 2, NB], F32)

        w_gate, gate_lo = twin_sb("w_gate", [P, 6, G3])
        gate_bias, bias_lo = twin_sb("gate_bias", [4, G3 + D])
        ring_words = ring[:].rearrange("p a b -> p (a b)").bitcast(F32)
        w_ih_raw = ring_words[:, 0:4 * G3].rearrange("p (a b) -> p a b", a=4)
        w_conv = ring_words[:, 4 * G3:4 * G3 + 4 * D].rearrange("p (a b) -> p a b", a=4)
        b_conv = sb("b_conv", [P, 8], F32)
        r_b1 = sb("r_b1", [P, 1], F32)
        r_w2 = sb("r_w2", [P, NE], F32)
        r_b2 = sb("r_b2", [P, 2, NE], F32)
        e_b1 = sb("e_b1", [P, NE, 2], F32)
        e_b2 = sb("e_b2", [P, NE, 2], F32)
        r_w1, r_lo = carve("dense", [2, P], twin=True)
        e_b3 = carve("dense", [D])[0:NE, :]
        e_w, e_lo = zip(*[carve("dense", [NE * 2, D], twin=True) for _ in range(3)])
        e_hi = [carve("dense", [NE * 2, D], F32R) for _ in range(3)]
        r_hi = carve("dense", [2, P], F32R)
        gate_hi = carve("dense", [6, G3], F32R)
        bias_hi = carve("dense", [G3 + D], F32R)[0:4, :]
        x_t = carve("dense", [2, D])
        h_t = carve("dense", [D])
        mean_a_t = carve("dense", [2, D])
        xh_t = carve("dense", [D])
        tile_hi, tile_lo = carve("dense", [6, P], F32R), carve("dense", [6, P], F32R)
        gates = carve("dense", [2 * D])
        gate_tmp = carve("dense", [D])
        new_t = carve("dense", [D])
        x1 = carve("dense", [2, D])
        xn = carve("dense", [2, D])
        xn_hi, xn_lo = carve("dense", [2, 2 * P], F32R), carve("dense", [2, 2 * P], F32R)
        router_h = carve("dense", [2 * P])
        h1, h1_hi, h1_lo = (carve("dense", [2, 2, 2 * P], dt) for dt in (F32, F32R, F32R))
        h2, h2_hi, h2_lo = (carve("dense", [2, 2, 2 * P], dt) for dt in (F32, F32R, F32R))
        acc = carve("dense", [2, D])
        flags = sb("flags", [P, 4], F32)
        flags_T = carve("dense", [P], F32R)[0:4, :]
        ln_s = sb("ln_s", [P, 12], F32)
        logits = sb("logits", [P, 2, NE], F32)
        prob = sb("prob", [P, 2, 8], F32)
        top = sb("top", [P, 2, 8], F32)
        top_at = sb("top_at", [P, 2, 8], U32)
        rt = sb("rt", [P, 24], F32)
        coef = sb("coef", [P, 2, NE], F32)
        coef2 = sb("coef2", [P, 2, NE], F32)
        coef_T = carve("dense", [2, P])[0:NE]

        names = ("consts const_step edges_in ln_step h_ready hi_ready "
                 "diff_ready split_ready table_stored dve_step onehot_ready onehot_used slots16_ready "
                 "slot_prefix_ready base_ready list_at_ready list_zeroed list_in scatter_staged merged sort_ready sort_used sort_summed decoded stage_ready "
                 "turn owners_marked owners_summed rows_landed slot_done node_onehot_used key_ready node_onehot_ready bucket_done inv_ready hi_mean_ready "
                 "inv_step evac_done out_done fold_in fold_zero small_in fold_summed fold_done experts_in x_used high_ready low_ready mean_a_free "
                 "h_tile_ready tile_a_turned tile_a_hi tile_a_ready tile_b_turned tile_b_ready flags_ready rz_summed "
                 "n_summed rz_ready pre_new_ready new_ready x1_ready var_ready std_ready xn_ready "
                 "xn_turned xn_hi_ready xn_T_ready router_summed router_ready logits_summed shifted_ready exp_ready "
                 "prob_gap_ready gap_exp_ready coef_ready coef_turned coef_T_ready b3_summed acc_started gate_step ffn_step l1_summed h1_hi_ready h1_ready "
                 "l2_summed h2_hi_ready h2_ready l3_summed combined acc_done acc_free out_landed").split()
        ln_in = [sem(f"ln_in{i}") for i in range(2)]
        spill_landed = [sem(f"spill_landed{i}") for i in range(2)]
        x_landed = [sem(f"x_landed{i}") for i in range(2)]
        S = {n: sem(n) for n in names}
        scatter_landed = [sem(f"scatter_landed{i}") for i in range(2)]
        ring_landed = [sem(f"ring_landed{i}") for i in range(RINGS)]
        store_landed = [sem(f"store_landed{i}") for i in range(2)]
        N_CONSTS = 16
        sums, counts = banks[4], banks[5]
        sort_hi, sort_lo = banks[0:2], banks[2:4]
        turned, rz_bank, n_bank, l1_bank, l2_bank, l3_bank = banks[0], banks[1], banks[2], banks[3], banks[6], banks[7]
        route_bank = n_bank

        def four(bank):
            return bank[:].rearrange("p (a b) -> p a b", a=4)

        def two(ap):
            return ap.rearrange("p (a b) -> p a b", a=2)

        block = ctx.enter_context(nc.Block())

        @block.gpsimd
        def _(pool):
            g = nc.gpsimd
            c = S["consts"]
            g.iota(iota_cols[:], [[1, NS]], base=0, channel_multiplier=0,
                   allow_small_or_imprecise_dtypes=True).then_inc(c, 1)
            g.iota(iota_bucket[:], [[1, NB]], base=0, channel_multiplier=0,
                   allow_small_or_imprecise_dtypes=True).then_inc(c, 1)
            g.iota(iota_down[:], [[-1, NB]], base=NB - 1, channel_multiplier=0,
                   allow_small_or_imprecise_dtypes=True).then_inc(c, 1)
            g.iota(pad_position[:], [[0, 1]], base=NS * P, channel_multiplier=1,
                   allow_small_or_imprecise_dtypes=True).then_inc(c, 1)
            g.memset(ones_col[:], 1.0).then_inc(c, 1)
            g.memset(zeros16[:], 0.0).then_inc(c, 1)
            g.memset(first_batch[:], BATCHES - 1).then_inc(c, 1)
            g.memset(ones16[:], 1.0).then_inc(c, 1)
            g.iota(bucket_key[:], [[KEY, NB]], base=KEY + 1, channel_multiplier=0,
                   allow_small_or_imprecise_dtypes=True).then_inc(c, 1)
            g.memset(ones_wide, 1.0).then_inc(c, 1)
            g.memset(lower, 1.0).then_inc(S["const_step"], 1)
            g.memset(pick_row, 0.0).then_inc(S["const_step"], 1)
            g.memset(spread_row, 0.0).then_inc(S["const_step"], 1)
            g.memset(lower_bucket, 1.0).then_inc(S["const_step"], 1)
            g.memset(ident[:], 0.0).then_inc(S["const_step"], 1)
            g.memset(gate_bias[:], 0.0).then_inc(S["fold_zero"], 1)
            g.memset(b_conv[:], 0.0).then_inc(S["fold_zero"], 1)
            g.memset(flags[:], 1.0).then_inc(c, 1)
            g.memset(prob[:], -1.0).then_inc(c, 1)
            pool.wait_ge(S["const_step"], 5)
            g.affine_select(out=spread_row, in_=spread_row, compare_op=ALU.not_equal, fill=float(RADIX),
                            base=0, pattern=[[-1, NB], [0, P]], channel_multiplier=1
                            ).then_inc(S["const_step"], 1)
            g.memset(pick_row[:, 127:128], 1.0).then_inc(S["const_step"], 1)
            g.memset(pick_row[:, 127 + HALF:128 + HALF], 1.0).then_inc(S["const_step"], 1)
            g.affine_select(out=lower, in_=lower, compare_op=ALU.is_gt, fill=0.0, base=0,
                            pattern=[[1, P]], channel_multiplier=-1).then_inc(c, 1)
            lb = lower_bucket.rearrange("p (a m) -> p a m", a=2)
            g.affine_select(out=lb, in_=lb, compare_op=ALU.is_gt, fill=0.0, base=0,
                            pattern=[[0, 2], [1, HALF]], channel_multiplier=-1).then_inc(c, 1)
            g.affine_select(out=ident[:], in_=ident[:], compare_op=ALU.not_equal, fill=1.0, base=0,
                            pattern=[[-1, P]], channel_multiplier=1).then_inc(c, 1)
            pool.wait_ge(S["const_step"], 8)
            g.affine_select(out=spread_row, in_=spread_row, compare_op=ALU.not_equal, fill=1.0,
                            base=-HALF, pattern=[[-1, NB], [0, P]], channel_multiplier=1).then_inc(c, 1)

            pool.wait_ge(S["list_zeroed"], 10 * 16)
            first = SORTED_TILES // (2 * SCATTER)
            for d, r_lo, past in ((0, first, -first), (1, 0, NS // (2 * SCATTER) - first)):
                pool.wait_ge(S["list_at_ready"], d + 1)
                with pool.Fori(r_lo, NS // (2 * SCATTER)) as r:
                    for k in range(2):
                        n_ = r + past
                        tiles = bass.ds(r * (2 * SCATTER) + k * SCATTER, SCATTER)
                        g.tensor_copy(at_stage[:, k, :], list_at[:, d, tiles]).then_inc(S["scatter_staged"], 1)
                        g.tensor_copy(payload_stage[:, k, :], payload[:, d, tiles]).then_inc(S["scatter_staged"], 1)
                        pool.wait_ge(S["scatter_staged"], n_ * 4 + (2 * k + 2))
                        pool.sem_inc(S["turn"], 1)
                        for q in range(SCATTER):
                            g.indirect_dma_start(
                                out=lists[d][:], out_offset=bass.IndirectOffsetOnAxis(ap=at_stage[:, k, q:q + 1], axis=0),
                                in_=payload_stage[:, k, q:q + 1], in_offset=None,
                            ).then_inc(scatter_landed[k], 16)
                    for k in range(2):
                        pool.wait_ge(scatter_landed[k], n_ * (16 * SCATTER) + 16 * SCATTER)
                    pool.sem_inc(S["turn"], 1)

            pool.wait_ge(S["table_stored"], NB // LB + 2)
            pool.wait_ge(S["fold_done"], 2)
            for d in range(2):
                pool.wait_ge(S["decoded"], d + 1)
                with pool.Fori(0, NS // RING) as r:
                    for k in range(RINGS):
                        pool.wait_ge(S["slot_done"], r * RING + (d * NS + k * BATCH + BATCH))
                        pool.sem_inc(S["turn"], 1)
                        g.tensor_copy(index_stage[:, k, :], gather_row[d][:, bass.ds(r * RING + k * BATCH, BATCH)]
                                      ).then_inc(S["stage_ready"], 1)
                        pool.wait_ge(S["stage_ready"], r * RINGS + (d * (NS // BATCH) + k + 1))
                        pool.sem_inc(S["turn"], 1)
                        for q in range(BATCH):
                            g.indirect_dma_start(
                                out=ring[:, k * BATCH + q, :], out_offset=None, in_=table[:],
                                in_offset=bass.IndirectOffsetOnAxis(ap=index_stage[:, k, q:q + 1], axis=0),
                            ).then_inc(ring_landed[k], 16)

        @block.sync
        def _(sp):
            sp.dma_start(key, edges).then_inc(S["edges_in"], 16)
            sp.wait_ge(S["consts"], N_CONSTS)
            for d in range(2):
                entries = lists[d].rearrange("(p n) o -> p (n o)", p=P)[:, 0:NS]
                for q in range(4):
                    sp.dma_start(entries[:, q * (NS // 4):(q + 1) * (NS // 4)],
                                 zeros16[:, 0:NS // 2].bitcast(I32)).then_inc(S["list_zeroed"], 16)
            for q in range(2):
                sp.dma_start(means[NP + q * P:NP + q * P + P, :], zeros16[:].bitcast(F32)
                             ).then_inc(S["list_zeroed"], 16)
            sp.sem_inc(S["table_stored"], 2)
            x_b = x[0:NP, :].rearrange("(s t p) d -> s p t d", t=LB, p=P)
            table_b = table.rearrange("(s t p) d -> s p t d", t=LB, p=P)
            for k in range(2):
                sp.dma_start(ln_x[k], x_b[k]).then_inc(ln_in[k], 16)

            def store_rows(r, more):
                for k in range(2):
                    sp.wait_ge(S["split_ready"], r * 2 + (k + 3))
                    sp.dma_start(table_b[bass.ds(r * 2 + k, 1), :, :, :].rearrange("a p t d -> (a p) t d"),
                                 ln_split[k]).then_inc(store_landed[k], 16)
                    if more:
                        sp.dma_start(ln_x[k], x_b[bass.ds(r * 2 + (k + 2), 1), :, :, :].rearrange("a p t d -> (a p) t d")
                                     ).then_inc(ln_in[k], 16)
                for k in range(2):
                    sp.wait_ge(store_landed[k], r * 16 + 16)
                    sp.sem_inc(S["table_stored"], 1)

            with sp.Fori(0, NB // LB // 2 - 1) as r:
                store_rows(r, True)
            store_rows(NB // LB // 2 - 1, False)
            for d in range(2):
                rounds = (d + 1) * (NS // (2 * SCATTER)) - SORTED_TILES // (2 * SCATTER)
                for k in range(2):
                    sp.wait_ge(scatter_landed[k], rounds * 16 * SCATTER)
                sp.dma_start(raw_list[:, d, :], lists[d].rearrange("(p n) o -> p (n o)", p=P)[:, 0:NS]
                             ).then_inc(S["list_in"], 16)
                sp.wait_ge(S["list_in"], d * 16 + 16)
            for d in range(2):
                if d == 0:
                    sp.wait_ge(S["decoded"], 2)
                    sp.dma_start(r_w1, w["r_w1"].rearrange("(c p) n -> p c n", p=P)).then_inc(S["experts_in"], 16)
                    sp.dma_start(e_b3, w["e_b3"]).then_inc(S["experts_in"], 16)
                    for n, name in enumerate(("e_w1", "e_w2", "e_w3")):
                        sp.dma_start(e_w[n], w[name].rearrange("e (c p) n -> p (e c) n", p=P)
                                     ).then_inc(S["experts_in"], 16)
                with sp.Fori(0, NS // RING) as r:
                    for k in range(RINGS):
                        sp.wait_ge(ring_landed[k], r * (16 * BATCH) + (d * (NS // RING) + 1) * 16 * BATCH)
                        sp.sem_inc(S["rows_landed"], 1)

        @block.scalar
        def _(act):
            a = nc.scalar
            for dst_, src_ in ((w_ih_raw, w["w_ih_T"].rearrange("(c p) n -> p c n", p=P)),
                               (w_conv[:, 0:2, :], w["w_in"].rearrange("(c p) n -> p c n", p=P)),
                               (w_conv[:, 2:4, :], w["w_out"].rearrange("(c p) n -> p c n", p=P)),
                               (w_gate[:, 4:6, :], w["w_hh_T"].rearrange("(c p) n -> p c n", p=P))):
                act.dma_start(dst_, src_).then_inc(S["fold_in"], 16)
            act.wait_ge(S["fold_zero"], 2)
            act.dma_start(gate_bias[2:3, 0:G3], w["b_ih"]).then_inc(S["fold_in"], 16)
            act.dma_start(gate_bias[2:3, G3:G3 + D], w["b_hh"][:, 2 * D:G3]).then_inc(S["fold_in"], 16)
            act.dma_start(gate_bias[3:4, 0:2 * D], w["b_hh"][:, 0:2 * D]).then_inc(S["fold_in"], 16)
            bc = b_conv[:].rearrange("p (a c m) -> p a c m", a=2, c=2)
            for n, name in enumerate(("b_in", "b_out")):
                for c in range(2):
                    act.dma_start(bc[:, n, c, n:n + 1], w[name][c * P:c * P + P, :]).then_inc(S["fold_in"], 16)
            smalls = ((r_b1[:], w["r_b1"]),
                      (r_w2[:], w["r_w2"]), (r_b2[:, 0, :], w["r_b2"].to_broadcast([P, NE])),
                      (r_b2[:, 1, :], w["r_b2"].to_broadcast([P, NE])), (e_b1[:], w["e_b1"]),
                      (e_b2[:], w["e_b2"]))
            for dst_, src_ in smalls:
                act.dma_start(dst_, src_).then_inc(S["small_in"], 16)
            act.wait_ge(S["fold_summed"], 1)
            for m in range(4):
                a.copy(w_gate[:, m, 0:2 * D], banks[2 * m][:, 0:2 * D])
                ins = a.copy(w_gate[:, m, 2 * D:G3], banks[2 * m + 1][:, 0:D])
            ins.then_inc(S["fold_done"], 1)
            act.wait_ge(S["fold_summed"], 2)
            a.copy(gate_bias[0:2, 0:2 * D], banks[0][0:2, 0:2 * D])
            a.copy(gate_bias[0:2, 2 * D:G3], banks[1][0:2, 0:D]).then_inc(S["fold_done"], 1)
            act.sem_inc(S["split_ready"], 2)
            with act.Fori(0, NB // LB // 2) as r:
                for k in range(2):
                    act.wait_ge(S["table_stored"], r * 2 + (k + 1))
                    act.sem_inc(S["turn"], 1)
                    act.wait_ge(S["h_ready"], r * 2 + (k + 1))
                    a.copy(ln_split[k][:, :, 0:D], ln_h[k]).then_inc(S["hi_ready"], 1)
                    act.wait_ge(S["diff_ready"], r * 2 + (k + 1))
                    a.activation(ln_split[k][:, :, D:2 * D], ln_h[k], ACT.Copy, scale=LO_SCALE
                                 ).then_inc(S["split_ready"], 1)

            def hi_mean_step(q):
                act.wait_ge(S["inv_ready"], q)
                a.activation(hi_mean[:], sums[:, 0:D], ACT.Copy, scale=inv_count[:, 1:2]
                             ).then_inc(S["hi_mean_ready"], 1)

            means_tiles = means.rearrange("(j p) d -> j p d", p=P)
            act.sem_inc(S["mean_a_free"], 2)
            act.wait_ge(S["decoded"], 2)
            with act.Fori(0, NB // 2) as r:
                for k in range(2):
                    hi_mean_step(r * 2 + (k + 1))
                    act.wait_ge(S["evac_done"], r * 2 + (k + 2))
                    act.dma_start(means_tiles[bass.ds(r * 2 + k, 1), :, :].rearrange("a p d -> (a p) d"),
                                  mean_a_t[:, k, :]).then_inc(spill_landed[k], 16)
                for k in range(2):
                    act.wait_ge(spill_landed[k], r * 16 + 16)
                    act.sem_inc(S["mean_a_free"], 1)
            act.wait_ge(S["experts_in"], 5 * 16)
            for hi_, raw in zip((gate_hi, bias_hi, r_hi, *e_hi), (w_gate[:], gate_bias[:], r_w1, *e_w)):
                a.copy(hi_, raw).then_inc(S["high_ready"], 1)
            x_tiles = x.rearrange("(j p) d -> j p d", p=P)
            out_tiles = out.rearrange("(j p) d -> j p d", p=P)
            act.sem_inc(S["acc_free"], 1)
            act.sem_inc(S["h1_hi_ready"], 1)
            act.sem_inc(S["h2_hi_ready"], 1)

            def load_tiles(r):
                for jj in range(2):
                    act.wait_ge(S["x_used"], r * 2 + (jj + 1))
                    for t_, src_ in ((x_t, x_tiles), (mean_a_t, means_tiles)):
                        act.dma_start(t_[:, jj, :], src_[bass.ds(r * 2 + jj, 1), :, :].rearrange("a p d -> (a p) d")
                                      ).then_inc(x_landed[jj], 16)

            def tile_a(r, o):
                act.wait_ge(S["tile_a_turned"], r * 2 + (o + 1))
                a.copy(tile_hi[:, 0:4, :], four(turned)).then_inc(S["tile_a_hi"], 1)
                hi_mean_step(r * 2 + (NB + o + 1))

            def gate_values(r, o):
                act.wait_ge(S["rz_summed"], r * 2 + (o + 1))
                a.activation(gates, rz_bank[:], ACT.Tanh, scale=0.5).then_inc(S["rz_ready"], 1)
                act.wait_ge(S["pre_new_ready"], r * 2 + (o + 1))
                a.activation(new_t, gate_tmp, ACT.Tanh).then_inc(S["new_ready"], 1)

            def turn_xn(r, o):
                jj = o % 2
                act.wait_ge(S["xn_turned"], r * 2 + (o + 1))
                a.copy(xn_hi[:, :, jj * P:jj * P + P], two(turned[:, jj * 2 * P:jj * 2 * P + 2 * P])
                       ).then_inc(S["xn_hi_ready"], 1)

            def routing(q):
                act.wait_ge(S["router_summed"], q + 1)
                a.activation(router_h, route_bank[:, 0:2 * P], ACT.Relu, bias=r_b1[:, 0:1]
                             ).then_inc(S["router_ready"], 1)
                hidden1(q, 0)
                for tt in range(2):
                    act.wait_ge(S["shifted_ready"], q * 2 + (tt + 1))
                    a.activation(prob[:, tt, 0:NE], logits[:, tt, :], ACT.Exp, bias=rt[:, 2 + tt:3 + tt],
                                 accum_out=rt[:, 4 + tt:5 + tt]).then_inc(S["exp_ready"], 1)
                act.wait_ge(S["prob_gap_ready"], q + 1)
                a.activation(rt[:, 10:12], rt[:, 8:10], ACT.Exp).then_inc(S["gap_exp_ready"], 1)

            def hidden(q, x_, used, summed, landed, bank, bias, whole, high, ready):
                act.wait_ge(used, q * NE + (x_ + 1))
                act.sem_inc(S["turn"], 1)
                act.wait_ge(summed, q * NE + (x_ + 1 + landed))
                for to in (high, whole):
                    for m in range(2):
                        ins = a.activation(to[:, x_ % 2, m, :], bank[:, m * 2 * P:(m + 1) * 2 * P], ACT.Relu,
                                           bias=bias[:, x_, m:m + 1])
                ins.then_inc(ready, 1)

            def hidden1(q, x_):
                hidden(q, x_, S["l2_summed"], S["l1_summed"], 0, l1_bank, e_b1, h1, h1_hi, S["h1_hi_ready"])

            def hidden2(q, x_):
                hidden(q, x_, S["l3_summed"], S["l2_summed"], CREDIT, l2_bank, e_b2, h2, h2_hi, S["h2_hi_ready"])

            def store_out(q):
                act.wait_ge(S["acc_done"], q + 1)
                for tt in range(2):
                    act.dma_start(out_tiles[bass.ds(q * 2 + tt, 1), :, :].rearrange("a p d -> (a p) d"),
                                  acc[:, tt, :]).then_inc(S["out_landed"], 16)
                act.wait_ge(S["out_landed"], q * 32 + 32)
                act.sem_inc(S["acc_free"], 1)

            load_tiles(0)
            for o in range(2):
                tile_a(0, o)
                gate_values(0, o)
            for o in range(2):
                turn_xn(0, o)
            load_tiles(1)
            with act.Fori(0, NB // 2 - 1) as q:
                tile_a(q, 2)
                routing(q)
                hidden1(q, 1)
                hidden2(q, 0)
                gate_values(q, 2)
                hidden1(q, 2)
                hidden2(q, 1)
                tile_a(q, 3)
                for x_ in (3, 4):
                    hidden1(q, x_)
                    hidden2(q, x_ - 1)
                gate_values(q, 3)
                hidden1(q, 5)
                hidden2(q, 4)
                hidden2(q, 5)
                for o in (2, 3):
                    turn_xn(q, o)
                load_tiles(q + 2)
                store_out(q)
            last = NB // 2 - 1
            routing(last)
            for x_ in range(1, NE + 1):
                if x_ < NE:
                    hidden1(last, x_)
                hidden2(last, x_ - 1)
            store_out(last)

        @block.vector
        def _(v):
            e = nc.vector
            steps = [0]

            def step(ins):
                steps[0] += 1
                ins.then_inc(S["dve_step"], 1)
                v.wait_ge(S["dve_step"], steps[0])

            v.wait_ge(S["consts"], N_CONSTS)
            v.wait_ge(S["edges_in"], 16)
            v.sem_inc(S["merged"], 2)
            def inverse_root(chain, y, variance, v_, t_):
                chain(e.tensor_scalar(v_, variance, EPS, None, ALU.add))
                chain(e.tensor_single_scalar(t_.bitcast(I32), v_.bitcast(I32), 1, ALU.arith_shift_right))
                chain(e.tensor_scalar(y.bitcast(I32), t_.bitcast(I32), -1.0, float(ROOT_SEED), ALU.mult, ALU.add))
                for _ in range(ROOT_STEPS):
                    chain(e.tensor_tensor(t_, y, y, ALU.mult))
                    chain(e.scalar_tensor_tensor(out=t_, in0=t_, scalar=-0.5, in1=v_, op0=ALU.mult, op1=ALU.mult))
                    chain(e.scalar_tensor_tensor(out=y, in0=t_, scalar=1.5, in1=y, op0=ALU.add, op1=ALU.mult))

            def layer_norm():
                with v.Fori(0, NB // LB // 2) as r:
                    for k in range(2):
                        v.wait_ge(ln_in[k], r * 16 + 16)
                        for t_ in range(LB):
                            ins = e.bn_stats(ln_stats[:, k, t_, :], ln_x[k][:, t_, :])
                        ins.then_inc(S["ln_step"], 1)
                        v.wait_ge(S["ln_step"], r * (2 * LN_STEPS) + (k * LN_STEPS + 1))
                        v.sem_inc(S["turn"], 1)
                        for t_ in range(LB):
                            ins = e.bn_aggr(ln_mv[:, k, t_, :], ln_stats[:, k, t_, :])
                        ins.then_inc(S["ln_step"], 1)
                        v.wait_ge(S["ln_step"], r * (2 * LN_STEPS) + (k * LN_STEPS + 2))
                        tiles = bass.ds(r * (2 * LB) + k * LB, LB)
                        e.tensor_copy(moments[:, tiles, :], ln_mv[:, k, :, :])
                        n = [2]

                        def ln_link(ins):
                            n[0] += 1
                            ins.then_inc(S["ln_step"], 1)
                            v.wait_ge(S["ln_step"], r * (2 * LN_STEPS) + (k * LN_STEPS + n[0]))

                        inverse_root(ln_link, ln_rstd[:, k, :], ln_mv[:, k, :, 1], ln_work[:, k, 0, :], ln_work[:, k, 1, :])
                        assert n[0] == LN_STEPS - 1
                        e.tensor_copy(rstd[:, tiles], ln_rstd[:, k, :]).then_inc(S["ln_step"], 1)
                        v.wait_ge(S["split_ready"], r * 2 + (k + 1))
                        for t_ in range(LB):
                            ins = e.tensor_scalar(ln_h[k][:, t_, :], ln_x[k][:, t_, :], ln_mv[:, k, t_, 0:1],
                                                  ln_rstd[:, k, t_:t_ + 1], ALU.subtract, ALU.mult)
                        ins.then_inc(S["h_ready"], 1)
                        v.wait_ge(S["hi_ready"], r * 2 + (k + 1))
                        e.tensor_tensor(ln_h[k], ln_h[k], ln_split[k][:, :, 0:D], ALU.subtract
                                        ).then_inc(S["diff_ready"], 1)

            def positions(d):
                q0 = d * 2 * NB
                k_, v_ = key[:, d, :], key[:, 1 - d, :]
                s0, s1, s2 = scratch
                step(e.tensor_single_scalar(s0, k_, 7, ALU.arith_shift_right))
                e.tensor_copy(bucket, s0)
                e.tensor_scalar(valid, k_, float(SENTINEL), None, ALU.is_lt)
                step(e.tensor_single_scalar(s1, k_, P - 1, ALU.bitwise_and))
                step(e.scalar_tensor_tensor(out=s2, in0=v_, scalar=256.0, in1=s1, op0=ALU.mult, op1=ALU.add))
                step(e.scalar_tensor_tensor(out=payload[:, d, :], in0=s2, scalar=1.0, in1=valid,
                                            op0=ALU.add, op1=ALU.mult))
                if d == 0:
                    e.tensor_single_scalar(s0, payload[:, d, :], 11, ALU.arith_shift_right)
                    step(e.tensor_single_scalar(s1, payload[:, d, :], 2047, ALU.bitwise_and))
                    e.tensor_copy(pay_hi, s0)
                    step(e.tensor_copy(pay_lo, s1))
                step(e.tensor_scalar(position, iota_cols[:], float(P), pad_position[:, 0:1], ALU.mult, ALU.add))

                def onehot(b, k, q, number=iota_bucket):
                    v.wait_ge(S["onehot_used"], q)
                    e.tensor_scalar(onehot_bucket[:, k, :], bucket, number[:, b], None, ALU.is_equal
                                    ).then_inc(S["onehot_ready"], 1)

                with v.Fori(0, NB // 2) as r:
                    for k in range(2):
                        onehot(bass.ds(r * 2 + k, 1), k, r * 2 + (q0 + k + 1), iota_down)
                v.wait_ge(S["onehot_used"], q0 + NB + 2)
                for h in range(2):
                    cols = slice(h * HS, h * HS + HS)
                    step(e.tensor_tensor_scan(prefix[:, cols], ones_wide, banks[h][:, 0:HS],
                                              prefix[:, HS - 1:HS] if h else 0.0, ALU.mult, ALU.add))
                step(e.tensor_scalar(bucket_i[:, 0:1], prefix[:, NS - 1:NS], float(P - 1), None, ALU.add))
                step(e.tensor_single_scalar(bucket_i[:, 1:2], bucket_i[:, 0:1], 7, ALU.arith_shift_right))
                e.tensor_scalar(bucket_slots16[:], bucket_i[:, 1:2], 1.0, None, ALU.max
                                ).then_inc(S["slots16_ready"], 1)
                v.wait_ge(S["slot_prefix_ready"], d + 1)
                step(e.tensor_copy(first_row[0:1, 0:NB], banks[7][0:1, 0:NB]))
                e.tensor_single_scalar(first_batch[0:1, d, 0:NB], first_row[0:1, 0:NB], BATCH.bit_length() - 1,
                                       ALU.arith_shift_right)
                e.tensor_copy(first_slot[:, d:d + 1], banks[6][:, 0:1])
                step(e.tensor_scalar(bucket_slots[:, 0:1], banks[6][:, 0:1], float(P), None, ALU.mult))
                for h in range(2):
                    cols = slice(h * HS, h * HS + HS)
                    step(e.scalar_tensor_tensor(out=s0[:, cols], in0=prefix[:, cols], scalar=bucket_slots[:, 0:1],
                                                in1=banks[h][:, 0:HS], op0=ALU.add, op1=ALU.subtract))
                e.tensor_single_scalar(s1[0:HALF], s0[0:HALF], 6, ALU.arith_shift_right)
                step(e.tensor_single_scalar(s1[HALF:P], s0[HALF:P], RADIX - 1, ALU.bitwise_and))
                e.tensor_copy(base_digits, s1).then_inc(S["base_ready"], 1)
                def merge(k, q, m):
                    v.wait_ge(S["onehot_used"], q)
                    v.sem_inc(S["turn"], 1)
                    for h in range(2):
                        cols = slice(h * HS, h * HS + HS)
                        ins = e.copy_predicated(position[:, cols], onehot_bucket[:, k, cols].bitcast(U16),
                                                banks[2 + 2 * k + h][:, 0:HS])
                    ins.then_inc(S["merged"], 1)
                    v.wait_ge(S["merged"], m)
                q1 = q0 + NB
                with v.Fori(0, NB // 2) as r:
                    for k in range(2):
                        onehot(bass.ds(r * 2 + k, 1), k, r * 2 + (q1 + k + 1))
                        merge(k, r * 2 + (q1 + k + 3), r * 2 + (d * NB + k + 3))
                step(e.tensor_copy(s0, position))
                e.tensor_single_scalar(s1, s0, 7, ALU.arith_shift_right)
                step(e.tensor_single_scalar(s2, s0, P - 1, ALU.bitwise_and))
                if d == 0:
                    e.tensor_copy(slot_of, s1)
                    e.tensor_copy(row_of, s2)
                e.scalar_tensor_tensor(out=list_at[:, d, :], in0=s2, scalar=float(2 * NS), in1=s1,
                                       op0=ALU.mult, op1=ALU.add).then_inc(S["list_at_ready"], 1)
                v.wait_ge(S["list_at_ready"], d + 1)

            positions(0)
            positions(1)
            layer_norm()

            def sort_step(t, k, u):
                v.wait_ge(S["sort_used"], u)
                for half, pay in ((0, pay_hi), (1, pay_lo)):
                    e.tensor_scalar(row_payload[:, k, half * P:half * P + P], iota_cols[:, 0:P],
                                    row_of[:, bass.ds(t, 1)], pay[:, bass.ds(t, 1)],
                                    ALU.is_equal, ALU.mult)
                e.tensor_scalar(slot_onehot[:, k, :], iota_cols[:], slot_of[:, bass.ds(t, 1)], None,
                                ALU.is_equal).then_inc(S["sort_ready"], 1)

            with v.Fori(0, SORTED_TILES // 2) as r:
                for k in range(2):
                    sort_step(r * 2 + k, k, r * 2 + (k + 1))
            v.wait_ge(S["sort_summed"], 1)
            for d in range(2):
                s0, s1, s2 = scratch
                step(e.tensor_scalar(onehot_bucket[0:NB, 0, :], iota_cols[0:NB, :], first_slot[0:NB, d:d + 1], None,
                                     ALU.is_ge))
                v.sem_inc(S["owners_marked"], 1)
                v.wait_ge(S["list_in"], d * 16 + 16)
                listed = raw_list[:, d, :]
                if d == 0:
                    for h in range(2):
                        cols = slice(h * HS, h * HS + HS)
                        step(e.tensor_tensor(s0[:, cols], sort_lo[h][:, 0:HS], listed[:, cols], ALU.add))
                        step(e.scalar_tensor_tensor(out=s1[:, cols], in0=sort_hi[h][:, 0:HS], scalar=2048.0,
                                                    in1=s0[:, cols], op0=ALU.mult, op1=ALU.add))
                    listed = s1
                step(e.tensor_single_scalar(s2, listed, 255, ALU.bitwise_and))
                v.wait_ge(S["owners_summed"], d + 1)
                for h in range(2):
                    cols = slice(h * HS, h * HS + HS)
                    step(e.scalar_tensor_tensor(out=receiver[d][:, cols], in0=banks[4 + h][:, 0:HS],
                                                scalar=float(KEY), in1=s2[:, cols], op0=ALU.mult, op1=ALU.add))
                e.tensor_single_scalar(gather_row[d][:, :], listed, 8, ALU.arith_shift_right
                                       ).then_inc(S["decoded"], 1)
                v.wait_ge(S["decoded"], d + 1)

            def bucket_mean(d, j, dest):
                lo = v.value_load(first_batch[0:1, d, bass.ds(j, 1)], min_val=0, max_val=BATCHES - 1)
                hi = v.value_load(first_batch[0:1, d, bass.ds(j + 1, 1)], min_val=0, max_val=BATCHES - 1)
                e.tensor_scalar(node_key[:], iota_cols[:, 0:P], bucket_key[:, bass.ds(j, 1)], None, ALU.add
                                ).then_inc(S["key_ready"], 1)
                v.wait_ge(S["key_ready"], j + (d * NB + 1))
                v.sem_inc(S["turn"], 1)

                def visit(b):
                    at_ = b + j
                    v.wait_ge(S["node_onehot_used"], at_ + (d * VISITS + 1))
                    v.sem_inc(S["turn"], 1)
                    e.tensor_tensor(
                        onehot_node[:, bass.ds((at_ + d * VISITS) % OH, 1), :, :].rearrange("p a s m -> p (a s) m"),
                        receiver[d][:, bass.ds(b * BATCH, BATCH)].rearrange("p (s o) -> p s o", o=1
                                                                            ).to_broadcast([P, BATCH, P]),
                        node_key[:].rearrange("p (o m) -> p o m", o=1).to_broadcast([P, BATCH, P]),
                        ALU.is_equal).then_inc(S["node_onehot_ready"], 1)

                with v.Fori(lo, hi) as b:
                    visit(b)
                visit(hi)
                v.wait_ge(S["bucket_done"], j + (d * NB + 1))
                e.tensor_scalar(has_edge[:, d, bass.ds(j, 1)], counts[:, 0:1], 1.0, None, ALU.min)
                e.tensor_scalar(inv_count[:, 0:1], counts[:, 0:1], 1.0, None, ALU.max
                                ).then_inc(S["inv_step"], 1)
                v.wait_ge(S["inv_step"], j * 2 + (d * 2 * NB + 1))
                e.reciprocal(inv_count[:, 1:2], inv_count[:, 0:1]).then_inc(S["inv_ready"], 1)
                v.wait_ge(S["inv_ready"], j + (d * NB + 1))
                e.tensor_scalar(inv_count[:, 2:3], inv_count[:, 1:2], 1.0 / LO_SCALE, None, ALU.mult
                                ).then_inc(S["inv_step"], 1)
                v.wait_ge(S["inv_step"], j * 2 + (d * 2 * NB + 2))
                v.wait_ge(S["hi_mean_ready"], j + (d * NB + 1))
                e.scalar_tensor_tensor(out=dest, in0=sums[:, D:2 * D], scalar=inv_count[:, 2:3],
                                       in1=hi_mean[:], op0=ALU.mult, op1=ALU.add).then_inc(S["evac_done"], 1)

            with v.Fori(0, NB // 2) as r:
                for k in range(2):
                    v.wait_ge(S["mean_a_free"], r * 2 + (k + 1))
                    v.sem_inc(S["turn"], 1)
                    bucket_mean(0, r * 2 + k, mean_a_t[:, k, :])
                    v.wait_ge(S["evac_done"], r * 2 + (k + 2))
                    v.sem_inc(S["turn"], 1)
            v.wait_ge(S["high_ready"], 6)
            for hi_, lo_, raw in zip((gate_hi, bias_hi, r_hi, *e_hi), (gate_lo[:], bias_lo[:], r_lo, *e_lo),
                                     (w_gate[:], gate_bias[:], r_w1, *e_w)):
                e.tensor_tensor(lo_, raw, hi_.bitcast(F32), ALU.subtract).then_inc(S["low_ready"], 1)

            v.sem_inc(S["x_used"], CREDIT)
            v.sem_inc(S["combined"], 1)
            v.wait_ge(S["small_in"], 6 * 16)
            n = {"gate_step": 0, "ffn_step": 0}

            def link(ins, name, base):
                n[name] += 1
                ins.then_inc(S[name], 1)
                v.wait_ge(S[name], base + n[name])

            def tile_begins(r, o):
                jj, j, j1 = o % 2, r * 2 + o, r * 2 + (o + 1)
                v.wait_ge(x_landed[jj], r * 32 + (o // 2 * 32 + 32))
                e.tensor_scalar(h_t, x_t[:, jj, :], moments[:, bass.ds(j, 1), 0], rstd[:, bass.ds(j, 1)],
                                ALU.subtract, ALU.mult).then_inc(S["h_tile_ready"], 1)
                v.wait_ge(S["h_tile_ready"], j1)
                e.tensor_tensor(xh_t, x_t[:, jj, :], h_t, ALU.add).then_inc(S["x_used"], 1)
                v.wait_ge(S["tile_a_hi"], j1)
                e.tensor_tensor(tile_lo[:, 0:4, :], four(turned), tile_hi[:, 0:4, :].bitcast(F32), ALU.subtract
                                ).then_inc(S["tile_a_ready"], 1)
                bucket_mean(1, j, mean_b[:])
                e.tensor_copy(flags[:, 0:2], has_edge[:, :, bass.ds(j, 1)].rearrange("p a b -> p (a b)")
                              ).then_inc(S["flags_ready"], 1)

            def tile_b(r, o):
                n["gate_step"] = 0
                v.wait_ge(S["tile_b_turned"], r * 2 + (o + 1))
                turned_b = two(turned[:, 0:D])
                link(e.tensor_copy(tile_hi[:, 4:6, :], turned_b), "gate_step", r * (2 * GATE_STEPS) + o * GATE_STEPS)
                e.tensor_tensor(tile_lo[:, 4:6, :], turned_b, tile_hi[:, 4:6, :].bitcast(F32), ALU.subtract)
                e.tensor_copy(flags_T, turned[0:4, D:D + P]).then_inc(S["tile_b_ready"], 1)

            def new_rows(r, o):
                jj, j1 = o % 2, r * 2 + (o + 1)
                base = r * (2 * GATE_STEPS) + o * GATE_STEPS

                def next_(ins):
                    link(ins, "gate_step", base)

                v.wait_ge(S["n_summed"], j1)
                v.wait_ge(S["rz_ready"], j1)
                next_(e.scalar_tensor_tensor(out=gate_tmp, in0=gates[:, 0:D], scalar=1.0,
                                             in1=n_bank[:, D:2 * D], op0=ALU.add, op1=ALU.mult))
                e.scalar_tensor_tensor(out=gate_tmp, in0=gate_tmp, scalar=0.5, in1=n_bank[:, 0:D],
                                       op0=ALU.mult, op1=ALU.add).then_inc(S["pre_new_ready"], 1)
                v.wait_ge(S["new_ready"], j1)
                next_(e.tensor_tensor(new_t, new_t, h_t, ALU.subtract))
                next_(e.scalar_tensor_tensor(out=new_t, in0=gates[:, D:2 * D], scalar=1.0, in1=new_t,
                                             op0=ALU.add, op1=ALU.mult))
                next_(e.scalar_tensor_tensor(out=x1[:, jj, :], in0=new_t, scalar=0.5, in1=xh_t,
                                             op0=ALU.mult, op1=ALU.add))
                next_(e.bn_stats(ln_s[:, 0:6], x1[:, jj, :]))
                v.sem_inc(S["turn"], 1)
                next_(e.bn_aggr(ln_s[:, 6:8], ln_s[:, 0:6]))
                inverse_root(next_, ln_s[:, 9:10], ln_s[:, 7:8], ln_s[:, 10:11], ln_s[:, 11:12])
                assert n["gate_step"] == GATE_STEPS
                e.tensor_scalar(xn[:, jj, :], x1[:, jj, :], ln_s[:, 6:7], ln_s[:, 9:10], ALU.subtract, ALU.mult
                                ).then_inc(S["xn_ready"], 1)

            def turn_xn(r, o):
                jj = o % 2
                v.wait_ge(S["xn_hi_ready"], r * 2 + (o // 2 * 2 + 2))
                e.tensor_tensor(xn_lo[:, :, jj * P:jj * P + P], two(turned[:, jj * 2 * P:jj * 2 * P + 2 * P]),
                                xn_hi[:, :, jj * P:jj * P + P].bitcast(F32), ALU.subtract
                                ).then_inc(S["xn_T_ready"], 1)

            def low(q, x_, hi_ready, whole, high, low_part, ready):
                v.wait_ge(hi_ready, q * NE + (x_ + 2))
                e.tensor_tensor(low_part[:, x_ % 2, :, :], whole[:, x_ % 2, :, :],
                                high[:, x_ % 2, :, :].bitcast(F32), ALU.subtract).then_inc(ready, 1)

            def low1(q, x_):
                low(q, x_, S["h1_hi_ready"], h1, h1_hi, h1_lo, S["h1_ready"])

            def low2(q, x_):
                low(q, x_, S["h2_hi_ready"], h2, h2_hi, h2_lo, S["h2_ready"])

            def route(q):
                n["ffn_step"] = 0

                def next_(ins):
                    link(ins, "ffn_step", q * FFN_STEPS)

                low1(q, 0)
                v.wait_ge(S["logits_summed"], q + 1)
                next_(e.tensor_tensor(logits[:], two(route_bank[:, 2 * P:2 * P + 2 * NE]), r_b2[:], ALU.add))
                next_(e.tensor_reduce(rt[:, 0:2], logits[:], AX_X, ALU.max))
                next_(e.tensor_scalar(rt[:, 2:4], rt[:, 0:2], -1.0, None, ALU.mult))
                v.sem_inc(S["shifted_ready"], 2)
                v.wait_ge(S["exp_ready"], q * 2 + 2)
                next_(e.reciprocal(rt[:, 6:8], rt[:, 4:6]))
                for tt in range(2):
                    next_(e.tensor_scalar(prob[:, tt, 0:NE], prob[:, tt, 0:NE], rt[:, 6 + tt:7 + tt], None,
                                          ALU.mult))
                for tt in range(2):
                    v.sem_inc(S["turn"], 1)
                    next_(e.max(top[:, tt, :], prob[:, tt, :]))
                    v.sem_inc(S["turn"], 1)
                    next_(e.max_index(top_at[:, tt, :], top[:, tt, :], prob[:, tt, :]))
                e.tensor_tensor(rt[:, 8:10], top[:, :, 1], top[:, :, 0], ALU.subtract
                                ).then_inc(S["prob_gap_ready"], 1)
                next_(e.tensor_copy(two(rt[:, 16:20]), top_at[:, :, 0:2]))
                v.wait_ge(S["gap_exp_ready"], q + 1)
                next_(e.tensor_scalar(rt[:, 12:14], rt[:, 10:12], 1.0, None, ALU.add))
                next_(e.reciprocal(rt[:, 20:22], rt[:, 12:14]))
                next_(e.tensor_tensor(rt[:, 22:24], rt[:, 10:12], rt[:, 20:22], ALU.mult))
                for tt in range(2):
                    e.tensor_scalar(coef[:, tt, :], iota_bucket[:, 0:NE], rt[:, 16 + 2 * tt:17 + 2 * tt],
                                    rt[:, 20 + tt:21 + tt], ALU.is_equal, ALU.mult)
                    next_(e.tensor_scalar(coef2[:, tt, :], iota_bucket[:, 0:NE], rt[:, 17 + 2 * tt:18 + 2 * tt],
                                          rt[:, 22 + tt:23 + tt], ALU.is_equal, ALU.mult))
                next_(e.tensor_tensor(coef[:], coef[:], coef2[:], ALU.add))
                v.sem_inc(S["coef_ready"], 1)

            def start_sum(q):
                low1(q, 1)
                v.wait_ge(S["coef_turned"], q + 1)
                e.tensor_copy(coef_T, two(route_bank[0:NE, 0:2 * P])).then_inc(S["coef_T_ready"], 1)
                low2(q, 0)
                v.wait_ge(S["acc_free"], q + 1)
                v.sem_inc(S["turn"], 1)
                v.wait_ge(S["b3_summed"], q + 1)
                for tt in range(2):
                    link(e.tensor_tensor(acc[:, tt, :], route_bank[:, tt * D:tt * D + D], x1[:, tt, :], ALU.add),
                         "ffn_step", q * FFN_STEPS)
                assert n["ffn_step"] == FFN_STEPS
                v.sem_inc(S["acc_started"], 1)

            def combine(q, x_):
                v.wait_ge(S["l3_summed"], q * NE + (x_ + 1 + CREDIT))
                for tt in range(2):
                    ins = e.scalar_tensor_tensor(out=acc[:, tt, :], in0=l3_bank[:, tt * D:tt * D + D],
                                                 scalar=coef[:, tt, x_:x_ + 1], in1=acc[:, tt, :],
                                                 op0=ALU.mult, op1=ALU.add)
                ins.then_inc(S["combined"], 1)
                v.wait_ge(S["combined"], q * NE + (x_ + 2))

            def experts(q, x_):
                if x_ < NE:
                    low1(q, x_)
                if x_ - 1 < NE:
                    low2(q, x_ - 1)
                combine(q, x_ - 2)

            for o in range(2):
                tile_begins(0, o)
                tile_b(0, o)
                new_rows(0, o)
            for o in range(2):
                turn_xn(0, o)
            with v.Fori(0, NB // 2 - 1) as q:
                tile_begins(q, 2)
                route(q)
                tile_b(q, 2)
                start_sum(q)
                new_rows(q, 2)
                experts(q, 2)
                tile_begins(q, 3)
                experts(q, 3)
                tile_b(q, 3)
                experts(q, 4)
                new_rows(q, 3)
                for x_ in (5, 6, 7):
                    experts(q, x_)
                v.sem_inc(S["acc_done"], 1)
                for o in (2, 3):
                    turn_xn(q, o)
            last = NB // 2 - 1
            route(last)
            start_sum(last)
            for x_ in range(2, NE + 2):
                experts(last, x_)
            v.sem_inc(S["acc_done"], 1)

        @block.tensor
        def _(pe):
            t = nc.tensor
            pe.sem_inc(S["onehot_used"], 2)
            pe.sem_inc(S["sort_used"], 2)
            pe.sem_inc(S["slot_done"], RING)
            pe.sem_inc(S["node_onehot_used"], OH)
            pe.sem_inc(S["evac_done"], 1)
            pe.sem_inc(S["l2_summed"], CREDIT)
            pe.sem_inc(S["l3_summed"], CREDIT)
            pe.wait_ge(S["fold_in"], 11 * 16)
            for a_ in range(2):
                for c in range(2):
                    m = 2 * a_ + c
                    for bank, lo_, hi_ in ((banks[2 * m], 0, 2 * D), (banks[2 * m + 1], 2 * D, G3)):
                        for k in range(2):
                            ins = t.matmul(bank[:, 0:hi_ - lo_], w_conv[:, 2 * a_ + k, c * P:c * P + P],
                                           w_ih_raw[:, 2 * a_ + k, lo_:hi_], start=(k == 0), stop=(k == 1))
            ins.then_inc(S["fold_summed"], 1)
            pe.wait_ge(S["fold_done"], 1)
            bc = b_conv[:].rearrange("p (a c m) -> p a c m", a=2, c=2)
            for bank, lo_, hi_ in ((banks[0], 0, 2 * D), (banks[1], 2 * D, G3)):
                for n_ in range(4):
                    ins = t.matmul(bank[0:2, 0:hi_ - lo_], bc[:, n_ // 2, n_ % 2, :], w_ih_raw[:, n_, lo_:hi_],
                                   start=(n_ == 0), stop=(n_ == 3))
            ins.then_inc(S["fold_summed"], 1)
            pe.wait_ge(S["fold_done"], 2)
            pe.wait_ge(S["consts"], N_CONSTS)
            for d in range(2):
                q0 = d * 2 * NB
                for h in range(2):
                    t.matmul(banks[h][:, 0:HS], zeros16[:, 0:P], zeros16[:, 0:HS], start=True, stop=False,
                             skip_group_check=True)
                with pe.Fori(0, NB // 2) as r:
                    for k in range(2):
                        b = r * 2 + k
                        pe.wait_ge(S["onehot_ready"], r * 2 + (q0 + k + 1))
                        for h in range(2):
                            ins = t.matmul(banks[h][:, 0:HS], pick_row[:, bass.ds(b + (P - NB), P)],
                                           onehot_bucket[:, k, h * HS:h * HS + HS], start=False, stop=False,
                                           skip_group_check=True)
                        ins.then_inc(S["onehot_used"], 1)
                pe.wait_ge(S["slots16_ready"], d + 1)
                t.matmul(banks[6][:, 0:1], lower_bucket, bucket_slots16[:], start=True, stop=True)
                t.matmul(banks[7][0:1, 0:NB], bucket_slots16[:], lower_bucket[:, 0:NB], start=True, stop=True
                         ).then_inc(S["slot_prefix_ready"], 1)
                pe.wait_ge(S["base_ready"], d + 1)
                with pe.Fori(0, NB // 2) as r:
                    for k in range(2):
                        b = r * 2 + k
                        pe.wait_ge(S["merged"], r * 2 + (d * NB + k + 1))
                        pe.wait_ge(S["onehot_ready"], r * 2 + (q0 + NB + k + 1))
                        for h in range(2):
                            o = banks[2 + 2 * k + h][:, 0:HS]
                            cols = slice(h * HS, h * HS + HS)
                            t.matmul(o, lower, onehot_bucket[:, k, cols], start=True, stop=False)
                            ins = t.matmul(o, spread_row[:, bass.ds(b, 1), :].rearrange("p a m -> p (a m)"),
                                           base_digits[:, cols], start=False, stop=True)
                        ins.then_inc(S["onehot_used"], 1)

            def sort_products(k):
                for bank, half in ((sort_hi, 0), (sort_lo, 1)):
                    for h in range(2):
                        ins = t.matmul(bank[h][:, 0:HS], row_payload[:, k, half * P:half * P + P],
                                       slot_onehot[:, k, h * HS:h * HS + HS], start=False, stop=False,
                                       skip_group_check=True)
                return ins

            def clear_sort():
                for bank in (*sort_hi, *sort_lo):
                    t.matmul(bank[:, 0:HS], zeros16[:, 0:P], zeros16[:, 0:HS], start=True, stop=False,
                             skip_group_check=True)

            pe.wait_ge(S["merged"], 2 * NB + 2)
            clear_sort()
            with pe.Fori(0, SORTED_TILES // 2) as r:
                for k in range(2):
                    pe.wait_ge(S["sort_ready"], r * 2 + (k + 1))
                    sort_products(k).then_inc(S["sort_used"], 1)
            pe.wait_ge(S["sort_used"], SORTED_TILES + 2)
            pe.sem_inc(S["sort_summed"], 1)
            for d in range(2):
                pe.wait_ge(S["owners_marked"], d + 1)
                for h in range(2):
                    ins = t.matmul(banks[4 + h][:, 0:HS], ones16[:], onehot_bucket[0:NB, 0, h * HS:h * HS + HS],
                                   start=True, stop=True)
                ins.then_inc(S["owners_summed"], 1)
            pe.wait_ge(S["decoded"], 2)

            def bucket_sum(d, j):
                lo = pe.value_load(first_batch[0:1, d, bass.ds(j, 1)], min_val=0, max_val=BATCHES - 1)
                hi = pe.value_load(first_batch[0:1, d, bass.ds(j + 1, 1)], min_val=0, max_val=BATCHES - 1)
                pe.wait_ge(S["evac_done"], j + (d * NB + 1))
                t.matmul(sums[:, :], zeros16[:, 0:P], zeros16[:], start=True, stop=False,
                         skip_group_check=True)
                t.matmul(counts[:, 0:1], zeros16[:, 0:P], ones_col[:], start=True, stop=False,
                         skip_group_check=True)

                def visit(b, frees):
                    at_ = b + j
                    pe.wait_ge(S["node_onehot_ready"], at_ + (d * VISITS + 1))
                    pe.wait_ge(S["rows_landed"], b + (d * BATCHES + 1))
                    pe.sem_inc(S["turn"], 1)
                    buf, part = (at_ + d * VISITS) % OH, b % RINGS
                    batches = ring[:].rearrange("p (r s) m -> p r (s m)", r=RINGS)
                    hots = onehot_node[:].rearrange("p r s m -> p r (s m)")
                    for q in range(BATCH):
                        oh = hots[:, bass.ds(buf, 1), q * P:q * P + P].rearrange("p a m -> p (a m)")
                        rows = batches[:, bass.ds(part, 1), q * 2 * D:(q + 1) * 2 * D].rearrange("p a m -> p (a m)")
                        summed = t.matmul(sums[:, :], oh, rows, start=False, stop=False, skip_group_check=True)
                        ins = t.matmul(counts[:, 0:1], oh, ones_col[:], start=False, stop=False,
                                       skip_group_check=True)
                        if q == BATCH - 1 and frees:
                            summed.then_inc(S["slot_done"], BATCH)
                    ins.then_inc(S["node_onehot_used"], 1)

                with pe.Fori(lo, hi) as b:
                    visit(b, True)
                visit(hi, False)
                t.matmul(counts[:, 0:1], zeros16[:, 0:P], ones_col[:], start=False, stop=True,
                         skip_group_check=True).then_inc(S["bucket_done"], 1)

            with pe.Fori(0, NB) as j:
                bucket_sum(0, j)
            pe.wait_ge(S["bucket_done"], NB)
            pe.sem_inc(S["slot_done"], BATCH)
            pe.wait_ge(S["small_in"], 6 * 16)
            pe.wait_ge(S["experts_in"], 5 * 16)

            pe.wait_ge(S["low_ready"], 6)

            def product(o, left, right, first, last):
                (a_hi, a_lo), (b_hi, b_lo) = left, right
                t.matmul(o, a_hi, b_hi, start=first, stop=False, skip_group_check=True)
                t.matmul(o, a_hi, b_lo, start=False, stop=False, skip_group_check=True)
                return t.matmul(o, a_lo, b_hi, start=False, stop=last, skip_group_check=True)

            def tile_begins(r, o):
                jj = o % 2
                pe.wait_ge(S["h_tile_ready"], r * 2 + (o + 1))
                for c in range(2):
                    t.transpose(turned[:, c * P:c * P + P], mean_a_t[:, jj, c * P:c * P + P], ident[:])
                for c in range(2):
                    ins = t.transpose(turned[:, (2 + c) * P:(3 + c) * P], h_t[:, c * P:c * P + P], ident[:])
                ins.then_inc(S["tile_a_turned"], 1)
                bucket_sum(1, r * 2 + o)

            def turn_b(r, o):
                pe.wait_ge(S["tile_a_ready"], r * 2 + (o + 1))
                pe.wait_ge(S["evac_done"], r * 2 + (NB + 2 + o))
                for c in range(2):
                    t.transpose(turned[:, c * P:c * P + P], mean_b[:, c * P:c * P + P], ident[:])
                pe.wait_ge(S["flags_ready"], r * 2 + (o + 1))
                t.transpose(turned[0:4, D:D + P], flags[:], ident[:]).then_inc(S["tile_b_turned"], 1)

            def gate_products(r, o):
                order = ((0, 0), (1, 1), (2, 4), (3, 5), (4, 2), (5, 3))
                for n_, (src_, wt) in enumerate(order):
                    if n_ == 4:
                        pe.wait_ge(S["tile_b_ready"], r * 2 + (o + 1))
                    product(rz_bank[:], (tile_hi[:, src_, :], tile_lo[:, src_, :]),
                            (gate_hi[:, wt, 0:2 * D], gate_lo[:, wt, 0:2 * D]), n_ == 0, False)
                t.matmul(rz_bank[:], flags_T, bias_hi[:, 0:2 * D], start=False, stop=False, skip_group_check=True)
                t.matmul(rz_bank[:], flags_T, bias_lo[:, 0:2 * D], start=False, stop=True, skip_group_check=True
                         ).then_inc(S["rz_summed"], 1)
                for n_, (src_, wt) in enumerate(order):
                    part = slice(D, 2 * D) if wt >= 4 else slice(0, D)
                    product(n_bank[:, part], (tile_hi[:, src_, :], tile_lo[:, src_, :]),
                            (gate_hi[:, wt, 2 * D:G3], gate_lo[:, wt, 2 * D:G3]), n_ == 0, False)
                t.matmul(n_bank[:], flags_T, bias_hi[:, 2 * D:G3 + D], start=False, stop=False,
                         skip_group_check=True)
                t.matmul(n_bank[:], flags_T, bias_lo[:, 2 * D:G3 + D], start=False, stop=True,
                         skip_group_check=True).then_inc(S["n_summed"], 1)

            def turn_xn(r, o):
                jj = o % 2
                pe.wait_ge(S["xn_ready"], r * 2 + (o + 1))
                for c in range(2):
                    ins = t.transpose(turned[:, (2 * jj + c) * P:(2 * jj + c + 1) * P], xn[:, jj, c * P:c * P + P],
                                      ident[:])
                return ins

            def turn_pair(r, o):
                turn_xn(r, o)
                turn_xn(r, o + 1).then_inc(S["xn_turned"], 2)

            def route(q):
                pe.wait_ge(S["xn_T_ready"], q * 2 + 2)
                for k in range(2):
                    ins = product(route_bank[:, 0:2 * P], (r_hi[:, k, :], r_lo[:, k, :]),
                                  (xn_hi[:, k, :], xn_lo[:, k, :]), k == 0, k == 1)
                ins.then_inc(S["router_summed"], 1)

            def score(q):
                pe.wait_ge(S["router_ready"], q + 1)
                for tt in range(2):
                    ins = t.matmul(route_bank[:, 2 * P + tt * NE:2 * P + tt * NE + NE],
                                   router_h[:, tt * P:tt * P + P], r_w2[:], start=True, stop=True)
                ins.then_inc(S["logits_summed"], 1)

            def last_biases(q):
                pe.wait_ge(S["coef_ready"], q + 1)
                for tt in range(2):
                    ins = t.transpose(route_bank[0:NE, tt * P:tt * P + P], coef[:, tt, :], ident[:])
                ins.then_inc(S["coef_turned"], 1)
                layer2(q, 0)
                pe.wait_ge(S["coef_T_ready"], q + 1)
                for tt in range(2):
                    ins = t.matmul(route_bank[:, tt * D:tt * D + D], coef_T[:, tt, :], e_b3[:], start=True, stop=True)
                ins.then_inc(S["b3_summed"], 1)

            def layer1(q, x_):
                pe.wait_ge(S["h1_hi_ready"], q * NE + (x_ + 1))
                for m in range(2):
                    cols = slice(m * P, m * P + P)
                    for k in range(2):
                        ins = product(l1_bank[:, m * 2 * P:(m + 1) * 2 * P],
                                      (e_hi[0][:, 2 * x_ + k, cols], e_lo[0][:, 2 * x_ + k, cols]),
                                      (xn_hi[:, k, :], xn_lo[:, k, :]), k == 0, k == 1)
                ins.then_inc(S["l1_summed"], 1)

            def layer2(q, x_):
                pe.wait_ge(S["h2_hi_ready"], q * NE + (x_ + 1))
                pe.wait_ge(S["h1_ready"], q * NE + (x_ + 1))
                for m in range(2):
                    cols = slice(m * P, m * P + P)
                    for k in range(2):
                        ins = product(l2_bank[:, m * 2 * P:(m + 1) * 2 * P],
                                      (e_hi[1][:, 2 * x_ + k, cols], e_lo[1][:, 2 * x_ + k, cols]),
                                      (h1_hi[:, x_ % 2, k, :], h1_lo[:, x_ % 2, k, :]), k == 0, k == 1)
                ins.then_inc(S["l2_summed"], 1)

            def layer3(q, x_):
                pe.wait_ge(S["combined"], q * NE + (x_ + 1))
                pe.wait_ge(S["h2_ready"], q * NE + (x_ + 1))
                for tt in range(2):
                    cols = slice(tt * P, tt * P + P)
                    for k in range(2):
                        ins = product(l3_bank[:, tt * D:tt * D + D],
                                      (h2_hi[:, x_ % 2, k, cols], h2_lo[:, x_ % 2, k, cols]),
                                      (e_hi[2][:, 2 * x_ + k, :], e_lo[2][:, 2 * x_ + k, :]), k == 0, k == 1)
                ins.then_inc(S["l3_summed"], 1)

            def experts(q, x_):
                if x_ < NE:
                    layer1(q, x_)
                if x_ - 1 < NE:
                    layer2(q, x_ - 1)
                layer3(q, x_ - 2)

            for o in range(2):
                tile_begins(0, o)
                turn_b(0, o)
                gate_products(0, o)
            turn_pair(0, 0)
            with pe.Fori(0, NB // 2 - 1) as q:
                pe.wait_ge(S["xn_T_ready"], q * 2 + 2)
                tile_begins(q, 2)
                route(q)
                layer1(q, 0)
                turn_b(q, 2)
                score(q)
                layer1(q, 1)
                last_biases(q)
                pe.wait_ge(S["acc_started"], q + 1)
                gate_products(q, 2)
                experts(q, 2)
                tile_begins(q, 3)
                experts(q, 3)
                turn_b(q, 3)
                experts(q, 4)
                gate_products(q, 3)
                for x_ in (5, 6, 7):
                    experts(q, x_)
                turn_pair(q, 2)
            last = NB // 2 - 1
            route(last)
            layer1(last, 0)
            score(last)
            layer1(last, 1)
            last_biases(last)
            for x_ in range(2, NE + 2):
                experts(last, x_)


def kernel(**inputs):
    import numpy as _np
    import concourse.bacc as _bacc
    from concourse.bass_utils import run_bass_kernel_spmd as _run

    nc = _bacc.Bacc("TRN2", target_bir_lowering=False, num_devices=1)
    x = _np.asarray(inputs["x"])
    xp = _np.zeros((NP + 2 * P, D), x.dtype)
    xp[:NODES] = x
    edges = _np.full((2, NS * P), SENTINEL, _np.int32)
    edges[0, :EDGES] = inputs["dst"]
    edges[1, :EDGES] = inputs["src"]
    edges = _np.ascontiguousarray(edges.reshape(2, NS, P).transpose(2, 0, 1))
    g = {n.split("_", 1)[1]: _np.asarray(a) for n, a in inputs.items() if n.startswith("L0_")}
    arrays = {
        "in_x": xp, "in_edges": edges,
        "in_w_ih_T": g["gnn_W_ih"].T, "in_w_hh_T": g["gnn_W_hh"].T, "in_w_in": g["gnn_W_in"],
        "in_w_out": g["gnn_W_out"], "in_b_in": g["gnn_b_in"][:, None], "in_b_out": g["gnn_b_out"][:, None],
        "in_b_ih": g["gnn_b_ih"][None], "in_b_hh": g["gnn_b_hh"][None],
        "in_r_w1": g["ffn_router_w1"], "in_r_b1": g["ffn_router_b1"][:, None],
        "in_r_w2": g["ffn_router_w2"], "in_r_b2": g["ffn_router_b2"][None],
        "in_e_w1": g["ffn_expert_w1"], "in_e_w2": g["ffn_expert_w2"], "in_e_w3": g["ffn_expert_w3"],
        "in_e_b1": g["ffn_expert_b1"].reshape(NE, 2, P).transpose(2, 0, 1),
        "in_e_b2": g["ffn_expert_b2"].reshape(NE, 2, P).transpose(2, 0, 1), "in_e_b3": g["ffn_expert_b3"],
    }
    arrays = {n: _np.ascontiguousarray(a) for n, a in arrays.items()}
    aps = {n: nc.dram_tensor(n, a.shape, mybir.dt.from_np(a.dtype), kind="ExternalInput").ap()
           for n, a in arrays.items()}
    out = nc.dram_tensor("out_0", (NP, D), F32, kind="ExternalOutput").ap()
    table = nc.dram_tensor("split_rows", (NP, 2 * D), F16, kind="Internal").ap()
    lists = [nc.dram_tensor(f"list_{d}", (LIST, 1), I32, kind="Internal").ap() for d in range(2)]
    means = nc.dram_tensor("in_edge_means", (NP + 2 * P, D), F32, kind="Internal").ap()
    gnn_moe_program(nc, aps["in_x"], aps["in_edges"], {n[3:]: ap for n, ap in aps.items()}, out, table, lists, means)
    r = _run(nc, [arrays], core_ids=[0])
    return r.results[0]["out_0"][:NODES]
```

```python
from contextlib import ExitStack

import concourse.bass as bass
from concourse import mybir

F32 = mybir.dt.float32
F32R = mybir.dt.float32r
F16 = mybir.dt.float16
I32 = mybir.dt.int32
U16 = mybir.dt.uint16
U32 = mybir.dt.uint32
ALU = mybir.AluOpType
ACT = mybir.ActivationFunctionType
AX_X = mybir.AxisListType.X

P = 128
NODES = 6250
EDGES = 100000
D = 256
NB = 50
NP = NB * P
NS = 832
HS = NS // 2
HALF = 64
RADIX = 64
LO_SCALE = 2048.0
BATCH = 4
RINGS = 4
RING = BATCH * RINGS
OH = 4
BATCHES = NS // BATCH
VISITS = BATCHES - 1 + NB
KEY = 256
SCATTER = 32
SORTED_TILES = 704
LIST = 2 * NS * P
SENTINEL = 8191
EPS = 1e-5
ROOT_SEED = 0x5F3759DF
ROOT_STEPS = 3
LB = 5
GATE_STEPS = 8 + 3 + 3 * ROOT_STEPS
FFN_STEPS = 19
LN_STEPS = 2 + 3 + 3 * ROOT_STEPS + 1
NE = 6
G3 = 3 * D
FIRST_PAIRS = 3
CREDIT = 2
assert EDGES // P + NB + 1 <= NS and NS % BATCH == 0


def gnn_moe_program(nc, x, edges, w, out, table, lists, means):
    ctx = ExitStack()
    with ctx:
        def sb(name, shape, dt):
            return ctx.enter_context(nc.sbuf_tensor(name, shape, dt))

        def sem(name):
            return ctx.enter_context(nc.semaphore(name))

        banks = [ctx.enter_context(nc.psum_tensor(f"bank{i}", [P, 512], F32)) for i in range(8)]

        iota_cols = sb("iota_cols", [P, NS], F16)
        pad_position = sb("pad_position", [P, 1], F32)
        iota_bucket = sb("iota_bucket", [P, NB], F32)
        iota_down = sb("iota_down", [P, NB], F32)
        ones_col = sb("ones_col", [P, 1], F16)
        zeros16 = sb("zeros16", [P, 512], F16)
        ident = sb("ident", [P, P], F32)

        REGION = 38272
        region_at = -(-nc.sbuf_base // 32) * 32
        sb("region", [P, REGION], F32)
        at = {"sort": 0, "dense": 0}

        def carve(user, shape, dt=F32, twin=False):
            words = 1
            for n in shape:
                words *= n
            words = words // 2 if dt == F16 else words
            words = -(-words // 8) * 8
            offset = region_at + 4 * at[user]
            at[user] += words
            assert at[user] <= REGION, (user, at[user])
            views = [nc.alloc_sbuf_tensor_at(f"{user}_{at[user]}{mark}", [P, *shape], dt_, offset=offset)[:]
                     for mark, dt_ in (("", dt), ("_low", F32R))[0:2 if twin else 1]]
            return views if twin else views[0]

        def twin_sb(name, shape):
            offset = -(-nc.sbuf_base // 32) * 32
            whole = sb(name, shape, F32)
            return whole, nc.alloc_sbuf_tensor_at(name + "_low", shape, F32R, offset=offset)

        ones_wide = carve("sort", [HS])
        lower = carve("sort", [P], F16)
        pick_row = carve("sort", [256], F16)
        lower_bucket = carve("sort", [P], F16)
        spread_row = carve("sort", [NB, P], F16)
        key = carve("sort", [2, NS], I32)
        scratch = [carve("sort", [NS], I32) for i in range(3)]
        valid = carve("sort", [NS], F32)
        bucket = carve("sort", [NS], F16)
        prefix = carve("sort", [NS], F32)
        base_digits = carve("sort", [NS], F16)
        bucket_slots = sb("bucket_slots", [P, 4], F32)
        bucket_slots16 = sb("bucket_slots16", [P, 1], F16)
        bucket_i = sb("bucket_i", [P, 2], I32)
        onehot_bucket = carve("sort", [2, NS], F16)
        position = carve("sort", [NS], F32)
        slot_of = carve("sort", [NS])
        row_of = carve("sort", [NS])
        pay_hi = carve("sort", [NS])
        pay_lo = carve("sort", [NS])
        list_at = carve("sort", [2, NS], I32)
        payload = carve("sort", [2, NS], I32)
        raw_list = list_at
        at_stage = carve("sort", [2, SCATTER], I32)
        payload_stage = carve("sort", [2, SCATTER], I32)
        first_slot = sb("first_slot", [P, 2], F32)
        first_batch = sb("first_batch", [1, 2, 64], I32)
        first_row = sb("first_row", [1, 64], I32)
        ones16 = sb("ones16", [NB, P], F16)
        bucket_key = sb("bucket_key", [P, NB], F32)
        node_key = sb("node_key", [P, P], F32)
        row_payload = carve("sort", [2, 2 * P], F16)
        gather_row_0 = carve("sort", [NS], I32)
        receiver_0 = carve("sort", [NS])
        at["norm"] = at["sort"]
        ln_x = [carve("norm", [LB, D]) for _ in range(2)]
        ln_h = [carve("norm", [LB, D]) for _ in range(2)]
        ln_split = [carve("norm", [LB, 2 * D], F16) for _ in range(2)]
        ln_stats = carve("norm", [2, LB, 6])
        ln_mv = carve("norm", [2, LB, 2])
        ln_rstd = carve("norm", [2, LB])
        ln_work = carve("norm", [2, 2, LB])
        slot_onehot = onehot_bucket
        gather_row = [gather_row_0, sb("gather_row_1", [P, NS], I32)]
        receiver = [receiver_0, sb("receiver_1", [P, NS], F32)]

        moments = sb("moments", [P, NB + 1, 2], F32)
        rstd = sb("rstd", [P, NB + 1], F32)

        ring = sb("ring", [P, RING, 2 * D], F16)
        index_stage = sb("index_stage", [P, 2, RING], I32)
        onehot_node = sb("onehot_node", [P, OH, BATCH, P], F16)
        inv_count = sb("inv_count", [P, 4], F32)
        hi_mean = sb("hi_mean", [P, D], F32)
        mean_b = sb("mean_b", [P, D], F32)
        has_edge = sb("has_edge", [P, 2, NB], F32)

        w_gate, gate_lo = twin_sb("w_gate", [P, 6, G3])
        gate_bias, bias_lo = twin_sb("gate_bias", [4, G3 + D])
        ring_words = ring[:].rearrange("p a b -> p (a b)").bitcast(F32)
        w_ih_raw = ring_words[:, 0:4 * G3].rearrange("p (a b) -> p a b", a=4)
        w_conv = ring_words[:, 4 * G3:4 * G3 + 4 * D].rearrange("p (a b) -> p a b", a=4)
        b_conv = sb("b_conv", [P, 8], F32)
        r_b1 = sb("r_b1", [P, 1], F32)
        r_w2 = sb("r_w2", [P, NE], F32)
        r_b2 = sb("r_b2", [P, 2, NE], F32)
        e_b1 = sb("e_b1", [P, NE, 2], F32)
        e_b2 = sb("e_b2", [P, NE, 2], F32)
        r_w1, r_lo = carve("dense", [2, P], twin=True)
        e_b3 = carve("dense", [D])[0:NE, :]
        e_w, e_lo = zip(*[carve("dense", [NE * 2, D], twin=True) for _ in range(3)])
        e_hi = [carve("dense", [NE * 2, D], F32R) for _ in range(3)]
        r_hi = carve("dense", [2, P], F32R)
        gate_hi = carve("dense", [6, G3], F32R)
        bias_hi = carve("dense", [G3 + D], F32R)[0:4, :]
        weights = [(e_hi[0], e_lo[0], e_w[0]), (e_hi[1], e_lo[1], e_w[1]), (e_hi[2], e_lo[2], e_w[2]),
                   (gate_hi, gate_lo[:], w_gate[:]), (bias_hi, bias_lo[:], gate_bias[:]), (r_hi, r_lo, r_w1)]
        x_t = carve("dense", [2, D])
        h_t = carve("dense", [2, D])
        mean_a_t = carve("dense", [2, D])
        tile_hi, tile_lo = carve("dense", [6, P], F32R), carve("dense", [6, P], F32R)
        gates = carve("dense", [2 * D])
        gate_tmp = carve("dense", [D])
        new_t = carve("dense", [D])
        x1 = carve("dense", [2, D])
        xn = carve("dense", [2, D])
        xn_hi, xn_lo = carve("dense", [2, 2 * P], F32R), carve("dense", [2, 2 * P], F32R)
        router_h = carve("dense", [2 * P])
        h1, h1_hi, h1_lo = (carve("dense", [2, 2, 2 * P], dt) for dt in (F32, F32R, F32R))
        h2, h2_hi, h2_lo = (carve("dense", [2, 2, 2 * P], dt) for dt in (F32, F32R, F32R))
        acc = carve("dense", [2, D])
        flags = sb("flags", [P, 4], F32)
        flags_T = carve("dense", [P], F32R)[0:4, :]
        ln_s = sb("ln_s", [P, 12], F32)
        logits = sb("logits", [P, 2, NE], F32)
        prob = sb("prob", [P, 2, 8], F32)
        top = sb("top", [P, 2, 8], F32)
        top_at = sb("top_at", [P, 2, 8], U32)
        rt = sb("rt", [P, 24], F32)
        coef = sb("coef", [P, 2, NE], F32)
        coef2 = sb("coef2", [P, 2, NE], F32)
        coef_T = carve("dense", [2, P])[0:NE]

        names = ("consts const_step edges_in ln_step h_ready hi_ready diff_ready split_ready table_stored "
                 "dve_step onehot_ready onehot_used slots16_ready slot_prefix_ready base_ready "
                 "list_at_ready list_zeroed list_in scatter_staged merged sort_ready sort_used sort_summed "
                 "decoded stage_ready turn owners_marked owners_summed rows_landed slot_done "
                 "node_onehot_used key_ready node_onehot_ready bucket_done inv_ready hi_mean_ready "
                 "inv_step evac_done fold_in fold_zero small_in fold_summed fold_done experts_in x_used "
                 "high_ready low_ready mean_a_free h_tile_ready tile_a_turned tile_a_hi tile_a_ready "
                 "tile_b_turned tile_b_ready flags_ready rz_summed n_summed rz_ready pre_new_ready "
                 "new_ready xn_ready xn_turned xn_hi_ready xn_T_ready router_summed router_ready "
                 "logits_summed shifted_ready exp_ready prob_gap_ready gap_exp_ready coef_ready "
                 "coef_turned coef_T_ready b3_summed acc_started gate_step ffn_step l1_summed h1_hi_ready "
                 "h1_ready l2_summed h2_hi_ready h2_ready l3_summed combined acc_done acc_free out_landed").split()
        ln_in = [sem(f"ln_in{i}") for i in range(2)]
        spill_landed = [sem(f"spill_landed{i}") for i in range(2)]
        x_landed = [sem(f"x_landed{i}") for i in range(2)]
        S = {n: sem(n) for n in names}
        scatter_landed = [sem(f"scatter_landed{i}") for i in range(2)]
        ring_landed = [sem(f"ring_landed{i}") for i in range(RINGS)]
        store_landed = [sem(f"store_landed{i}") for i in range(2)]
        N_CONSTS = 18
        sums, counts = banks[4], banks[5]
        sort_hi, sort_lo = banks[0:2], banks[2:4]
        turned, rz_bank, n_bank, l1_bank, l2_bank, l3_bank = banks[0], banks[1], banks[2], banks[3], banks[6], banks[7]
        mean_bank = (rz_bank, turned)
        route_bank = n_bank

        def four(bank):
            return bank[:].rearrange("p (a b) -> p a b", a=4)

        def two(ap):
            return ap.rearrange("p (a b) -> p a b", a=2)

        block = ctx.enter_context(nc.Block())

        @block.gpsimd
        def _(pool):
            g = nc.gpsimd
            c = S["consts"]
            g.iota(iota_cols[:], [[1, NS]], base=0, channel_multiplier=0,
                   allow_small_or_imprecise_dtypes=True).then_inc(c, 1)
            g.iota(iota_bucket[:], [[1, NB]], base=0, channel_multiplier=0,
                   allow_small_or_imprecise_dtypes=True).then_inc(c, 1)
            g.iota(iota_down[:], [[-1, NB]], base=NB - 1, channel_multiplier=0,
                   allow_small_or_imprecise_dtypes=True).then_inc(c, 1)
            g.iota(pad_position[:], [[0, 1]], base=NS * P, channel_multiplier=1,
                   allow_small_or_imprecise_dtypes=True).then_inc(c, 1)
            g.memset(moments[:, NB:NB + 1, :], 0.0).then_inc(c, 1)
            g.memset(rstd[:, NB:NB + 1], 1.0).then_inc(c, 1)
            g.memset(ones_col[:], 1.0).then_inc(c, 1)
            g.memset(zeros16[:], 0.0).then_inc(c, 1)
            g.memset(first_batch[:], BATCHES - 1).then_inc(c, 1)
            g.memset(ones16[:], 1.0).then_inc(c, 1)
            g.iota(bucket_key[:], [[KEY, NB]], base=KEY + 1, channel_multiplier=0,
                   allow_small_or_imprecise_dtypes=True).then_inc(c, 1)
            g.memset(ones_wide, 1.0).then_inc(c, 1)
            g.memset(lower, 1.0).then_inc(S["const_step"], 1)
            g.memset(pick_row, 0.0).then_inc(S["const_step"], 1)
            g.memset(spread_row, 0.0).then_inc(S["const_step"], 1)
            g.memset(lower_bucket, 1.0).then_inc(S["const_step"], 1)
            g.memset(ident[:], 0.0).then_inc(S["const_step"], 1)
            g.memset(gate_bias[:], 0.0).then_inc(S["fold_zero"], 1)
            g.memset(b_conv[:], 0.0).then_inc(S["fold_zero"], 1)
            g.memset(flags[:], 1.0).then_inc(c, 1)
            g.memset(prob[:], -1.0).then_inc(c, 1)
            pool.wait_ge(S["const_step"], 5)
            g.affine_select(out=spread_row, in_=spread_row, compare_op=ALU.not_equal, fill=float(RADIX),
                            base=0, pattern=[[-1, NB], [0, P]], channel_multiplier=1
                            ).then_inc(S["const_step"], 1)
            g.memset(pick_row[:, 127:128], 1.0).then_inc(S["const_step"], 1)
            g.memset(pick_row[:, 127 + HALF:128 + HALF], 1.0).then_inc(S["const_step"], 1)
            g.affine_select(out=lower, in_=lower, compare_op=ALU.is_gt, fill=0.0, base=0,
                            pattern=[[1, P]], channel_multiplier=-1).then_inc(c, 1)
            lb = lower_bucket.rearrange("p (a m) -> p a m", a=2)
            g.affine_select(out=lb, in_=lb, compare_op=ALU.is_gt, fill=0.0, base=0,
                            pattern=[[0, 2], [1, HALF]], channel_multiplier=-1).then_inc(c, 1)
            g.affine_select(out=ident[:], in_=ident[:], compare_op=ALU.not_equal, fill=1.0, base=0,
                            pattern=[[-1, P]], channel_multiplier=1).then_inc(c, 1)
            pool.wait_ge(S["const_step"], 8)
            g.affine_select(out=spread_row, in_=spread_row, compare_op=ALU.not_equal, fill=1.0,
                            base=-HALF, pattern=[[-1, NB], [0, P]], channel_multiplier=1).then_inc(c, 1)

            pool.wait_ge(S["list_zeroed"], 10 * 16)
            first = SORTED_TILES // (2 * SCATTER)
            for d, r_lo, past in ((0, first, -first), (1, 0, NS // (2 * SCATTER) - first)):
                pool.wait_ge(S["list_at_ready"], d + 1)
                with pool.Fori(r_lo, NS // (2 * SCATTER)) as r:
                    for k in range(2):
                        n_ = r + past
                        if d == 1:
                            pool.wait_ge(scatter_landed[k], n_ * (16 * SCATTER))
                            pool.sem_inc(S["turn"], 1)
                        tiles = bass.ds(r * (2 * SCATTER) + k * SCATTER, SCATTER)
                        g.tensor_copy(at_stage[:, k, :], list_at[:, d, tiles]).then_inc(S["scatter_staged"], 1)
                        g.tensor_copy(payload_stage[:, k, :], payload[:, d, tiles]).then_inc(S["scatter_staged"], 1)
                        pool.wait_ge(S["scatter_staged"], n_ * 4 + (2 * k + 2))
                        pool.sem_inc(S["turn"], 1)
                        for q in range(SCATTER):
                            g.indirect_dma_start(
                                out=lists[d][:], out_offset=bass.IndirectOffsetOnAxis(ap=at_stage[:, k, q:q + 1], axis=0),
                                in_=payload_stage[:, k, q:q + 1], in_offset=None,
                            ).then_inc(scatter_landed[k], 16)
                    if d == 0:
                        for k in range(2):
                            pool.wait_ge(scatter_landed[k], n_ * (16 * SCATTER) + 16 * SCATTER)
                        pool.sem_inc(S["turn"], 1)

            pool.wait_ge(S["table_stored"], NB // LB + 2)
            pool.wait_ge(S["fold_done"], 2)
            for d in range(2):
                pool.wait_ge(S["decoded"], d + 1)
                with pool.Fori(0, NS // RING // 2) as r:
                    for k in range(2 * RINGS):
                        pool.wait_ge(S["slot_done"], r * (2 * RING) + (d * NS + k * BATCH + BATCH))
                        pool.sem_inc(S["turn"], 1)
                        round_, part = k // RINGS, k % RINGS
                        if part == 0:
                            g.tensor_copy(index_stage[:, round_, :],
                                          gather_row[d][:, bass.ds(r * (2 * RING) + round_ * RING, RING)]
                                          ).then_inc(S["stage_ready"], 1)
                            pool.wait_ge(S["stage_ready"], r * 2 + (d * (NS // RING) + round_ + 1))
                            pool.sem_inc(S["turn"], 1)
                        for q in range(BATCH):
                            at_ = part * BATCH + q
                            g.indirect_dma_start(
                                out=ring[:, at_, :], out_offset=None, in_=table[:],
                                in_offset=bass.IndirectOffsetOnAxis(ap=index_stage[:, round_, at_:at_ + 1], axis=0),
                            ).then_inc(ring_landed[part], 16)

        @block.sync
        def _(sp):
            sp.dma_start(key, edges).then_inc(S["edges_in"], 16)
            sp.wait_ge(S["consts"], N_CONSTS)
            for d in range(2):
                entries = lists[d].rearrange("(p n) o -> p (n o)", p=P)[:, 0:NS]
                for q in range(4):
                    sp.dma_start(entries[:, q * (NS // 4):(q + 1) * (NS // 4)],
                                 zeros16[:, 0:NS // 2].bitcast(I32)).then_inc(S["list_zeroed"], 16)
            for q in range(2):
                sp.dma_start(means[NP + q * P:NP + q * P + P, :], zeros16[:].bitcast(F32)
                             ).then_inc(S["list_zeroed"], 16)
            sp.sem_inc(S["table_stored"], 2)
            x_b = x[0:NP, :].rearrange("(s t p) d -> s p t d", t=LB, p=P)
            table_b = table.rearrange("(s t p) d -> s p t d", t=LB, p=P)
            for k in range(2):
                sp.dma_start(ln_x[k], x_b[k]).then_inc(ln_in[k], 16)

            def store_rows(r, more):
                for k in range(2):
                    sp.wait_ge(S["split_ready"], r * 2 + (k + 3))
                    sp.dma_start(table_b[bass.ds(r * 2 + k, 1), :, :, :].rearrange("a p t d -> (a p) t d"),
                                 ln_split[k]).then_inc(store_landed[k], 16)
                    if more:
                        sp.dma_start(ln_x[k], x_b[bass.ds(r * 2 + (k + 2), 1), :, :, :].rearrange("a p t d -> (a p) t d")
                                     ).then_inc(ln_in[k], 16)
                for k in range(2):
                    sp.wait_ge(store_landed[k], r * 16 + 16)
                    sp.sem_inc(S["table_stored"], 1)

            with sp.Fori(0, NB // LB // 2 - 1) as r:
                store_rows(r, True)
            store_rows(NB // LB // 2 - 1, False)
            for d in range(2):
                rounds = (d + 1) * (NS // (2 * SCATTER)) - SORTED_TILES // (2 * SCATTER)
                for k in range(2):
                    sp.wait_ge(scatter_landed[k], rounds * 16 * SCATTER)
                sp.dma_start(raw_list[:, d, :], lists[d].rearrange("(p n) o -> p (n o)", p=P)[:, 0:NS]
                             ).then_inc(S["list_in"], 16)
                sp.wait_ge(S["list_in"], d * 16 + 16)
            for d in range(2):
                if d == 0:
                    sp.wait_ge(S["decoded"], 2)
                    sp.dma_start(r_w1, w["r_w1"].rearrange("(c p) n -> p c n", p=P)).then_inc(S["experts_in"], 16)
                    sp.dma_start(e_b3, w["e_b3"]).then_inc(S["experts_in"], 16)
                    for n, name in enumerate(("e_w1", "e_w2", "e_w3")):
                        sp.dma_start(e_w[n], w[name].rearrange("e (c p) n -> p (e c) n", p=P)
                                     ).then_inc(S["experts_in"], 16)
                with sp.Fori(0, NS // RING) as r:
                    for k in range(RINGS):
                        sp.wait_ge(ring_landed[k], r * (16 * BATCH) + (d * (NS // RING) + 1) * 16 * BATCH)
                        sp.sem_inc(S["rows_landed"], 1)

        @block.scalar
        def _(act):
            a = nc.scalar
            for dst_, src_ in ((w_ih_raw, w["w_ih_T"].rearrange("(c p) n -> p c n", p=P)),
                               (w_conv[:, 0:2, :], w["w_in"].rearrange("(c p) n -> p c n", p=P)),
                               (w_conv[:, 2:4, :], w["w_out"].rearrange("(c p) n -> p c n", p=P)),
                               (w_gate[:, 4:6, :], w["w_hh_T"].rearrange("(c p) n -> p c n", p=P))):
                act.dma_start(dst_, src_).then_inc(S["fold_in"], 16)
            act.wait_ge(S["fold_zero"], 2)
            act.dma_start(gate_bias[2:3, 0:G3], w["b_ih"]).then_inc(S["fold_in"], 16)
            act.dma_start(gate_bias[2:3, G3:G3 + D], w["b_hh"][:, 2 * D:G3]).then_inc(S["fold_in"], 16)
            act.dma_start(gate_bias[3:4, 0:2 * D], w["b_hh"][:, 0:2 * D]).then_inc(S["fold_in"], 16)
            bc = b_conv[:].rearrange("p (a c m) -> p a c m", a=2, c=2)
            for n, name in enumerate(("b_in", "b_out")):
                for c in range(2):
                    act.dma_start(bc[:, n, c, n:n + 1], w[name][c * P:c * P + P, :]).then_inc(S["fold_in"], 16)
            smalls = ((r_b1[:], w["r_b1"]),
                      (r_w2[:], w["r_w2"]), (r_b2[:, 0, :], w["r_b2"].to_broadcast([P, NE])),
                      (r_b2[:, 1, :], w["r_b2"].to_broadcast([P, NE])), (e_b1[:], w["e_b1"]),
                      (e_b2[:], w["e_b2"]))
            for dst_, src_ in smalls:
                act.dma_start(dst_, src_).then_inc(S["small_in"], 16)
            act.wait_ge(S["fold_summed"], 1)
            for m in range(4):
                a.copy(w_gate[:, m, 0:2 * D], banks[2 * m][:, 0:2 * D])
                ins = a.copy(w_gate[:, m, 2 * D:G3], banks[2 * m + 1][:, 0:D])
            ins.then_inc(S["fold_done"], 1)
            act.wait_ge(S["fold_summed"], 2)
            a.copy(gate_bias[0:2, 0:2 * D], banks[0][0:2, 0:2 * D])
            a.copy(gate_bias[0:2, 2 * D:G3], banks[1][0:2, 0:D]).then_inc(S["fold_done"], 1)
            act.sem_inc(S["split_ready"], 2)
            with act.Fori(0, NB // LB // 2) as r:
                for k in range(2):
                    act.wait_ge(S["table_stored"], r * 2 + (k + 1))
                    act.sem_inc(S["turn"], 1)
                    act.wait_ge(S["h_ready"], r * 2 + (k + 1))
                    a.copy(ln_split[k][:, :, 0:D], ln_h[k]).then_inc(S["hi_ready"], 1)
                    act.wait_ge(S["diff_ready"], r * 2 + (k + 1))
                    a.activation(ln_split[k][:, :, D:2 * D], ln_h[k], ACT.Copy, scale=LO_SCALE
                                 ).then_inc(S["split_ready"], 1)

            def hi_mean_step(q):
                act.wait_ge(S["inv_ready"], q)
                a.activation(hi_mean[:], sums[:, 0:D], ACT.Copy, scale=inv_count[:, 1:2]
                             ).then_inc(S["hi_mean_ready"], 1)

            means_tiles = means.rearrange("(j p) d -> j p d", p=P)
            act.sem_inc(S["mean_a_free"], 2)
            act.wait_ge(S["decoded"], 2)
            for first, last, split in ((0, FIRST_PAIRS, weights[0:2]), (FIRST_PAIRS, NB // 2, weights[2:])):
                with act.Fori(first, last) as r:
                    for k in range(2):
                        hi_mean_step(r * 2 + (k + 1))
                        act.wait_ge(S["evac_done"], r * 2 + (k + 2))
                        act.dma_start(means_tiles[bass.ds(r * 2 + k, 1), :, :].rearrange("a p d -> (a p) d"),
                                      mean_a_t[:, k, :]).then_inc(spill_landed[k], 16)
                    for k in range(2):
                        act.wait_ge(spill_landed[k], r * 16 + 16)
                        act.sem_inc(S["mean_a_free"], 1)
                act.wait_ge(S["experts_in"], 5 * 16)
                for hi_, lo_, raw in split:
                    a.copy(hi_, raw).then_inc(S["high_ready"], 1)
            x_tiles = x.rearrange("(j p) d -> j p d", p=P)
            out_tiles = out.rearrange("(j p) d -> j p d", p=P)
            act.sem_inc(S["acc_free"], 1)
            act.sem_inc(S["h1_hi_ready"], 1)
            act.sem_inc(S["h2_hi_ready"], 1)

            def load_tile(r, o):
                jj = o % 2
                act.wait_ge(S["x_used"], r * 2 + (o + 1))
                for t_, src_ in ((x_t, x_tiles), (mean_a_t, means_tiles)):
                    act.dma_start(t_[:, jj, :], src_[bass.ds(r * 2 + o, 1), :, :].rearrange("a p d -> (a p) d")
                                  ).then_inc(x_landed[jj], 16)

            def tile_a(r, o):
                act.wait_ge(S["tile_a_turned"], r * 2 + (o + 1))
                a.copy(tile_hi[:, 0:4, :], four(mean_bank[o % 2])).then_inc(S["tile_a_hi"], 1)

            def out_mean(r, o):
                hi_mean_step(r * 2 + (NB + o + 1))

            def gate_values(r, o):
                act.wait_ge(S["rz_summed"], r * 2 + (o + 1))
                a.activation(gates, rz_bank[:], ACT.Tanh, scale=0.5).then_inc(S["rz_ready"], 1)
                act.wait_ge(S["pre_new_ready"], r * 2 + (o + 1))
                a.activation(new_t, gate_tmp, ACT.Tanh).then_inc(S["new_ready"], 1)

            def turn_xn(r, o):
                jj = o % 2
                act.wait_ge(S["xn_turned"], r * 2 + (o + 1))
                a.copy(xn_hi[:, :, jj * P:jj * P + P], two(turned[:, jj * 2 * P:jj * 2 * P + 2 * P])
                       ).then_inc(S["xn_hi_ready"], 1)

            def routing(q):
                act.wait_ge(S["router_summed"], q + 1)
                a.activation(router_h, route_bank[:, 0:2 * P], ACT.Relu, bias=r_b1[:, 0:1]
                             ).then_inc(S["router_ready"], 1)
                hidden1(q, 0)

            def scores(q):
                for tt in range(2):
                    act.wait_ge(S["shifted_ready"], q * 2 + (tt + 1))
                    a.activation(prob[:, tt, 0:NE], logits[:, tt, :], ACT.Exp, bias=rt[:, 2 + tt:3 + tt],
                                 accum_out=rt[:, 4 + tt:5 + tt]).then_inc(S["exp_ready"], 1)
                act.wait_ge(S["prob_gap_ready"], q + 1)
                a.activation(rt[:, 10:12], rt[:, 8:10], ACT.Exp).then_inc(S["gap_exp_ready"], 1)

            def hidden(q, x_, used, summed, landed, bank, bias, whole, high, ready):
                act.wait_ge(used, q * NE + (x_ + 1))
                act.sem_inc(S["turn"], 1)
                act.wait_ge(summed, q * NE + (x_ + 1 + landed))
                for to in (high, whole):
                    for m in range(2):
                        ins = a.activation(to[:, x_ % 2, m, :], bank[:, m * 2 * P:(m + 1) * 2 * P], ACT.Relu,
                                           bias=bias[:, x_, m:m + 1])
                ins.then_inc(ready, 1)

            def hidden1(q, x_):
                hidden(q, x_, S["l2_summed"], S["l1_summed"], 0, l1_bank, e_b1, h1, h1_hi, S["h1_hi_ready"])

            def hidden2(q, x_):
                hidden(q, x_, S["l3_summed"], S["l2_summed"], CREDIT, l2_bank, e_b2, h2, h2_hi, S["h2_hi_ready"])

            def store_out(q):
                act.wait_ge(S["acc_done"], q + 1)
                for tt in range(2):
                    act.dma_start(out_tiles[bass.ds(q * 2 + tt, 1), :, :].rearrange("a p d -> (a p) d"),
                                  acc[:, tt, :]).then_inc(S["out_landed"], 16)
                act.wait_ge(S["out_landed"], q * 32 + 32)
                act.sem_inc(S["acc_free"], 1)

            for o in range(2):
                load_tile(0, o)
            for o in range(2):
                tile_a(0, o)
                out_mean(0, o)
                gate_values(0, o)
            for o in range(2):
                turn_xn(0, o)
            for o in range(2, 4):
                load_tile(0, o)
            with act.Fori(0, NB // 2 - 1) as q:
                tile_a(q, 2)
                routing(q)
                out_mean(q, 2)
                scores(q)
                hidden1(q, 1)
                hidden2(q, 0)
                gate_values(q, 2)
                hidden1(q, 2)
                hidden2(q, 1)
                tile_a(q, 3)
                out_mean(q, 3)
                hidden1(q, 3)
                hidden2(q, 2)
                gate_values(q, 3)
                load_tile(q, 4)
                for x_ in (4, 5):
                    hidden1(q, x_)
                    hidden2(q, x_ - 1)
                hidden2(q, 5)
                for o in (2, 3):
                    turn_xn(q, o)
                load_tile(q, 5)
                store_out(q)
            last = NB // 2 - 1
            routing(last)
            scores(last)
            for x_ in range(1, NE + 1):
                if x_ < NE:
                    hidden1(last, x_)
                hidden2(last, x_ - 1)
            store_out(last)

        @block.vector
        def _(v):
            e = nc.vector
            steps = [0]

            def step(ins):
                steps[0] += 1
                ins.then_inc(S["dve_step"], 1)
                v.wait_ge(S["dve_step"], steps[0])

            v.wait_ge(S["consts"], N_CONSTS)
            v.wait_ge(S["edges_in"], 16)
            v.sem_inc(S["merged"], 2)
            def inverse_root(chain, y, variance, v_, t_):
                chain(e.tensor_scalar(v_, variance, EPS, None, ALU.add))
                chain(e.tensor_single_scalar(t_.bitcast(I32), v_.bitcast(I32), 1, ALU.arith_shift_right))
                chain(e.tensor_scalar(y.bitcast(I32), t_.bitcast(I32), -1.0, float(ROOT_SEED), ALU.mult, ALU.add))
                for _ in range(ROOT_STEPS):
                    chain(e.tensor_tensor(t_, y, y, ALU.mult))
                    chain(e.scalar_tensor_tensor(out=t_, in0=t_, scalar=-0.5, in1=v_, op0=ALU.mult, op1=ALU.mult))
                    chain(e.scalar_tensor_tensor(out=y, in0=t_, scalar=1.5, in1=y, op0=ALU.add, op1=ALU.mult))

            def layer_norm():
                with v.Fori(0, NB // LB // 2) as r:
                    for k in range(2):
                        v.wait_ge(ln_in[k], r * 16 + 16)
                        for t_ in range(LB):
                            ins = e.bn_stats(ln_stats[:, k, t_, :], ln_x[k][:, t_, :])
                        ins.then_inc(S["ln_step"], 1)
                        v.wait_ge(S["ln_step"], r * (2 * LN_STEPS) + (k * LN_STEPS + 1))
                        v.sem_inc(S["turn"], 1)
                        for t_ in range(LB):
                            ins = e.bn_aggr(ln_mv[:, k, t_, :], ln_stats[:, k, t_, :])
                        ins.then_inc(S["ln_step"], 1)
                        v.wait_ge(S["ln_step"], r * (2 * LN_STEPS) + (k * LN_STEPS + 2))
                        tiles = bass.ds(r * (2 * LB) + k * LB, LB)
                        e.tensor_copy(moments[:, tiles, :], ln_mv[:, k, :, :])
                        n = [2]

                        def ln_link(ins):
                            n[0] += 1
                            ins.then_inc(S["ln_step"], 1)
                            v.wait_ge(S["ln_step"], r * (2 * LN_STEPS) + (k * LN_STEPS + n[0]))

                        inverse_root(ln_link, ln_rstd[:, k, :], ln_mv[:, k, :, 1], ln_work[:, k, 0, :], ln_work[:, k, 1, :])
                        assert n[0] == LN_STEPS - 1
                        e.tensor_copy(rstd[:, tiles], ln_rstd[:, k, :]).then_inc(S["ln_step"], 1)
                        v.wait_ge(S["split_ready"], r * 2 + (k + 1))
                        for t_ in range(LB):
                            ins = e.tensor_scalar(ln_h[k][:, t_, :], ln_x[k][:, t_, :], ln_mv[:, k, t_, 0:1],
                                                  ln_rstd[:, k, t_:t_ + 1], ALU.subtract, ALU.mult)
                        ins.then_inc(S["h_ready"], 1)
                        v.wait_ge(S["hi_ready"], r * 2 + (k + 1))
                        e.tensor_tensor(ln_h[k], ln_h[k], ln_split[k][:, :, 0:D], ALU.subtract
                                        ).then_inc(S["diff_ready"], 1)

            def positions(d):
                q0 = d * 2 * NB
                k_, v_ = key[:, d, :], key[:, 1 - d, :]
                s0, s1, s2 = scratch
                step(e.tensor_single_scalar(s0, k_, 7, ALU.arith_shift_right))
                e.tensor_copy(bucket, s0)
                e.tensor_scalar(valid, k_, float(SENTINEL), None, ALU.is_lt)
                step(e.tensor_single_scalar(s1, k_, P - 1, ALU.bitwise_and))
                step(e.scalar_tensor_tensor(out=s2, in0=v_, scalar=256.0, in1=s1, op0=ALU.mult, op1=ALU.add))
                step(e.scalar_tensor_tensor(out=payload[:, d, :], in0=s2, scalar=1.0, in1=valid,
                                            op0=ALU.add, op1=ALU.mult))
                if d == 0:
                    e.tensor_single_scalar(s0, payload[:, d, :], 11, ALU.arith_shift_right)
                    step(e.tensor_single_scalar(s1, payload[:, d, :], 2047, ALU.bitwise_and))
                    e.tensor_copy(pay_hi, s0)
                    step(e.tensor_copy(pay_lo, s1))
                step(e.tensor_scalar(position, iota_cols[:], float(P), pad_position[:, 0:1], ALU.mult, ALU.add))

                def onehot(b, k, q, number=iota_bucket):
                    v.wait_ge(S["onehot_used"], q)
                    e.tensor_scalar(onehot_bucket[:, k, :], bucket, number[:, b], None, ALU.is_equal
                                    ).then_inc(S["onehot_ready"], 1)

                with v.Fori(0, NB // 2) as r:
                    for k in range(2):
                        onehot(bass.ds(r * 2 + k, 1), k, r * 2 + (q0 + k + 1), iota_down)
                v.wait_ge(S["onehot_used"], q0 + NB + 2)
                for h in range(2):
                    cols = slice(h * HS, h * HS + HS)
                    step(e.tensor_tensor_scan(prefix[:, cols], ones_wide, banks[h][:, 0:HS],
                                              prefix[:, HS - 1:HS] if h else 0.0, ALU.mult, ALU.add))
                step(e.tensor_scalar(bucket_i[:, 0:1], prefix[:, NS - 1:NS], float(P - 1), None, ALU.add))
                step(e.tensor_single_scalar(bucket_i[:, 1:2], bucket_i[:, 0:1], 7, ALU.arith_shift_right))
                e.tensor_scalar(bucket_slots16[:], bucket_i[:, 1:2], 1.0, None, ALU.max
                                ).then_inc(S["slots16_ready"], 1)
                v.wait_ge(S["slot_prefix_ready"], d + 1)
                step(e.tensor_copy(first_row[0:1, 0:NB], banks[7][0:1, 0:NB]))
                e.tensor_single_scalar(first_batch[0:1, d, 0:NB], first_row[0:1, 0:NB], BATCH.bit_length() - 1,
                                       ALU.arith_shift_right)
                e.tensor_copy(first_slot[:, d:d + 1], banks[6][:, 0:1])
                step(e.tensor_scalar(bucket_slots[:, 0:1], banks[6][:, 0:1], float(P), None, ALU.mult))
                for h in range(2):
                    cols = slice(h * HS, h * HS + HS)
                    step(e.scalar_tensor_tensor(out=s0[:, cols], in0=prefix[:, cols], scalar=bucket_slots[:, 0:1],
                                                in1=banks[h][:, 0:HS], op0=ALU.add, op1=ALU.subtract))
                e.tensor_single_scalar(s1[0:HALF], s0[0:HALF], 6, ALU.arith_shift_right)
                step(e.tensor_single_scalar(s1[HALF:P], s0[HALF:P], RADIX - 1, ALU.bitwise_and))
                e.tensor_copy(base_digits, s1).then_inc(S["base_ready"], 1)
                def merge(k, q, m):
                    v.wait_ge(S["onehot_used"], q)
                    v.sem_inc(S["turn"], 1)
                    for h in range(2):
                        cols = slice(h * HS, h * HS + HS)
                        ins = e.copy_predicated(position[:, cols], onehot_bucket[:, k, cols].bitcast(U16),
                                                banks[2 + 2 * k + h][:, 0:HS])
                    ins.then_inc(S["merged"], 1)
                    v.wait_ge(S["merged"], m)
                q1 = q0 + NB

                def onehot_of(r, b):
                    onehot(bass.ds(r * 2 + b, 1), b % 2, r * 2 + (q1 + b + 1))

                def merge_of(r, b):
                    merge(b % 2, r * 2 + (q1 + b + 3), r * 2 + (d * NB + b + 3))

                onehot_of(0, 0)
                with v.Fori(0, NB // 2 - 1) as r:
                    for b in range(2):
                        onehot_of(r, b + 1)
                        merge_of(r, b)
                onehot_of(0, NB - 1)
                merge_of(0, NB - 2)
                merge_of(0, NB - 1)
                step(e.tensor_copy(s0, position))
                e.tensor_single_scalar(s1, s0, 7, ALU.arith_shift_right)
                step(e.tensor_single_scalar(s2, s0, P - 1, ALU.bitwise_and))
                if d == 0:
                    e.tensor_copy(slot_of, s1)
                    e.tensor_copy(row_of, s2)
                e.scalar_tensor_tensor(out=list_at[:, d, :], in0=s2, scalar=float(2 * NS), in1=s1,
                                       op0=ALU.mult, op1=ALU.add).then_inc(S["list_at_ready"], 1)
                v.wait_ge(S["list_at_ready"], d + 1)

            positions(0)
            positions(1)
            layer_norm()

            def sort_step(t, k, u):
                v.wait_ge(S["sort_used"], u)
                for half, pay in ((0, pay_hi), (1, pay_lo)):
                    e.tensor_scalar(row_payload[:, k, half * P:half * P + P], iota_cols[:, 0:P],
                                    row_of[:, bass.ds(t, 1)], pay[:, bass.ds(t, 1)],
                                    ALU.is_equal, ALU.mult)
                e.tensor_scalar(slot_onehot[:, k, :], iota_cols[:], slot_of[:, bass.ds(t, 1)], None,
                                ALU.is_equal).then_inc(S["sort_ready"], 1)

            with v.Fori(0, SORTED_TILES // 2) as r:
                for k in range(2):
                    sort_step(r * 2 + k, k, r * 2 + (k + 1))
            v.wait_ge(S["sort_summed"], 1)
            for d in range(2):
                s0, s1, s2 = scratch
                step(e.tensor_scalar(onehot_bucket[0:NB, 0, :], iota_cols[0:NB, :], first_slot[0:NB, d:d + 1], None,
                                     ALU.is_ge))
                v.sem_inc(S["owners_marked"], 1)
                v.wait_ge(S["list_in"], d * 16 + 16)
                listed = raw_list[:, d, :]
                if d == 0:
                    for h in range(2):
                        cols = slice(h * HS, h * HS + HS)
                        step(e.tensor_tensor(s0[:, cols], sort_lo[h][:, 0:HS], listed[:, cols], ALU.add))
                        step(e.scalar_tensor_tensor(out=s1[:, cols], in0=sort_hi[h][:, 0:HS], scalar=2048.0,
                                                    in1=s0[:, cols], op0=ALU.mult, op1=ALU.add))
                    listed = s1
                step(e.tensor_single_scalar(s2, listed, 255, ALU.bitwise_and))
                v.wait_ge(S["owners_summed"], d + 1)
                for h in range(2):
                    cols = slice(h * HS, h * HS + HS)
                    step(e.scalar_tensor_tensor(out=receiver[d][:, cols], in0=banks[4 + h][:, 0:HS],
                                                scalar=float(KEY), in1=s2[:, cols], op0=ALU.mult, op1=ALU.add))
                e.tensor_single_scalar(gather_row[d][:, :], listed, 8, ALU.arith_shift_right
                                       ).then_inc(S["decoded"], 1)
                v.wait_ge(S["decoded"], d + 1)

            def first_onehots(d, j):
                lo = v.value_load(first_batch[0:1, d, bass.ds(j, 1)], min_val=0, max_val=BATCHES - 1)
                hi = v.value_load(first_batch[0:1, d, bass.ds(j + 1, 1)], min_val=0, max_val=BATCHES - 1)
                e.tensor_scalar(node_key[:], iota_cols[:, 0:P], bucket_key[:, bass.ds(j, 1)], None, ALU.add
                                ).then_inc(S["key_ready"], 1)
                v.wait_ge(S["key_ready"], j + (d * NB + 1))
                v.sem_inc(S["turn"], 1)

                def visit(b):
                    at_ = b + j
                    v.wait_ge(S["node_onehot_used"], at_ + (d * VISITS + 1))
                    v.sem_inc(S["turn"], 1)
                    e.tensor_tensor(
                        onehot_node[:, bass.ds((at_ + d * VISITS) % OH, 1), :, :].rearrange("p a s m -> p (a s) m"),
                        receiver[d][:, bass.ds(b * BATCH, BATCH)].rearrange("p (s o) -> p s o", o=1
                                                                            ).to_broadcast([P, BATCH, P]),
                        node_key[:].rearrange("p (o m) -> p o m", o=1).to_broadcast([P, BATCH, P]),
                        ALU.is_equal).then_inc(S["node_onehot_ready"], 1)

                visit(lo)
                return lo, hi, visit

            def bucket_mean(d, j, dest, begun, meanwhile=None):
                lo, hi, visit = begun
                v.sem_inc(S["turn"], 1)
                with v.If(hi > lo):
                    with v.Fori(lo + 1, hi + 1) as b:
                        visit(b)
                if meanwhile:
                    meanwhile()
                v.wait_ge(S["bucket_done"], j + (d * NB + 1))
                e.tensor_scalar(has_edge[:, d, bass.ds(j, 1)], counts[:, 0:1], 1.0, None, ALU.min)
                e.tensor_scalar(inv_count[:, 0:1], counts[:, 0:1], 1.0, None, ALU.max
                                ).then_inc(S["inv_step"], 1)
                v.wait_ge(S["inv_step"], j * 2 + (d * 2 * NB + 1))
                e.reciprocal(inv_count[:, 1:2], inv_count[:, 0:1]).then_inc(S["inv_ready"], 1)
                v.wait_ge(S["inv_ready"], j + (d * NB + 1))
                e.tensor_scalar(inv_count[:, 2:3], inv_count[:, 1:2], 1.0 / LO_SCALE, None, ALU.mult
                                ).then_inc(S["inv_step"], 1)
                v.wait_ge(S["inv_step"], j * 2 + (d * 2 * NB + 2))
                v.wait_ge(S["hi_mean_ready"], j + (d * NB + 1))
                e.scalar_tensor_tensor(out=dest, in0=sums[:, D:2 * D], scalar=inv_count[:, 2:3],
                                       in1=hi_mean[:], op0=ALU.mult, op1=ALU.add).then_inc(S["evac_done"], 1)

            for first, last, split, done in ((0, FIRST_PAIRS, weights[0:2], 0), (FIRST_PAIRS, NB // 2, weights[2:], 2)):
                with v.Fori(first, last) as r:
                    for k in range(2):
                        v.wait_ge(S["mean_a_free"], r * 2 + (k + 1))
                        v.sem_inc(S["turn"], 1)
                        bucket_mean(0, r * 2 + k, mean_a_t[:, k, :], first_onehots(0, r * 2 + k))
                        v.wait_ge(S["evac_done"], r * 2 + (k + 2))
                        v.sem_inc(S["turn"], 1)
                for i_, (hi_, lo_, raw) in enumerate(split):
                    v.wait_ge(S["high_ready"], done + i_ + 1)
                    e.tensor_tensor(lo_, raw, hi_.bitcast(F32), ALU.subtract).then_inc(S["low_ready"], 1)

            v.sem_inc(S["x_used"], CREDIT)
            v.sem_inc(S["combined"], 1)
            v.wait_ge(S["small_in"], 6 * 16)
            n = {"gate_step": 0, "ffn_step": 0}

            def link(ins, name, base):
                n[name] += 1
                ins.then_inc(S[name], 1)
                v.wait_ge(S[name], base + n[name])

            def node_rows(r, o):
                jj, j = o % 2, r * 2 + o
                v.wait_ge(x_landed[jj], r * 32 + (o // 2 * 32 + 32))
                e.tensor_scalar(h_t[:, jj, :], x_t[:, jj, :], moments[:, bass.ds(j, 1), 0], rstd[:, bass.ds(j, 1)],
                                ALU.subtract, ALU.mult).then_inc(S["h_tile_ready"], 1)

            def out_means(r, o, begun, meanwhile=None):
                def low_a():
                    if meanwhile:
                        meanwhile()
                    v.wait_ge(S["tile_a_hi"], r * 2 + (o + 1))
                    e.tensor_tensor(tile_lo[:, 0:4, :], four(mean_bank[o % 2]), tile_hi[:, 0:4, :].bitcast(F32),
                                    ALU.subtract).then_inc(S["tile_a_ready"], 1)

                bucket_mean(1, r * 2 + o, mean_b[:], begun, low_a)
                e.tensor_copy(flags[:, 0:2], has_edge[:, :, bass.ds(r * 2 + o, 1)].rearrange("p a b -> p (a b)")
                              ).then_inc(S["flags_ready"], 1)

            def tile_b(r, o):
                n["gate_step"] = 0
                v.wait_ge(S["tile_b_turned"], r * 2 + (o + 1))
                turned_b = two(turned[:, 0:D])
                link(e.tensor_copy(tile_hi[:, 4:6, :], turned_b), "gate_step", r * (2 * GATE_STEPS) + o * GATE_STEPS)
                e.tensor_tensor(tile_lo[:, 4:6, :], turned_b, tile_hi[:, 4:6, :].bitcast(F32), ALU.subtract)
                e.tensor_copy(flags_T, turned[0:4, D:D + P]).then_inc(S["tile_b_ready"], 1)

            def new_rows(r, o):
                jj, j1 = o % 2, r * 2 + (o + 1)
                base = r * (2 * GATE_STEPS) + o * GATE_STEPS

                def next_(ins):
                    link(ins, "gate_step", base)

                v.wait_ge(S["n_summed"], j1)
                v.wait_ge(S["rz_ready"], j1)
                v.wait_ge(S["h_tile_ready"], j1)
                next_(e.scalar_tensor_tensor(out=gate_tmp, in0=gates[:, 0:D], scalar=1.0,
                                             in1=n_bank[:, D:2 * D], op0=ALU.add, op1=ALU.mult))
                e.scalar_tensor_tensor(out=gate_tmp, in0=gate_tmp, scalar=0.5, in1=n_bank[:, 0:D],
                                       op0=ALU.mult, op1=ALU.add).then_inc(S["pre_new_ready"], 1)
                v.wait_ge(S["new_ready"], j1)
                next_(e.tensor_tensor(new_t, new_t, h_t[:, jj, :], ALU.subtract))
                next_(e.scalar_tensor_tensor(out=new_t, in0=gates[:, D:2 * D], scalar=1.0, in1=new_t,
                                             op0=ALU.add, op1=ALU.mult))
                next_(e.scalar_tensor_tensor(out=x1[:, jj, :], in0=new_t, scalar=0.5, in1=x_t[:, jj, :],
                                             op0=ALU.mult, op1=ALU.add))
                v.sem_inc(S["x_used"], 1)
                next_(e.tensor_tensor(x1[:, jj, :], x1[:, jj, :], h_t[:, jj, :], ALU.add))

            def normalise(r, o):
                jj = o % 2

                def next_(ins):
                    link(ins, "gate_step", r * (2 * GATE_STEPS) + o * GATE_STEPS)

                next_(e.bn_stats(ln_s[:, 0:6], x1[:, jj, :]))
                v.sem_inc(S["turn"], 1)
                next_(e.bn_aggr(ln_s[:, 6:8], ln_s[:, 0:6]))
                inverse_root(next_, ln_s[:, 9:10], ln_s[:, 7:8], ln_s[:, 10:11], ln_s[:, 11:12])
                assert n["gate_step"] == GATE_STEPS
                e.tensor_scalar(xn[:, jj, :], x1[:, jj, :], ln_s[:, 6:7], ln_s[:, 9:10], ALU.subtract, ALU.mult
                                ).then_inc(S["xn_ready"], 1)

            def turn_pair(q):
                v.wait_ge(S["xn_hi_ready"], q * 2 + 2)
                for jj in range(2):
                    e.tensor_tensor(xn_lo[:, :, jj * P:jj * P + P], two(turned[:, jj * 2 * P:jj * 2 * P + 2 * P]),
                                    xn_hi[:, :, jj * P:jj * P + P].bitcast(F32), ALU.subtract
                                    ).then_inc(S["xn_T_ready"], 1)

            def low(q, x_, hi_ready, whole, high, low_part, ready):
                v.wait_ge(hi_ready, q * NE + (x_ + 2))
                e.tensor_tensor(low_part[:, x_ % 2, :, :], whole[:, x_ % 2, :, :],
                                high[:, x_ % 2, :, :].bitcast(F32), ALU.subtract).then_inc(ready, 1)

            def low1(q, x_):
                low(q, x_, S["h1_hi_ready"], h1, h1_hi, h1_lo, S["h1_ready"])

            def low2(q, x_):
                low(q, x_, S["h2_hi_ready"], h2, h2_hi, h2_lo, S["h2_ready"])

            def route(q):
                n["ffn_step"] = 0

                def next_(ins):
                    link(ins, "ffn_step", q * FFN_STEPS)

                v.wait_ge(S["logits_summed"], q + 1)
                next_(e.tensor_tensor(logits[:], two(route_bank[:, 2 * P:2 * P + 2 * NE]), r_b2[:], ALU.add))
                next_(e.tensor_reduce(rt[:, 0:2], logits[:], AX_X, ALU.max))
                next_(e.tensor_scalar(rt[:, 2:4], rt[:, 0:2], -1.0, None, ALU.mult))
                v.sem_inc(S["shifted_ready"], 2)
                v.wait_ge(S["exp_ready"], q * 2 + 2)
                next_(e.reciprocal(rt[:, 6:8], rt[:, 4:6]))
                for tt in range(2):
                    next_(e.tensor_scalar(prob[:, tt, 0:NE], prob[:, tt, 0:NE], rt[:, 6 + tt:7 + tt], None,
                                          ALU.mult))
                for tt in range(2):
                    v.sem_inc(S["turn"], 1)
                    next_(e.max(top[:, tt, :], prob[:, tt, :]))
                    v.sem_inc(S["turn"], 1)
                    next_(e.max_index(top_at[:, tt, :], top[:, tt, :], prob[:, tt, :]))
                e.tensor_tensor(rt[:, 8:10], top[:, :, 1], top[:, :, 0], ALU.subtract
                                ).then_inc(S["prob_gap_ready"], 1)
                next_(e.tensor_copy(two(rt[:, 16:20]), top_at[:, :, 0:2]))
                v.wait_ge(S["gap_exp_ready"], q + 1)
                next_(e.tensor_scalar(rt[:, 12:14], rt[:, 10:12], 1.0, None, ALU.add))
                next_(e.reciprocal(rt[:, 20:22], rt[:, 12:14]))
                next_(e.tensor_tensor(rt[:, 22:24], rt[:, 10:12], rt[:, 20:22], ALU.mult))
                for tt in range(2):
                    e.tensor_scalar(coef[:, tt, :], iota_bucket[:, 0:NE], rt[:, 16 + 2 * tt:17 + 2 * tt],
                                    rt[:, 20 + tt:21 + tt], ALU.is_equal, ALU.mult)
                    next_(e.tensor_scalar(coef2[:, tt, :], iota_bucket[:, 0:NE], rt[:, 17 + 2 * tt:18 + 2 * tt],
                                          rt[:, 22 + tt:23 + tt], ALU.is_equal, ALU.mult))
                next_(e.tensor_tensor(coef[:], coef[:], coef2[:], ALU.add))
                v.sem_inc(S["coef_ready"], 1)

            def start_sum(q):
                low1(q, 1)
                v.wait_ge(S["coef_turned"], q + 1)
                e.tensor_copy(coef_T, two(route_bank[0:NE, 0:2 * P])).then_inc(S["coef_T_ready"], 1)
                low2(q, 0)
                v.wait_ge(S["acc_free"], q + 1)
                v.sem_inc(S["turn"], 1)
                v.wait_ge(S["b3_summed"], q + 1)
                for tt in range(2):
                    link(e.tensor_tensor(acc[:, tt, :], route_bank[:, tt * D:tt * D + D], x1[:, tt, :], ALU.add),
                         "ffn_step", q * FFN_STEPS)
                assert n["ffn_step"] == FFN_STEPS
                v.sem_inc(S["acc_started"], 1)

            def combine(q, x_):
                v.wait_ge(S["l3_summed"], q * NE + (x_ + 1 + CREDIT))
                for tt in range(2):
                    ins = e.scalar_tensor_tensor(out=acc[:, tt, :], in0=l3_bank[:, tt * D:tt * D + D],
                                                 scalar=coef[:, tt, x_:x_ + 1], in1=acc[:, tt, :],
                                                 op0=ALU.mult, op1=ALU.add)
                ins.then_inc(S["combined"], 1)
                v.wait_ge(S["combined"], q * NE + (x_ + 2))

            def experts(q, x_):
                if x_ < NE:
                    low1(q, x_)
                if x_ - 1 < NE:
                    low2(q, x_ - 1)
                combine(q, x_ - 2)

            for o in range(2):
                node_rows(0, o)
                v.sem_inc(S["turn"], 1)
                out_means(0, o, first_onehots(1, o))
                tile_b(0, o)
                new_rows(0, o)
                normalise(0, o)
            node_rows(0, 2)
            with v.Fori(0, NB // 2 - 1) as q:
                turn_pair(q)
                out_means(q, 2, first_onehots(1, q * 2 + 2), lambda: low1(q, 0))
                tile_b(q, 2)
                route(q)
                node_rows(q, 3)
                start_sum(q)
                begun = first_onehots(1, q * 2 + 3)
                new_rows(q, 2)
                out_means(q, 3, begun, lambda: (experts(q, 2), normalise(q, 2)))
                tile_b(q, 3)
                experts(q, 3)
                new_rows(q, 3)
                experts(q, 4)
                experts(q, 5)
                normalise(q, 3)
                experts(q, 6)
                node_rows(q, 4)
                experts(q, 7)
                v.sem_inc(S["acc_done"], 1)
            last = NB // 2 - 1
            turn_pair(last)
            low1(last, 0)
            route(last)
            start_sum(last)
            for x_ in range(2, NE + 2):
                experts(last, x_)
            v.sem_inc(S["acc_done"], 1)

        @block.tensor
        def _(pe):
            t = nc.tensor
            pe.sem_inc(S["onehot_used"], 2)
            pe.sem_inc(S["sort_used"], 2)
            pe.sem_inc(S["slot_done"], RING)
            pe.sem_inc(S["node_onehot_used"], OH)
            pe.sem_inc(S["evac_done"], 1)
            pe.sem_inc(S["l2_summed"], CREDIT)
            pe.sem_inc(S["l3_summed"], CREDIT)
            pe.wait_ge(S["fold_in"], 11 * 16)
            for a_ in range(2):
                for c in range(2):
                    m = 2 * a_ + c
                    for bank, lo_, hi_ in ((banks[2 * m], 0, 2 * D), (banks[2 * m + 1], 2 * D, G3)):
                        for k in range(2):
                            ins = t.matmul(bank[:, 0:hi_ - lo_], w_conv[:, 2 * a_ + k, c * P:c * P + P],
                                           w_ih_raw[:, 2 * a_ + k, lo_:hi_], start=(k == 0), stop=(k == 1))
            ins.then_inc(S["fold_summed"], 1)
            pe.wait_ge(S["fold_done"], 1)
            bc = b_conv[:].rearrange("p (a c m) -> p a c m", a=2, c=2)
            for bank, lo_, hi_ in ((banks[0], 0, 2 * D), (banks[1], 2 * D, G3)):
                for n_ in range(4):
                    ins = t.matmul(bank[0:2, 0:hi_ - lo_], bc[:, n_ // 2, n_ % 2, :], w_ih_raw[:, n_, lo_:hi_],
                                   start=(n_ == 0), stop=(n_ == 3))
            ins.then_inc(S["fold_summed"], 1)
            pe.wait_ge(S["fold_done"], 2)
            pe.wait_ge(S["consts"], N_CONSTS)
            for d in range(2):
                q0 = d * 2 * NB
                for h in range(2):
                    t.matmul(banks[h][:, 0:HS], zeros16[:, 0:P], zeros16[:, 0:HS], start=True, stop=False,
                             skip_group_check=True)
                with pe.Fori(0, NB // 2) as r:
                    for k in range(2):
                        b = r * 2 + k
                        pe.wait_ge(S["onehot_ready"], r * 2 + (q0 + k + 1))
                        for h in range(2):
                            ins = t.matmul(banks[h][:, 0:HS], pick_row[:, bass.ds(b + (P - NB), P)],
                                           onehot_bucket[:, k, h * HS:h * HS + HS], start=False, stop=False,
                                           skip_group_check=True)
                        ins.then_inc(S["onehot_used"], 1)
                pe.wait_ge(S["slots16_ready"], d + 1)
                t.matmul(banks[6][:, 0:1], lower_bucket, bucket_slots16[:], start=True, stop=True)
                t.matmul(banks[7][0:1, 0:NB], bucket_slots16[:], lower_bucket[:, 0:NB], start=True, stop=True
                         ).then_inc(S["slot_prefix_ready"], 1)
                pe.wait_ge(S["base_ready"], d + 1)
                with pe.Fori(0, NB // 2) as r:
                    for k in range(2):
                        b = r * 2 + k
                        pe.wait_ge(S["merged"], r * 2 + (d * NB + k + 1))
                        pe.wait_ge(S["onehot_ready"], r * 2 + (q0 + NB + k + 1))
                        for h in range(2):
                            o = banks[2 + 2 * k + h][:, 0:HS]
                            cols = slice(h * HS, h * HS + HS)
                            t.matmul(o, lower, onehot_bucket[:, k, cols], start=True, stop=False)
                            ins = t.matmul(o, spread_row[:, bass.ds(b, 1), :].rearrange("p a m -> p (a m)"),
                                           base_digits[:, cols], start=False, stop=True)
                        ins.then_inc(S["onehot_used"], 1)

            def sort_products(k):
                for bank, half in ((sort_hi, 0), (sort_lo, 1)):
                    for h in range(2):
                        ins = t.matmul(bank[h][:, 0:HS], row_payload[:, k, half * P:half * P + P],
                                       slot_onehot[:, k, h * HS:h * HS + HS], start=False, stop=False,
                                       skip_group_check=True)
                return ins

            def clear_sort():
                for bank in (*sort_hi, *sort_lo):
                    t.matmul(bank[:, 0:HS], zeros16[:, 0:P], zeros16[:, 0:HS], start=True, stop=False,
                             skip_group_check=True)

            pe.wait_ge(S["merged"], 2 * NB + 2)
            clear_sort()
            with pe.Fori(0, SORTED_TILES // 2) as r:
                for k in range(2):
                    pe.wait_ge(S["sort_ready"], r * 2 + (k + 1))
                    sort_products(k).then_inc(S["sort_used"], 1)
            pe.wait_ge(S["sort_used"], SORTED_TILES + 2)
            pe.sem_inc(S["sort_summed"], 1)
            for d in range(2):
                pe.wait_ge(S["owners_marked"], d + 1)
                for h in range(2):
                    ins = t.matmul(banks[4 + h][:, 0:HS], ones16[:], onehot_bucket[0:NB, 0, h * HS:h * HS + HS],
                                   start=True, stop=True)
                ins.then_inc(S["owners_summed"], 1)
            pe.wait_ge(S["decoded"], 2)

            def bucket_sum(d, j):
                lo = pe.value_load(first_batch[0:1, d, bass.ds(j, 1)], min_val=0, max_val=BATCHES - 1)
                hi = pe.value_load(first_batch[0:1, d, bass.ds(j + 1, 1)], min_val=0, max_val=BATCHES - 1)
                pe.wait_ge(S["evac_done"], j + (d * NB + 1))
                t.matmul(sums[:, :], zeros16[:, 0:P], zeros16[:], start=True, stop=False,
                         skip_group_check=True)
                t.matmul(counts[:, 0:1], zeros16[:, 0:P], ones_col[:], start=True, stop=False,
                         skip_group_check=True)

                def visit(b, frees):
                    at_ = b + j
                    pe.wait_ge(S["node_onehot_ready"], at_ + (d * VISITS + 1))
                    pe.wait_ge(S["rows_landed"], b + (d * BATCHES + 1))
                    pe.sem_inc(S["turn"], 1)
                    buf, part = (at_ + d * VISITS) % OH, b % RINGS
                    batches = ring[:].rearrange("p (r s) m -> p r (s m)", r=RINGS)
                    hots = onehot_node[:].rearrange("p r s m -> p r (s m)")
                    for q in range(BATCH):
                        oh = hots[:, bass.ds(buf, 1), q * P:q * P + P].rearrange("p a m -> p (a m)")
                        rows = batches[:, bass.ds(part, 1), q * 2 * D:(q + 1) * 2 * D].rearrange("p a m -> p (a m)")
                        summed = t.matmul(sums[:, :], oh, rows, start=False, stop=False, skip_group_check=True)
                        ins = t.matmul(counts[:, 0:1], oh, ones_col[:], start=False, stop=False,
                                       skip_group_check=True)
                        if q == BATCH - 1 and frees:
                            summed.then_inc(S["slot_done"], BATCH)
                    ins.then_inc(S["node_onehot_used"], 1)

                with pe.If(hi > lo):
                    with pe.Fori(lo, hi) as b:
                        visit(b, True)
                visit(hi, False)
                t.matmul(counts[:, 0:1], zeros16[:, 0:P], ones_col[:], start=False, stop=True,
                         skip_group_check=True).then_inc(S["bucket_done"], 1)

            with pe.Fori(0, NB) as j:
                bucket_sum(0, j)
            pe.wait_ge(S["bucket_done"], NB)
            pe.sem_inc(S["slot_done"], BATCH)
            pe.wait_ge(S["small_in"], 6 * 16)
            pe.wait_ge(S["experts_in"], 5 * 16)

            pe.wait_ge(S["low_ready"], 6)

            def product(o, left, right, first, last):
                (a_hi, a_lo), (b_hi, b_lo) = left, right
                t.matmul(o, a_hi, b_hi, start=first, stop=False, skip_group_check=True)
                t.matmul(o, a_hi, b_lo, start=False, stop=False, skip_group_check=True)
                return t.matmul(o, a_lo, b_hi, start=False, stop=last, skip_group_check=True)

            def turn_a(r, o):
                jj = o % 2
                pe.wait_ge(S["h_tile_ready"], r * 2 + (o + 1))
                for c in range(2):
                    t.transpose(mean_bank[jj][:, c * P:c * P + P], mean_a_t[:, jj, c * P:c * P + P], ident[:])
                for c in range(2):
                    ins = t.transpose(mean_bank[jj][:, (2 + c) * P:(3 + c) * P], h_t[:, jj, c * P:c * P + P], ident[:])
                ins.then_inc(S["tile_a_turned"], 1)

            def turn_b(r, o):
                pe.wait_ge(S["tile_a_ready"], r * 2 + (o + 1))
                pe.wait_ge(S["evac_done"], r * 2 + (NB + 2 + o))
                for c in range(2):
                    t.transpose(turned[:, c * P:c * P + P], mean_b[:, c * P:c * P + P], ident[:])
                pe.wait_ge(S["flags_ready"], r * 2 + (o + 1))
                t.transpose(turned[0:4, D:D + P], flags[:], ident[:]).then_inc(S["tile_b_turned"], 1)

            order = ((0, 0), (1, 1), (2, 4), (3, 5), (4, 2), (5, 3))

            def rz_products(r, o):
                for n_, (src_, wt) in enumerate(order):
                    if n_ == 4:
                        pe.wait_ge(S["tile_b_ready"], r * 2 + (o + 1))
                    product(rz_bank[:], (tile_hi[:, src_, :], tile_lo[:, src_, :]),
                            (gate_hi[:, wt, 0:2 * D], gate_lo[:, wt, 0:2 * D]), n_ == 0, False)
                t.matmul(rz_bank[:], flags_T, bias_hi[:, 0:2 * D], start=False, stop=False, skip_group_check=True)
                t.matmul(rz_bank[:], flags_T, bias_lo[:, 0:2 * D], start=False, stop=True, skip_group_check=True
                         ).then_inc(S["rz_summed"], 1)

            def n_products():
                for n_, (src_, wt) in enumerate(order):
                    part = slice(D, 2 * D) if wt >= 4 else slice(0, D)
                    product(n_bank[:, part], (tile_hi[:, src_, :], tile_lo[:, src_, :]),
                            (gate_hi[:, wt, 2 * D:G3], gate_lo[:, wt, 2 * D:G3]), n_ == 0, False)
                t.matmul(n_bank[:], flags_T, bias_hi[:, 2 * D:G3 + D], start=False, stop=False,
                         skip_group_check=True)
                t.matmul(n_bank[:], flags_T, bias_lo[:, 2 * D:G3 + D], start=False, stop=True,
                         skip_group_check=True).then_inc(S["n_summed"], 1)

            def turn_xn(r, o):
                jj = o % 2
                pe.wait_ge(S["xn_ready"], r * 2 + (o + 1))
                for c in range(2):
                    ins = t.transpose(turned[:, (2 * jj + c) * P:(2 * jj + c + 1) * P], xn[:, jj, c * P:c * P + P],
                                      ident[:])
                return ins

            def turn_pair(r, o):
                turn_xn(r, o)
                turn_xn(r, o + 1).then_inc(S["xn_turned"], 2)

            def route(q):
                pe.wait_ge(S["xn_T_ready"], q * 2 + 2)
                for k in range(2):
                    ins = product(route_bank[:, 0:2 * P], (r_hi[:, k, :], r_lo[:, k, :]),
                                  (xn_hi[:, k, :], xn_lo[:, k, :]), k == 0, k == 1)
                ins.then_inc(S["router_summed"], 1)

            def score(q):
                pe.wait_ge(S["router_ready"], q + 1)
                for tt in range(2):
                    ins = t.matmul(route_bank[:, 2 * P + tt * NE:2 * P + tt * NE + NE],
                                   router_h[:, tt * P:tt * P + P], r_w2[:], start=True, stop=True)
                ins.then_inc(S["logits_summed"], 1)

            def last_biases(q):
                pe.wait_ge(S["coef_ready"], q + 1)
                for tt in range(2):
                    ins = t.transpose(route_bank[0:NE, tt * P:tt * P + P], coef[:, tt, :], ident[:])
                ins.then_inc(S["coef_turned"], 1)
                layer2(q, 0)
                pe.wait_ge(S["coef_T_ready"], q + 1)
                for tt in range(2):
                    ins = t.matmul(route_bank[:, tt * D:tt * D + D], coef_T[:, tt, :], e_b3[:], start=True, stop=True)
                ins.then_inc(S["b3_summed"], 1)

            def layer1(q, x_):
                pe.wait_ge(S["h1_hi_ready"], q * NE + (x_ + 1))
                for m in range(2):
                    cols = slice(m * P, m * P + P)
                    for k in range(2):
                        ins = product(l1_bank[:, m * 2 * P:(m + 1) * 2 * P],
                                      (e_hi[0][:, 2 * x_ + k, cols], e_lo[0][:, 2 * x_ + k, cols]),
                                      (xn_hi[:, k, :], xn_lo[:, k, :]), k == 0, k == 1)
                ins.then_inc(S["l1_summed"], 1)

            def layer2(q, x_):
                pe.wait_ge(S["h2_hi_ready"], q * NE + (x_ + 1))
                pe.wait_ge(S["h1_ready"], q * NE + (x_ + 1))
                for m in range(2):
                    cols = slice(m * P, m * P + P)
                    for k in range(2):
                        ins = product(l2_bank[:, m * 2 * P:(m + 1) * 2 * P],
                                      (e_hi[1][:, 2 * x_ + k, cols], e_lo[1][:, 2 * x_ + k, cols]),
                                      (h1_hi[:, x_ % 2, k, :], h1_lo[:, x_ % 2, k, :]), k == 0, k == 1)
                ins.then_inc(S["l2_summed"], 1)

            def layer3(q, x_):
                pe.wait_ge(S["combined"], q * NE + (x_ + 1))
                pe.wait_ge(S["h2_ready"], q * NE + (x_ + 1))
                for tt in range(2):
                    cols = slice(tt * P, tt * P + P)
                    for k in range(2):
                        ins = product(l3_bank[:, tt * D:tt * D + D],
                                      (h2_hi[:, x_ % 2, k, cols], h2_lo[:, x_ % 2, k, cols]),
                                      (e_hi[2][:, 2 * x_ + k, :], e_lo[2][:, 2 * x_ + k, :]), k == 0, k == 1)
                ins.then_inc(S["l3_summed"], 1)

            def experts(q, x_):
                if x_ < NE:
                    layer1(q, x_)
                if x_ - 1 < NE:
                    layer2(q, x_ - 1)
                layer3(q, x_ - 2)

            for o in range(2):
                turn_a(0, o)
                bucket_sum(1, o)
                turn_b(0, o)
                rz_products(0, o)
                n_products()
            turn_pair(0, 0)
            with pe.Fori(0, NB // 2 - 1) as q:
                turn_a(q, 2)
                route(q)
                layer1(q, 0)
                bucket_sum(1, q * 2 + 2)
                score(q)
                layer1(q, 1)
                turn_b(q, 2)
                rz_products(q, 2)
                last_biases(q)
                turn_a(q, 3)
                layer1(q, 2)
                pe.wait_ge(S["acc_started"], q + 1)
                n_products()
                layer2(q, 1)
                layer3(q, 0)
                bucket_sum(1, q * 2 + 3)
                layer1(q, 3)
                turn_b(q, 3)
                layer2(q, 2)
                layer3(q, 1)
                rz_products(q, 3)
                n_products()
                for x_ in (4, 5, 6):
                    experts(q, x_)
                turn_pair(q, 2)
                experts(q, 7)
            last = NB // 2 - 1
            route(last)
            layer1(last, 0)
            score(last)
            layer1(last, 1)
            last_biases(last)
            for x_ in range(2, NE + 2):
                experts(last, x_)


def kernel(**inputs):
    import numpy as _np
    import concourse.bacc as _bacc
    from concourse.bass_utils import run_bass_kernel_spmd as _run

    nc = _bacc.Bacc("TRN2", target_bir_lowering=False, num_devices=1)
    x = _np.asarray(inputs["x"])
    xp = _np.zeros((NP + 2 * P, D), x.dtype)
    xp[:NODES] = x
    edges = _np.full((2, NS * P), SENTINEL, _np.int32)
    edges[0, :EDGES] = inputs["dst"]
    edges[1, :EDGES] = inputs["src"]
    edges = _np.ascontiguousarray(edges.reshape(2, NS, P).transpose(2, 0, 1))
    g = {n.split("_", 1)[1]: _np.asarray(a) for n, a in inputs.items() if n.startswith("L0_")}
    arrays = {
        "in_x": xp, "in_edges": edges,
        "in_w_ih_T": g["gnn_W_ih"].T, "in_w_hh_T": g["gnn_W_hh"].T, "in_w_in": g["gnn_W_in"],
        "in_w_out": g["gnn_W_out"], "in_b_in": g["gnn_b_in"][:, None], "in_b_out": g["gnn_b_out"][:, None],
        "in_b_ih": g["gnn_b_ih"][None], "in_b_hh": g["gnn_b_hh"][None],
        "in_r_w1": g["ffn_router_w1"], "in_r_b1": g["ffn_router_b1"][:, None],
        "in_r_w2": g["ffn_router_w2"], "in_r_b2": g["ffn_router_b2"][None],
        "in_e_w1": g["ffn_expert_w1"], "in_e_w2": g["ffn_expert_w2"], "in_e_w3": g["ffn_expert_w3"],
        "in_e_b1": g["ffn_expert_b1"].reshape(NE, 2, P).transpose(2, 0, 1),
        "in_e_b2": g["ffn_expert_b2"].reshape(NE, 2, P).transpose(2, 0, 1), "in_e_b3": g["ffn_expert_b3"],
    }
    arrays = {n: _np.ascontiguousarray(a) for n, a in arrays.items()}
    aps = {n: nc.dram_tensor(n, a.shape, mybir.dt.from_np(a.dtype), kind="ExternalInput").ap()
           for n, a in arrays.items()}
    out = nc.dram_tensor("out_0", (NP, D), F32, kind="ExternalOutput").ap()
    table = nc.dram_tensor("split_rows", (NP, 2 * D), F16, kind="Internal").ap()
    lists = [nc.dram_tensor(f"list_{d}", (LIST, 1), I32, kind="Internal").ap() for d in range(2)]
    means = nc.dram_tensor("in_edge_means", (NP + 2 * P, D), F32, kind="Internal").ap()
    gnn_moe_program(nc, aps["in_x"], aps["in_edges"], {n[3:]: ap for n, ap in aps.items()}, out, table, lists, means)
    r = _run(nc, [arrays], core_ids=[0])
    return r.results[0]["out_0"][:NODES]
```
